# Optimizing a Trainium2 kernel written in Bass

```python
import numpy as np
import jax
import jax.numpy as jnp

def _softmax(x, axis=-1):
    return jax.nn.softmax(x, axis=axis)

def _gelu(x):
    return jax.nn.gelu(x, approximate=True)

def _silu(x):
    return jax.nn.silu(x)

def _sigmoid(x):
    return jax.nn.sigmoid(x)

def _layernorm(x, axis=-1, eps=1e-05):
    m = jnp.mean(x, axis=axis, keepdims=True)
    v = jnp.var(x, axis=axis, keepdims=True)
    return (x - m) / jnp.sqrt(v + eps)

def _scatter_add(tgt, idx, src, axis=0):
    return tgt.at[idx].add(src)

def _segment_sum(src, seg, n):
    return jax.ops.segment_sum(src, seg, n)
kernel_name = 'mk_adaln_d2_jaxref_r8_bec909'

def setup_inputs(seed: int=0):
    np.random.seed(seed)
    _w = jnp.asarray

    def _L0_attn_setup():
        import jax, jax.numpy as jnp
        import numpy as np
        B, S, D, H = (2, 256, 128, 16)
        DK = D // H
        key = jax.random.key(seed)
        ks = jax.random.split(key, 9)
        s = 0.02
        return {'embeddings': jax.random.normal(ks[0], (B, S, D), jnp.float32), 'Wq': jax.random.normal(ks[1], (H, D, DK), jnp.float32) * s, 'bq': jax.random.normal(ks[2], (H, DK), jnp.float32) * s, 'Wk': jax.random.normal(ks[3], (H, D, DK), jnp.float32) * s, 'bk': jax.random.normal(ks[4], (H, DK), jnp.float32) * s, 'Wv': jax.random.normal(ks[5], (H, D, DK), jnp.float32) * s, 'bv': jax.random.normal(ks[6], (H, DK), jnp.float32) * s, 'Wo': jax.random.normal(ks[7], (D, D), jnp.float32) * s, 'bo': jax.random.normal(ks[8], (D,), jnp.float32) * s}
    _L0_attn_in = _L0_attn_setup()

    def _L0_ffn_setup():
        import jax, jax.numpy as jnp
        import numpy as np
        from jax import lax
        D = 128
        H = 176
        E = 8
        K = 2
        ROUTER_SCALE = 1.0

        def _expert(x, w1, b1, w3, b3, w2, b2):
            h = jax.nn.silu((x @ w1 + b1) * (x @ w3 + b3))
            return h @ w2 + b2
        key = jax.random.key(seed)
        ks = jax.random.split(key, 16)
        s = 0.02
        inp = {'x': jax.random.normal(ks[0], (2, 256, D), dtype=jnp.float32), 'gate_w': jax.random.normal(ks[1], (E, D), dtype=jnp.float32) * s, 'gate_b': jax.random.normal(ks[2], (E,), dtype=jnp.float32) * s, 'w1': jax.random.normal(ks[3], (E, D, H), dtype=jnp.float32) * s, 'b1': jax.random.normal(ks[4], (E, H), dtype=jnp.float32) * s, 'w3': jax.random.normal(ks[5], (E, D, H), dtype=jnp.float32) * s, 'b3': jax.random.normal(ks[6], (E, H), dtype=jnp.float32) * s, 'w2': jax.random.normal(ks[7], (E, H, D), dtype=jnp.float32) * s, 'b2': jax.random.normal(ks[8], (E, D), dtype=jnp.float32) * s, 'sw1': jax.random.normal(ks[9], (D, H), dtype=jnp.float32) * s, 'sb1': jax.random.normal(ks[10], (H,), dtype=jnp.float32) * s, 'sw3': jax.random.normal(ks[11], (D, H), dtype=jnp.float32) * s, 'sb3': jax.random.normal(ks[12], (H,), dtype=jnp.float32) * s, 'sw2': jax.random.normal(ks[13], (H, D), dtype=jnp.float32) * s, 'sb2': jax.random.normal(ks[14], (D,), dtype=jnp.float32) * s}
        return inp
    _L0_ffn_in = _L0_ffn_setup()
    _L0_c = _w((lambda *s: np.random.randn(*s).astype(np.float32) * 0.05)(8, 128))
    _L0_wmod = _w((lambda *s: np.random.randn(*s).astype(np.float32) * 0.05)(128, 6 * 128) * 128 ** (-0.5))

    def _L1_attn_setup():
        import jax, jax.numpy as jnp
        import numpy as np
        import math
        NUM_HEADS = 16

        def get_slopes(n):

            def pow2(n):
                start = 2 ** (-2 ** (-(math.log2(n) - 3)))
                return [start * start ** i for i in range(n)]
            if math.log2(n).is_integer():
                return pow2(n)
            c = 2 ** math.floor(math.log2(n))
            return pow2(c) + get_slopes(2 * c)[0::2][:n - c]
        key = jax.random.key(seed)
        ks = jax.random.split(key, 5)
        B, T, C = (2, 256, 128)
        return {'x': jax.random.normal(ks[0], (B, T, C), dtype=jnp.float32), 'W_qkv': jax.random.normal(ks[1], (C, 3 * C), dtype=jnp.float32) * 0.02, 'b_qkv': jax.random.normal(ks[2], (3 * C,), dtype=jnp.float32) * 0.02, 'W_proj': jax.random.normal(ks[3], (C, C), dtype=jnp.float32) * 0.02, 'b_proj': jax.random.normal(ks[4], (C,), dtype=jnp.float32) * 0.02}
    _L1_attn_in = _L1_attn_setup()

    def _L1_ffn_setup():
        import jax, jax.numpy as jnp
        import numpy as np
        import math
        BETA = 0.9
        THRESHOLD = 1.0
        NUM_STEPS = 5
        ALPHA = 2.0

        @jax.custom_vjp
        def spike_fn(u):
            return (u > 0).astype(u.dtype)

        def _spike_fwd(u):
            return (spike_fn(u), u)

        def _spike_bwd(u, g):
            s = jnp.pi / 2.0 * ALPHA * u
            return (g * (ALPHA / 2.0) / (1.0 + s * s),)
        spike_fn.defvjp(_spike_fwd, _spike_bwd)
        key = jax.random.key(seed)
        k1, k2, k3 = jax.random.split(key, 3)
        n_embd = 128
        x = jax.random.normal(k1, (4, 256, n_embd), dtype=jnp.float32)
        W_fc = jax.random.normal(k2, (4 * n_embd, n_embd), dtype=jnp.float32) / math.sqrt(n_embd)
        W_proj = jax.random.normal(k3, (n_embd, 4 * n_embd), dtype=jnp.float32) / math.sqrt(4 * n_embd)
        return {'x': x, 'W_fc': W_fc, 'W_proj': W_proj}
    _L1_ffn_in = _L1_ffn_setup()
    _L1_c = _w((lambda *s: np.random.randn(*s).astype(np.float32) * 0.05)(8, 128))
    _L1_wmod = _w((lambda *s: np.random.randn(*s).astype(np.float32) * 0.05)(128, 6 * 128) * 128 ** (-0.5))
    _d = {'L0_attn_embeddings': _L0_attn_in['embeddings'], 'L0_attn_Wq': _L0_attn_in['Wq'], 'L0_attn_bq': _L0_attn_in['bq'], 'L0_attn_Wk': _L0_attn_in['Wk'], 'L0_attn_bk': _L0_attn_in['bk'], 'L0_attn_Wv': _L0_attn_in['Wv'], 'L0_attn_bv': _L0_attn_in['bv'], 'L0_attn_Wo': _L0_attn_in['Wo'], 'L0_attn_bo': _L0_attn_in['bo'], 'L0_ffn_gate_w': _L0_ffn_in['gate_w'], 'L0_ffn_gate_b': _L0_ffn_in['gate_b'], 'L0_ffn_w1': _L0_ffn_in['w1'], 'L0_ffn_b1': _L0_ffn_in['b1'], 'L0_ffn_w3': _L0_ffn_in['w3'], 'L0_ffn_b3': _L0_ffn_in['b3'], 'L0_ffn_w2': _L0_ffn_in['w2'], 'L0_ffn_b2': _L0_ffn_in['b2'], 'L0_ffn_sw1': _L0_ffn_in['sw1'], 'L0_ffn_sb1': _L0_ffn_in['sb1'], 'L0_ffn_sw3': _L0_ffn_in['sw3'], 'L0_ffn_sb3': _L0_ffn_in['sb3'], 'L0_ffn_sw2': _L0_ffn_in['sw2'], 'L0_ffn_sb2': _L0_ffn_in['sb2'], 'L0_c': _L0_c, 'L0_wmod': _L0_wmod, 'L1_attn_W_qkv': _L1_attn_in['W_qkv'], 'L1_attn_b_qkv': _L1_attn_in['b_qkv'], 'L1_attn_W_proj': _L1_attn_in['W_proj'], 'L1_attn_b_proj': _L1_attn_in['b_proj'], 'L1_ffn_W_fc': _L1_ffn_in['W_fc'], 'L1_ffn_W_proj': _L1_ffn_in['W_proj'], 'L1_c': _L1_c, 'L1_wmod': _L1_wmod}
    _x0 = _d['L0_attn_embeddings']
    _d['L0_attn_embeddings'] = jax.random.normal(jax.random.fold_in(jax.random.key(seed), 1), (8, 512, 128), dtype=_x0.dtype)
    del _x0
    return _d

def reference(L0_attn_embeddings, L0_attn_Wq, L0_attn_bq, L0_attn_Wk, L0_attn_bk, L0_attn_Wv, L0_attn_bv, L0_attn_Wo, L0_attn_bo, L0_ffn_gate_w, L0_ffn_gate_b, L0_ffn_w1, L0_ffn_b1, L0_ffn_w3, L0_ffn_b3, L0_ffn_w2, L0_ffn_b2, L0_ffn_sw1, L0_ffn_sb1, L0_ffn_sw3, L0_ffn_sb3, L0_ffn_sw2, L0_ffn_sb2, L0_c, L0_wmod, L1_attn_W_qkv, L1_attn_b_qkv, L1_attn_W_proj, L1_attn_b_proj, L1_ffn_W_fc, L1_ffn_W_proj, L1_c, L1_wmod):

    def _L0_attn_ref(embeddings, Wq, bq, Wk, bk, Wv, bv, Wo, bo):
        import jax, jax.numpy as jnp
        import numpy as np
        B, S, D, H = (2, 256, 128, 16)
        DK = D // H
        b, s, d = embeddings.shape
        dk = Wq.shape[-1]
        q = jnp.einsum('bsd,hdk->bhsk', embeddings, Wq) + bq[None, :, None, :]
        k = jnp.einsum('bsd,hdk->bhsk', embeddings, Wk) + bk[None, :, None, :]
        v = jnp.einsum('bsd,hdk->bhsk', embeddings, Wv) + bv[None, :, None, :]
        scores = jnp.einsum('bhqk,bhsk->bhqs', q, k) / jnp.sqrt(jnp.float32(dk))
        causal_mask = jnp.triu(jnp.ones((s, s), dtype=bool), k=1)
        scores = jnp.where(causal_mask, jnp.float32(-1000000000.0), scores)
        weights = jax.nn.softmax(scores, axis=-1)
        ctx = jnp.einsum('bhqs,bhsk->bhqk', weights, v)
        concat = ctx.transpose(0, 2, 1, 3).reshape(b, s, d)
        return concat @ Wo + bo

    def _L0_ffn_ref(x, gate_w, gate_b, w1, b1, w3, b3, w2, b2, sw1, sb1, sw3, sb3, sw2, sb2):
        import jax, jax.numpy as jnp
        import numpy as np
        from jax import lax
        D = 128
        H = 176
        E = 8
        K = 2
        ROUTER_SCALE = 1.0

        def _expert(x, w1, b1, w3, b3, w2, b2):
            h = jax.nn.silu((x @ w1 + b1) * (x @ w3 + b3))
            return h @ w2 + b2
        shape = x.shape
        xf = x.reshape(-1, D)
        T = xf.shape[0]
        scores = jax.nn.softmax(xf @ gate_w.T, axis=-1)
        biased = scores + gate_b
        _, idx = lax.top_k(biased, K)
        w = jnp.take_along_axis(scores, idx, axis=-1) * ROUTER_SCALE
        rw = jnp.zeros((T, E), dtype=xf.dtype).at[jnp.arange(T)[:, None], idx].add(w)
        h = jax.nn.silu((jnp.einsum('td,edh->teh', xf, w1) + b1) * (jnp.einsum('td,edh->teh', xf, w3) + b3))
        oe = jnp.einsum('teh,ehd->ted', h, w2) + b2
        y = jnp.einsum('te,ted->td', rw, oe)
        z = _expert(xf, sw1, sb1, sw3, sb3, sw2, sb2)
        return (y + z).reshape(shape)

    def _L1_attn_ref(x, W_qkv, b_qkv, W_proj, b_proj):
        import jax, jax.numpy as jnp
        import numpy as np
        import math
        NUM_HEADS = 16

        def get_slopes(n):

            def pow2(n):
                start = 2 ** (-2 ** (-(math.log2(n) - 3)))
                return [start * start ** i for i in range(n)]
            if math.log2(n).is_integer():
                return pow2(n)
            c = 2 ** math.floor(math.log2(n))
            return pow2(c) + get_slopes(2 * c)[0::2][:n - c]
        B, T, C = x.shape
        H = NUM_HEADS
        D = C // H
        qkv = x @ W_qkv + b_qkv
        q, k, v = jnp.split(qkv, 3, axis=-1)
        q = q.reshape(B, T, H, D).transpose(0, 2, 1, 3)
        k = k.reshape(B, T, H, D).transpose(0, 2, 1, 3)
        v = v.reshape(B, T, H, D).transpose(0, 2, 1, 3)
        slopes = jnp.asarray(get_slopes(H), dtype=jnp.float32)
        idx = jnp.arange(T)
        alibi = jnp.minimum(idx[None, :] - idx[:, None], 0).astype(jnp.float32)
        bias = slopes[:, None, None] * alibi
        scale = 1.0 / math.sqrt(D)
        scores = jnp.einsum('bhtd,bhsd->bhts', q, k) * scale + bias[None]
        w = jax.nn.softmax(scores, axis=-1)
        y = jnp.einsum('bhts,bhsd->bhtd', w, v)
        y = y.transpose(0, 2, 1, 3).reshape(B, T, C)
        return y @ W_proj + b_proj

    def _L1_ffn_ref(x, W_fc, W_proj):
        import jax, jax.numpy as jnp
        import numpy as np
        import math
        BETA = 0.9
        THRESHOLD = 1.0
        NUM_STEPS = 5
        ALPHA = 2.0

        @jax.custom_vjp
        def spike_fn(u):
            return (u > 0).astype(u.dtype)

        def _spike_fwd(u):
            return (spike_fn(u), u)

        def _spike_bwd(u, g):
            s = jnp.pi / 2.0 * ALPHA * u
            return (g * (ALPHA / 2.0) / (1.0 + s * s),)
        spike_fn.defvjp(_spike_fwd, _spike_bwd)
        h = jnp.square(jax.nn.relu(jnp.einsum('bsd,fd->bsf', x, W_fc)))
        y = jnp.einsum('bsf,df->bsd', h, W_proj)

        def step(mem, _):
            reset = jax.lax.stop_gradient(spike_fn(mem - THRESHOLD))
            mem_new = BETA * mem + y - reset * THRESHOLD
            spk = spike_fn(mem_new - THRESHOLD)
            return (mem_new, spk)
        mem0 = jnp.zeros_like(y)
        _, spks = jax.lax.scan(step, mem0, None, length=NUM_STEPS)
        return jnp.sum(spks, axis=0) / NUM_STEPS
    x = L0_attn_embeddings
    mod = (_silu(L0_c) @ L0_wmod).reshape(L0_c.shape[0], 6, 1, -1)
    sa, ca, ga, sb, cb, gb = (mod[:, 0], mod[:, 1], mod[:, 2], mod[:, 3], mod[:, 4], mod[:, 5])
    ga = (2 * (ga >= 0) - 1) * jnp.maximum(jnp.abs(ga), 0.25)
    gb = (2 * (gb >= 0) - 1) * jnp.maximum(jnp.abs(gb), 0.25)
    h = _layernorm(x, axis=-1) * (1 + ca) + sa
    x = x + ga * _L0_attn_ref(h, L0_attn_Wq, L0_attn_bq, L0_attn_Wk, L0_attn_bk, L0_attn_Wv, L0_attn_bv, L0_attn_Wo, L0_attn_bo)
    h = _layernorm(x, axis=-1) * (1 + cb) + sb
    x = x + gb * _L0_ffn_ref(h, L0_ffn_gate_w, L0_ffn_gate_b, L0_ffn_w1, L0_ffn_b1, L0_ffn_w3, L0_ffn_b3, L0_ffn_w2, L0_ffn_b2, L0_ffn_sw1, L0_ffn_sb1, L0_ffn_sw3, L0_ffn_sb3, L0_ffn_sw2, L0_ffn_sb2)
    mod = (_silu(L1_c) @ L1_wmod).reshape(L1_c.shape[0], 6, 1, -1)
    sa, ca, ga, sb, cb, gb = (mod[:, 0], mod[:, 1], mod[:, 2], mod[:, 3], mod[:, 4], mod[:, 5])
    ga = (2 * (ga >= 0) - 1) * jnp.maximum(jnp.abs(ga), 0.25)
    gb = (2 * (gb >= 0) - 1) * jnp.maximum(jnp.abs(gb), 0.25)
    h = _layernorm(x, axis=-1) * (1 + ca) + sa
    x = x + ga * _L1_attn_ref(h, L1_attn_W_qkv, L1_attn_b_qkv, L1_attn_W_proj, L1_attn_b_proj)
    h = _layernorm(x, axis=-1) * (1 + cb) + sb
    x = x + gb * _L1_ffn_ref(h, L1_ffn_W_fc, L1_ffn_W_proj)
    return x

_drawn_inputs = setup_inputs


def setup_inputs(seed=0):
    import zlib

    import numpy as np

    out = dict(_drawn_inputs(seed))
    spreads = {}
    factors = {'L0_attn_Wq': 8.0,
     'L0_attn_bq': 8.0,
     'L0_attn_Wk': 8.0,
     'L0_attn_bk': 64.0,
     'L0_attn_Wv': 8.0,
     'L0_attn_bv': 8.0,
     'L0_attn_Wo': 8.0,
     'L0_attn_bo': 8.0,
     'L0_ffn_gate_w': 8.0,
     'L0_ffn_gate_b': 8.0,
     'L0_ffn_w1': 8.0,
     'L0_ffn_b1': 8.0,
     'L0_ffn_w3': 8.0,
     'L0_ffn_b3': 8.0,
     'L0_ffn_w2': 8.0,
     'L0_ffn_b2': 31.806,
     'L0_ffn_sw1': 8.0,
     'L0_ffn_sb1': 8.0,
     'L0_ffn_sw3': 8.0,
     'L0_ffn_sb3': 8.0,
     'L0_ffn_sw2': 8.0,
     'L0_ffn_sb2': 8.0,
     'L0_c': 6.68,
     'L0_wmod': 6.495,
     'L1_attn_W_qkv': 8.0,
     'L1_attn_b_qkv': 8.0,
     'L1_attn_W_proj': 8.0,
     'L1_attn_b_proj': 8.0}
    for name, (base, spread) in spreads.items():
        noise = np.random.default_rng([zlib.crc32(name.encode()), seed]).standard_normal(out[name].shape)
        drawn = base * np.exp(spread * noise) if base else spread * noise
        out[name] = jnp.asarray(drawn.astype(out[name].dtype))
    for name, factor in factors.items():
        out[name] = (out[name] * factor).astype(out[name].dtype)
    return out
```

```python
from contextlib import ExitStack

import concourse.bass as bass
from concourse import mybir

F32 = mybir.dt.float32
F32R = mybir.dt.float32r
BF16 = mybir.dt.bfloat16
U32 = mybir.dt.uint32
ALU = mybir.AluOpType
ACT = mybir.ActivationFunctionType
AX = mybir.AxisListType

P = 128
NBATCH, SEQ, D = 8, 512, 128
HEADS, DK = 16, 8
TILES = SEQ // P
GROUP = 4
GROUPS = HEADS // GROUP
EPS = 1e-5
EXPERTS, HID = 8, 176
ALL_EXP = EXPERTS + 1
HTILES = -(-ALL_EXP * HID // P)
HPAD = HTILES * P
FFN = 512
STEPS, BETA = 5, 0.9
GATE_MIN = 0.25
CH_SA, CH_CA, CH_GA, CH_SB, CH_CB, CH_GB = range(6)

Q_PARTS = (0, 0, 1, 1, 0, 2)
K_PARTS = (0, 1, 0, 1, 2, 0)
R_ALIBI = 8 * len(Q_PARTS)
N_ALIBI = 6 * (TILES - 1)
R_SHIFT = R_ALIBI + N_ALIBI
R_ALL = R_SHIFT + 3
ALIBI_SHIFT = -20.0
DENS = DK
VW = 32


def both(ap, n):
    return ap.unsqueeze(1).to_broadcast([ap.shape[0], n, ap.shape[1]])


def each(ap, n):
    return ap.unsqueeze(2).to_broadcast([ap.shape[0], ap.shape[1], n])


def semaphores(nc, ctx, phase, names):
    return {n: ctx.enter_context(nc.semaphore(f"{phase}_{n}")) for n in names.split()}


def wait_apart(s, eng, sem, value):
    eng.wait_ge(sem, value)
    if not isinstance(value, int):
        eng.sem_inc(s["apart"], 1)


def setup_phase(nc, dram, sb):
    x, ident = sb["x"], sb["ident"]
    with ExitStack() as ctx:
        def tile(name, shape, dt=F32):
            return ctx.enter_context(nc.sbuf_tensor(name, shape, dt))

        cT = tile("cT", [P, 2, NBATCH])
        half = tile("c_tanh", [P, 2, NBATCH])
        sil2 = tile("c_silu2", [P, 2, NBATCH])
        sil = tile("c_silu", [P, 2, NBATCH])
        silB = tile("c_siluB", [P, 2, NBATCH, P])
        wmod = tile("wmod", [P, 2, 6 * D])
        graw = tile("gate_sign", [P, 4, P])
        gabs = tile("gate_abs", [P, 4, P])
        gmax = tile("gate_max", [P, 4, P])
        ps = ctx.enter_context(nc.psum_tensor("setup_ps", [P, 8, 512], F32))
        s = semaphores(nc, ctx, "su", "load xload zero ident tanh sil2 sil silB mm gsign gabs gmax gate mods free bo")
        block = ctx.enter_context(nc.Block())

        small = ["wqkv0", "bqk0", "wo0", "wqkv1", "bqk1", "wo1", "bv0", "bv1", "bo0", "bo1",
                 "gate_w", "gate_b", "b1", "b3", "b2", "iota8"]

        @block.sync
        def _(sp):
            sp.dma_start(cT[:, 0, :], dram["c0"]).then_inc(s["load"], 16)
            sp.dma_start(cT[:, 1, :], dram["c1"]).then_inc(s["load"], 16)
            for layer in range(2):
                sp.dma_start(wmod[:, layer, :], dram[f"wmod{layer}"]).then_inc(s["load"], 16)
            for b in range(NBATCH):
                sp.dma_start(x[:, b * SEQ:(b + 1) * SEQ].rearrange("p (t d) -> p t d", t=TILES),
                             dram["x"][b].rearrange("(t p) d -> p t d", p=P)).then_inc(s["xload"], 16)
            n_other = 0
            for n in small:
                src = dram[n]
                if n in ("bv0", "bv1", "bo0", "bo1", "gate_b", "iota8"):
                    src = src.partition_broadcast(P)
                sp.dma_start(sb[n][:], src).then_inc(s["xload"], 16)
                n_other += 1
            sp.wait_ge(s["xload"], 16 * (NBATCH + n_other))

        @block.gpsimd
        def _(g):
            g.memset(ident[:], 0.0).then_inc(s["zero"], 1)
            g.memset(sb["mhalf"][:], -0.5)
            g.wait_ge(s["zero"], 1)
            g.affine_select(out=ident[:], in_=ident[:], compare_op=ALU.not_equal, fill=1.0, base=0,
                            pattern=[[-1, P]], channel_multiplier=1).then_inc(s["ident"], 1)

        @block.scalar
        def _(a):
            a.wait_ge(s["load"], 64)
            nc.scalar.activation(half[:], cT[:], ACT.Tanh, scale=0.5).then_inc(s["tanh"], 1)

        @block.tensor
        def _(t):
            t.wait_ge(s["sil"], 1)
            for layer in range(2):
                for i, ch in enumerate((CH_SA, CH_CA, CH_SB, CH_CB)):
                    last = t.matmul(ps[:, 0, (layer * 4 + i) * 8:(layer * 4 + i) * 8 + 8],
                                    wmod[:, layer, ch * D:(ch + 1) * D], sil[:, layer, :], start=True, stop=True)
            last.then_inc(s["mm"], 1)
            t.wait_ge(s["silB"], 1)
            n = 0
            for layer in range(2):
                for ch in (CH_GA, CH_GB):
                    for h in range(2):
                        if n >= 7:
                            t.wait_ge(s["gabs"], n - 6)
                        for b in range(4):
                            last = t.matmul(ps[:, 1 + n % 7, b * P:(b + 1) * P], silB[:, layer, 4 * h + b, :],
                                            wmod[:, layer, ch * D:(ch + 1) * D], start=True, stop=True)
                        last.then_inc(s["mm"], 1)
                        n += 1

        @block.vector
        def _(v):
            v.wait_ge(s["tanh"], 1)
            v.scalar_tensor_tensor(sil2[:], half[:], 1.0, cT[:], ALU.add, ALU.mult).then_inc(s["sil2"], 1)
            v.wait_ge(s["sil2"], 1)
            v.tensor_scalar(sil[:], sil2[:], 0.5, None, ALU.mult).then_inc(s["sil"], 1)
            v.wait_ge(s["sil"], 1)
            v.tensor_copy(silB[:], sil[:].unsqueeze(3).to_broadcast([P, 2, NBATCH, P])).then_inc(s["silB"], 1)
            v.wait_ge(s["mm"], 1)
            for layer in range(2):
                for i in range(4):
                    v.tensor_scalar(sb["mods"][:, layer, i, :], ps[:, 0, (layer * 4 + i) * 8:(layer * 4 + i) * 8 + 8],
                                    float(i % 2), None, ALU.add)
            n = 0
            for layer in range(2):
                for ch in ("A", "B"):
                    for h in range(2):
                        src = ps[:, 1 + n % 7, :].rearrange("p (b d) -> p b d", b=4)
                        v.wait_ge(s["mm"], n + 2)
                        if n:
                            v.wait_ge(s["gate"], n)
                        v.tensor_scalar(graw[:], src, 0.0, 2.0, ALU.is_ge, ALU.mult).then_inc(s["gsign"], 1)
                        v.wait_ge(s["gsign"], n + 1)
                        v.scalar_tensor_tensor(gabs[:], graw[:], -1.0, src, ALU.add, ALU.mult).then_inc(s["gabs"], 1)
                        v.wait_ge(s["gabs"], n + 1)
                        v.tensor_scalar(gmax[:], gabs[:], GATE_MIN, None, ALU.max).then_inc(s["gmax"], 1)
                        v.wait_ge(s["gmax"], n + 1)
                        v.scalar_tensor_tensor(sb[f"gate{ch}{layer}"][:, 4 * h:4 * h + 4, :], graw[:], -1.0, gmax[:],
                                               ALU.add, ALU.mult).then_inc(s["gate"], 1)
                        n += 1


def attention_phase(nc, dram, sb, layer):
    causal = layer == 0
    ph = f"at{layer}"
    x, ident, gate, mods = sb["x"], sb["ident"], sb[f"gateA{layer}"], sb["mods"]
    wqkv, bqk, wo, bv, bo_row = (sb[f"{n}{layer}"] for n in ("wqkv", "bqk", "wo", "bv", "bo"))
    with ExitStack() as ctx:
        def tile(name, shape, dt=F32):
            return ctx.enter_context(nc.sbuf_tensor(f"{ph}_{name}", shape, dt))

        QP = tile("QP", [R_ALL, 2, HEADS, SEQ], BF16)
        KP = tile("KP", [R_ALL, 2, HEADS, SEQ], BF16)
        E = tile("E", [P, TILES, GROUP, SEQ])
        VP = tile("VP", [P, 2, TILES, HEADS, VW])
        xn = tile("xn", [P, TILES, P])
        hT = tile("hT", [P, SEQ])
        parts = {n: tile(n, [P, SEQ], BF16) for n in ("q0", "q1", "q2", "k0", "k1", "k2")}
        rest = {n: tile(f"rest_{n}", [P, SEQ]) for n in "qk"}
        Oev = tile("Oev", [P, GROUPS, SEQ])
        ctxN = tile("ctxN", [P, SEQ])
        den = tile("den", [P, SEQ // 8])
        rden = tile("rden", [P, SEQ // 8])
        rden4 = tile("rden4", [GROUP, GROUPS * SEQ])
        denB = tile("denB", [P, SEQ])
        ctxT = tile("ctxT", [P, SEQ])
        gbo = tile("gbo", [P, P])
        t1 = tile("t1", [P, SEQ])
        st = tile("st", [P, TILES, 6])
        mv = tile("mv", [P, TILES, 2])
        ve = tile("ve", [P, TILES])
        rstd = tile("rstd", [P, TILES])
        mx = tile("mx", [P, 2, GROUP * TILES])
        nmx = tile("nmx", [P, 2, 2, GROUP * TILES], BF16)
        nrow = tile("nrow", [2 * GROUP * TILES, 2, P], BF16)
        idb = tile("idb", [P, P], BF16)
        wq_s = tile("wq_s", [P, D])
        bq_s = tile("bq_s", [P, 1])
        if causal:
            mask = tile("mask", [P, P], BF16)
        else:
            mask = tile("mask", [P, HEADS, P], BF16)
            factor = tile("factor", [P, HEADS, P])

        def bank(name, n=1):
            return ctx.enter_context(nc.psum_tensor(f"{ph}_{name}", [P, n, 512], F32))

        Mb, Sb, Ob, Tb = bank("Mb", 3), bank("Sb", 3), bank("Ob"), bank("Tb")

        s = semaphores(nc, ctx, ph, "const table zero ones wscale fac stats aggr veps rstd norm fill free hT p0 p1 p2 "
                 "rest maxs maxd nr0 nr1 nrow score exp diag vp pv oev gath compact rden rden4 dden ctx t1 gbo xup apart")
        pk, = ([ctx.enter_context(nc.semaphore(f"{ph}_{n}{g}")) for g in range(2)] for n in ("stacked",))
        mrow = [ctx.enter_context(nc.semaphore(f"{ph}_shift_rows{g}")) for g in range(GROUPS)]
        block = ctx.enter_context(nc.Block())

        scale = float(DK) ** -0.5

        def fill(b, name):
            if isinstance(b, int) and b == -1:
                return ["ln", "q", "k", "v", "m-2", "m-1"].index(name)
            order = ["ln", "q", "k", "v", "m0", "m1", "ctx", "m2", "m3"]
            if isinstance(b, int) and b == 0:
                order.remove("ctx")
                return 6 + order.index(name)
            if isinstance(b, int) and b == NBATCH - 1:
                order = ["m0", "m1", "ctx", "ctx_last"]
            return b * 9 + (5 + order.index(name))

        PER_M = GROUPS * GROUP * TILES
        UNITS = GROUPS * TILES
        VLAG = 2

        def before(n):
            return n - 3 if n >= 3 else (-1, -3, -2)[n]

        def groups_of(b, g):
            return (b, g + 2) if g < 2 else (b + 1, g - 2)

        last_b = NBATCH - 1

        def pairs(eng, steps):
            steps(0, 0)
            steps(1, 1)
            with eng.Fori(1, NBATCH // 2 - 1) as pair:
                steps(pair * 2, 0)
                steps(pair * 2 + 1, 1)
            steps(last_b - 1, 0)
            steps(last_b, 1)

        def is_last(b):
            return isinstance(b, int) and b == last_b

        def is_first(b):
            return isinstance(b, int) and b == 0

        @block.tensor
        def _(pe):
            def fill_wait(k):
                if not (isinstance(k, int) and k == 0):
                    pe.wait_ge(s["free"], k)

            def norm_T(bn, k):
                fill_wait(k)
                pe.wait_ge(s["norm"], bn + 1)
                for t in range(TILES):
                    last = pe.transpose(Tb[:, 0, t * P:(t + 1) * P], xn[:, t, :], ident[:])
                last.then_inc(s["fill"], 1)

            def project(which, bn, k):
                fill_wait(k)
                pe.wait_ge(s["hT"], bn + 1)
                if which == "v":
                    for t in range(TILES):
                        last = pe.matmul(Tb[:, 0, t * P:(t + 1) * P], hT[:, t * P:(t + 1) * P],
                                         wqkv[:, 2 * D:3 * D], start=True, stop=True)
                else:
                    w = wq_s[:] if which == "q" else wqkv[:, D:2 * D]
                    last = pe.matmul(Tb[:, 0, :], w, hT[:], start=True, stop=True)
                last.then_inc(s["fill"], 1)

            def max_scores(bm, gm, i, half):
                h = GROUP * gm + i
                if i == 0 and gm == 0:
                    for which in range(2):
                        pe.wait_ge(pk[which], 96 * (bm + 1))
                for qt in range(TILES):
                    n = (GROUP * gm + i) * TILES + qt
                    if not (isinstance(bm, int) and bm == 0 and n < 3):
                        pe.wait_ge(s["maxd"], bm * PER_M + (before(n) + 1))
                    width = (qt + 1) * P if causal else SEQ
                    out = Mb[:, n % 3, :]
                    pe.matmul(out[:, 0:width], QP[0:R_SHIFT, half, h, qt * P:(qt + 1) * P],
                              KP[0:R_SHIFT, half, h, 0:width],
                              start=True, stop=True)
                    pe.matmul(out[:, qt * P:(qt + 1) * P], idb[:], mask[:] if causal else mask[:, h, :],
                              start=False, stop=True, skip_group_check=True).then_inc(s["maxs"], 1)

            def max_T(bm, gm, k):
                fill_wait(k)
                pe.wait_ge(s["nr1"], GROUPS * bm + (gm + 1))
                pe.transpose(Tb[0:32, 0, 0:P // 2].bitcast(BF16), nmx[:, gm % 2].rearrange("p a c -> p (a c)"),
                             idb[:]).then_inc(s["fill"], 1)

            def key_scores(b, g, kt, half):
                if kt == 0:
                    pe.wait_ge(mrow[g], 16 * (b + 1))
                for i in range(GROUP):
                    h = GROUP * g + i
                    n = (GROUP * g + kt) * GROUP + i
                    if not (is_first(b) and n < 3):
                        pe.wait_ge(s["exp"], b * PER_M + (before(n) + 1))
                    q0 = kt * P if causal else 0
                    pe.matmul(Sb[:, n % 3, q0:SEQ], KP[:, half, h, kt * P:(kt + 1) * P], QP[:, half, h, q0:SEQ],
                              start=True, stop=True).then_inc(s["score"], 1)

            def values(bp, gp, kt, half):
                pe.wait_ge(s["diag"], UNITS * bp + (TILES * gp + kt + 1))
                if kt == 0:
                    if gp == 0:
                        pe.wait_ge(s["vp"], bp + 1)
                    if not (isinstance(bp, int) and bp == 0 and gp == 0):
                        pe.wait_ge(s["oev"], GROUPS * bp + gp)
                q0 = kt * P if causal else 0
                for i in range(GROUP):
                    last = pe.matmul(Ob[VW * i:VW * (i + 1), 0, q0:SEQ], VP[:, half, kt, GROUP * gp + i, :],
                                     E[:, kt, i, q0:SEQ], start=(kt == 0), stop=(kt == TILES - 1))
                last.then_inc(s["pv"], 1)

            def out_proj(bo, k):
                fill_wait(k)
                pe.wait_ge(s["ctx"], bo + 1)
                for t in range(TILES):
                    last = pe.matmul(Tb[:, 0, t * P:(t + 1) * P], ctxT[:, t * P:(t + 1) * P], wo[:],
                                     start=True, stop=True)
                last.then_inc(s["fill"], 1)

            def steps(b, half):
                for g in range(GROUPS):
                    bm, gm = groups_of(b, g)
                    bp, gp = (b, g - 1) if g else (b - 1, GROUPS - 1)
                    maxima = not (is_last(b) and g >= 2)
                    pro = g == 0 and not is_last(b)
                    for i in range(GROUP):
                        if pro and i == 1:
                            norm_T(b + 1, fill(b, "ln"))
                        if pro and i == 2:
                            project("q", b + 1, fill(b, "q"))
                        if pro and i == 3:
                            project("k", b + 1, fill(b, "k"))
                        if maxima:
                            max_scores(bm, gm, i, half if g < 2 else 1 - half)
                        key_scores(b, g, i, half)
                        if i >= VLAG:
                            values(b, g, i - VLAG, half)
                        elif not (is_first(b) and g == 0):
                            values(bp, gp, i + TILES - VLAG, half if g else 1 - half)
                        if g == 2 and i == 1 and not is_first(b):
                            out_proj(b - 1, fill(b, "ctx"))
                    if pro:
                        project("v", b + 1, fill(b, "v"))
                    if maxima:
                        max_T(bm, gm, fill(b, f"m{g}"))

            pe.wait_ge(s["wscale"], 1)
            pe.wait_ge(s["const"], 144)
            norm_T(0, 0)
            for k, which in enumerate("qkv"):
                project(which, 0, k + 1)
            for gm in range(2):
                for i in range(GROUP):
                    max_scores(0, gm, i, 0)
                max_T(0, gm, 4 + gm)
            pairs(pe, steps)
            for kt in range(TILES - VLAG, TILES):
                values(last_b, GROUPS - 1, kt, 1)
            out_proj(last_b, fill(last_b, "ctx_last"))

        @block.scalar
        def _(a):
            def read_hT(bn, k):
                a.wait_ge(s["fill"], k + 1)
                nc.scalar.activation(hT[:], Tb[:, 0, :], ACT.Identity, bias=mods[:, layer, 0, bass.ds(bn, 1)],
                                     scale=mods[:, layer, 1, bass.ds(bn, 1)]).then_inc(s["hT"], 1)
                a.wait_ge(s["hT"], bn + 1)
                a.sem_inc(s["free"], 1)

            def part0(which, bn, k):
                a.wait_ge(s["fill"], k + 1)
                if not (isinstance(bn, int) and bn == 0):
                    a.wait_ge(pk[0 if which == "q" else 1], 96 * bn)
                bias = bq_s[:] if which == "q" else bqk[:, 1:2]
                nc.scalar.activation(parts[f"{which}0"][:], Tb[:, 0, :], ACT.Identity, bias=bias).then_inc(s["p0"], 1)

            def shift_rows(bm, gm, k):
                a.wait_ge(s["fill"], k + 1)
                if not (isinstance(bm, int) and bm == 0 and gm < 2):
                    a.wait_ge(mrow[(gm - 2) % GROUPS], 16 * (bm + (1 if gm >= 2 else 0)))
                nc.scalar.activation(nrow[:, gm % 2, :], Tb[0:32, 0, 0:P // 2].bitcast(BF16), ACT.Copy)\
                  .then_inc(s["nrow"], 1)
                a.wait_ge(s["nrow"], GROUPS * bm + (gm + 1))
                a.sem_inc(s["free"], 1)

            def exps(b, g, kt):
                for i in range(GROUP):
                    n = (GROUP * g + kt) * GROUP + i
                    a.wait_ge(s["score"], b * PER_M + (n + 1))
                    if i == 0 and not (is_first(b) and g == 0):
                        a.wait_ge(s["pv"], UNITS * b + (TILES * (g - 1) + kt + 1))
                    q0 = kt * P if causal else 0
                    nc.scalar.activation(E[:, kt, i, q0:SEQ], Sb[:, n % 3, q0:SEQ], ACT.Exp).then_inc(s["exp"], 1)

            def read_O(bp, gp):
                a.wait_ge(s["pv"], UNITS * bp + TILES * (gp + 1))
                if gp == 0 and not (isinstance(bp, int) and bp == 0):
                    a.wait_ge(s["gath"], 64 * bp)
                    a.wait_ge(s["compact"], 16 * bp)
                nc.scalar.activation(Oev[:, gp, :], Ob[:, 0, :], ACT.Copy).then_inc(s["oev"], 1)

            def steps(b, half):
                for g in range(GROUPS):
                    pro = g == 0 and not is_last(b)
                    for i in range(GROUP):
                        exps(b, g, i)
                        if i == 0:
                            if g == 0:
                                shift_rows(b, 1, fill(-1, "m-1") if is_first(b) else b * 9 + 4)
                            elif not (is_last(b) and g == 3):
                                shift_rows(*groups_of(b, g - 1), fill(b, f"m{g - 1}"))
                        if i == 1 and not (is_first(b) and g == 0):
                            read_O(*((b, g - 1) if g else (b - 1, GROUPS - 1)))
                        if pro and i == 1:
                            read_hT(b + 1, fill(b, "ln"))
                        if pro and i == 2:
                            part0("q", b + 1, fill(b, "q"))
                        if pro and i == 3:
                            part0("k", b + 1, fill(b, "k"))

            if not causal:
                a.wait_ge(s["table"], 16)
                nc.scalar.activation(factor[:], factor[:], ACT.Exp).then_inc(s["fac"], 1)
            a.wait_ge(s["wscale"], 1)
            read_hT(0, 0)
            part0("q", 0, 1)
            part0("k", 0, 2)
            shift_rows(0, 0, 4)
            pairs(a, steps)
            read_O(last_b, GROUPS - 1)

        @block.vector
        def _(v):
            def stats(bn):
                for t in range(TILES):
                    last = v.bn_stats(st[:, t, :], x[:, bass.ds(bn * SEQ + t * P, P)])
                last.then_inc(s["stats"], 1)
                wait_apart(s, v, s["stats"], bn + 1)
                for t in range(TILES):
                    last = v.bn_aggr(mv[:, t, :], st[:, t, :])
                last.then_inc(s["aggr"], 1)
                v.wait_ge(s["aggr"], bn + 1)
                v.tensor_scalar(ve[:], mv[:, :, 1], EPS, None, ALU.add).then_inc(s["veps"], 1)

            def normalise(bn):
                v.wait_ge(s["rstd"], bn + 1)
                if not (isinstance(bn, int) and bn == 0):
                    v.wait_ge(s["hT"], bn)
                for t in range(TILES):
                    last = v.tensor_scalar(xn[:, t, :], x[:, bass.ds(bn * SEQ + t * P, P)], mv[:, t, 0:1],
                                           rstd[:, t:t + 1], ALU.subtract, ALU.mult)
                last.then_inc(s["norm"], 1)

            def remainder(which, bn):
                v.wait_ge(s["p0"], 2 * bn + (1 if which == "q" else 2))
                if not (isinstance(bn, int) and bn == 0):
                    v.wait_ge(s["p2"], 2 * bn)
                bias = bq_s[:] if which == "q" else bqk[:, 1:2]
                v.scalar_tensor_tensor(rest[which][:], Tb[:, 0, :], bias, parts[f"{which}0"][:],
                                       ALU.add, ALU.subtract).then_inc(s["rest"], 1)
                v.wait_ge(s["rest"], 2 * bn + (1 if which == "q" else 2))
                v.sem_inc(s["free"], 1)

            def read_V(bn, half, k):
                v.wait_ge(s["fill"], k + 1)
                if not (isinstance(bn, int) and bn < 2):
                    v.wait_ge(s["pv"], UNITS * bn - UNITS)
                v.tensor_tensor(VP[:, half, :, :, 0:DK], Tb[:, 0, :].rearrange("p (t h d) -> p t h d", t=TILES, h=HEADS),
                                both(bv[:], TILES).rearrange("p t (h d) -> p t h d", h=HEADS), ALU.add).then_inc(s["vp"], 1)
                v.wait_ge(s["vp"], bn + 1)
                v.sem_inc(s["free"], 1)

            def reduce_max(bm, gm, i):
                for qt in range(TILES):
                    n = (GROUP * gm + i) * TILES + qt
                    v.wait_ge(s["maxs"], bm * PER_M + (n + 1))
                    if i == 0 and qt == 0 and not (isinstance(bm, int) and bm == 0 and gm < 2):
                        v.wait_ge(s["nrow"], GROUPS * bm + (gm - 1))
                    width = (qt + 1) * P if causal else SEQ
                    v.tensor_reduce(mx[:, gm % 2, i * TILES + qt:i * TILES + qt + 1], Mb[:, n % 3, 0:width],
                                    AX.X, ALU.max).then_inc(s["maxd"], 1)

            def negate(bm, gm):
                v.wait_ge(s["maxd"], bm * PER_M + 16 * (gm + 1))
                v.tensor_scalar(nmx[:, gm % 2, 0, :], mx[:, gm % 2, :], -1.0, None, ALU.mult).then_inc(s["nr0"], 1)
                v.wait_ge(s["nr0"], GROUPS * bm + (gm + 1))
                v.scalar_tensor_tensor(nmx[:, gm % 2, 1, :], mx[:, gm % 2, :], -1.0, nmx[:, gm % 2, 0, :],
                                       ALU.mult, ALU.subtract).then_inc(s["nr1"], 1)

            def recip(bo):
                v.wait_ge(s["compact"], 16 * (bo + 1))
                if not (isinstance(bo, int) and bo == 0):
                    v.wait_ge(s["rden4"], 16 * bo)
                v.reciprocal(rden[:], den[:]).then_inc(s["rden"], 1)

            def context(bo):
                v.wait_ge(s["gath"], 64 * (bo + 1))
                v.wait_ge(s["dden"], 64 * (bo + 1))
                if not (isinstance(bo, int) and bo == 0):
                    v.wait_ge(s["t1"], bo)
                v.tensor_tensor(ctxT[:], ctxN[:], denB[:], ALU.mult).then_inc(s["ctx"], 1)

            def gated(bo, k):
                v.wait_ge(s["fill"], k + 1)
                if not (isinstance(bo, int) and bo == 0):
                    v.wait_ge(s["xup"], bo)
                v.tensor_tensor(t1[:].rearrange("p (t d) -> p t d", t=TILES),
                                Tb[:, 0, :].rearrange("p (t d) -> p t d", t=TILES),
                                gate[:, bass.ds(bo, 1), :].to_broadcast([P, TILES, P]), ALU.mult).then_inc(s["t1"], 1)
                v.wait_ge(s["t1"], bo + 1)
                v.sem_inc(s["free"], 1)

            def steps(b, half):
                for g in range(GROUPS):
                    bm, gm = groups_of(b, g)
                    maxima = not (is_last(b) and g >= 2)
                    pro = g == 0 and not is_last(b)
                    if pro:
                        stats(b + 1)
                    for i in range(GROUP):
                        if maxima:
                            reduce_max(bm, gm, i)
                        if i == 0:
                            if pro:
                                normalise(b + 1)
                        if pro and i == 2:
                            remainder("q", b + 1)
                        if pro and i == 3:
                            remainder("k", b + 1)
                        if not is_first(b):
                            if g == 0 and i == 3:
                                recip(b - 1)
                            if g == 1 and i == 2:
                                context(b - 1)
                            if g == 2 and i == 2:
                                gated(b - 1, fill(b, "ctx"))
                    if maxima:
                        negate(bm, gm)
                    if pro:
                        read_V(b + 1, 1 - half, fill(b, "v"))

            stats(0)
            v.tensor_scalar(wq_s[:], wqkv[:, 0:D], scale, None, ALU.mult)
            v.tensor_copy(idb[:], ident[:])
            v.tensor_scalar(bq_s[:], bqk[:, 0:1], scale, None, ALU.mult).then_inc(s["wscale"], 1)
            v.wait_ge(s["wscale"], 1)
            normalise(0)
            remainder("q", 0)
            remainder("k", 0)
            v.wait_ge(s["zero"], 2)
            read_V(0, 0, 3)
            for gm in range(2):
                for i in range(GROUP):
                    reduce_max(0, gm, i)
                negate(0, gm)
            pairs(v, steps)
            recip(last_b)
            context(last_b)
            gated(last_b, fill(last_b, "ctx_last"))

        @block.gpsimd
        def _(p):
            def powers(bn):
                p.wait_ge(s["veps"], bn + 1)
                p.tensor_tensor(rstd[:], ve[:], sb["mhalf"][:], ALU.pow).then_inc(s["rstd"], 1)

            def split(which, bn):
                k = 2 * bn + (1 if which == "q" else 2)
                if not (isinstance(bn, int) and bn == 0):
                    p.wait_ge(pk[0 if which == "q" else 1], 96 * bn)
                wait_apart(s, p, s["rest"], k)
                p.tensor_scalar(parts[f"{which}1"][:], rest[which][:], 1.0, None, ALU.mult).then_inc(s["p1"], 1)
                wait_apart(s, p, s["p1"], k)
                p.tensor_tensor(parts[f"{which}2"][:], rest[which][:], parts[f"{which}1"][:],
                                ALU.subtract).then_inc(s["p2"], 1)

            def diagonal(b, g, kt):
                wait_apart(s, p, s["exp"], b * PER_M + (GROUP * g + kt + 1) * GROUP)
                blocks = E[:, kt, :, kt * P:(kt + 1) * P]
                if causal:
                    p.affine_select(out=blocks, in_=blocks, compare_op=ALU.is_ge, fill=0.0, base=0,
                                    pattern=[[0, GROUP], [1, P]], channel_multiplier=-1).then_inc(s["diag"], 1)
                else:
                    p.tensor_tensor(blocks, blocks, factor[:, GROUP * g:GROUP * (g + 1), :],
                                    ALU.mult).then_inc(s["diag"], 1)

            def update_x(bo):
                xb = x[:, bass.ds(bo * SEQ, SEQ)]
                p.tensor_tensor(gbo[:].unsqueeze(1), gate[:, bass.ds(bo, 1), :], bo_row[:].unsqueeze(1),
                                ALU.mult).then_inc(s["gbo"], 1)
                wait_apart(s, p, s["t1"], bo + 1)
                p.tensor_tensor(xb, xb, t1[:], ALU.add).then_inc(s["xup"], 1)
                p.wait_ge(s["xup"], bo + 1)
                wait_apart(s, p, s["gbo"], bo + 1)
                xv = xb.rearrange("p (t d) -> p t d", t=TILES)
                p.tensor_tensor(xv, xv, both(gbo[:], TILES), ALU.add)

            def steps(b, half):
                for g in range(GROUPS):
                    pro = g == 0 and not is_last(b)
                    if pro:
                        powers(b + 1)
                    for i in range(GROUP):
                        diagonal(b, g, i)
                        if pro and i == 2:
                            split("q", b + 1)
                        if pro and i == 3:
                            split("k", b + 1)
                    if g == 2 and not is_first(b):
                        update_x(b - 1)

            p.memset(VP[:], 0.0).then_inc(s["zero"], 1)
            p.wait_ge(s["zero"], 1)
            p.memset(VP[:, :, :, :, DENS:DENS + 1], 1.0).then_inc(s["zero"], 1)
            if not causal:
                p.wait_ge(s["fac"], 1)
            powers(0)
            split("q", 0)
            split("k", 0)
            pairs(p, steps)
            update_x(last_b)

        @block.sync
        def _(sp):
            def stack(bn, half, which):
                if not (isinstance(bn, int) and bn < 2):
                    wait_apart(s, sp, s["score"], PER_M * bn - PER_M)
                k = 2 * bn + (1 + which)
                sp.wait_ge(s["p2"], k)
                sp.wait_ge(s["p0"], k)
                for r in range(6):
                    dst = (QP, KP)[which]
                    part = parts["qk"[which] + str((Q_PARTS, K_PARTS)[which][r])]
                    sp.dma_start(dst[8 * r:8 * r + 8, half, :, :], part[:]).then_inc(pk[which], 16)

            def send_rows(bm, gm, half):
                sp.wait_ge(s["nrow"], GROUPS * bm + (gm + 1))
                sp.dma_start(QP[R_SHIFT + 1:R_ALL, half, GROUP * gm:GROUP * (gm + 1), :],
                             nrow[:, gm % 2, :]).then_inc(mrow[gm], 16)

            def gather(bo):
                wait_apart(s, sp, s["oev"], GROUPS * (bo + 1))
                if not (isinstance(bo, int) and bo == 0):
                    sp.wait_ge(s["ctx"], bo)
                sp.dma_start(den[:], Oev[DENS::VW, :, :]).then_inc(s["compact"], 16)
                for i in range(GROUP):
                    sp.dma_start(ctxN[32 * i:32 * i + 32, :], Oev[VW * i:VW * i + DK, :, :]).then_inc(s["gath"], 16)

            def spread(bo):
                sp.wait_ge(s["rden"], bo + 1)
                sp.dma_start(rden4[:], rden[:]).then_inc(s["rden4"], 16)
                sp.wait_ge(s["rden4"], 16 * (bo + 1))
                for g in range(GROUPS):
                    sp.dma_start(denB[g::GROUPS, :],
                                 rden4[:, g * SEQ:(g + 1) * SEQ].unsqueeze(1).to_broadcast([GROUP, DK, SEQ]))\
                      .then_inc(s["dden"], 16)

            def steps(b, half):
                for g in range(GROUPS):
                    if g == 0:
                        send_rows(b, 1, half)
                    elif not (is_last(b) and g == 3):
                        send_rows(*groups_of(b, g - 1), half if g < 3 else 1 - half)
                    if g == 0 and not is_first(b):
                        gather(b - 1)
                    if g < 2 and not is_last(b):
                        stack(b + 1, 1 - half, g)
                    if g == 1 and not is_first(b):
                        spread(b - 1)

            for half in range(2):
                sp.dma_start(QP[R_ALIBI:R_SHIFT, half], dram[f"aliq{layer}"]).then_inc(s["const"], 16)
                sp.dma_start(KP[R_ALIBI:R_SHIFT, half], dram[f"alik{layer}"]).then_inc(s["const"], 16)
                sp.dma_start(QP[R_SHIFT:R_SHIFT + 1, half], dram[f"shiftq{layer}"]).then_inc(s["const"], 16)
                sp.dma_start(KP[R_SHIFT:R_ALL, half], dram["ones3"]).then_inc(s["const"], 16)
            sp.dma_start(mask[:], dram[f"mask{layer}"]).then_inc(s["const"], 16)
            if not causal:
                sp.dma_start(factor[:], dram["alibi"]).then_inc(s["table"], 16)
            stack(0, 0, 0)
            stack(0, 0, 1)
            send_rows(0, 0, 0)
            pairs(sp, steps)
            gather(last_b)
            spread(last_b)


def expert_phase(nc, dram, sb):
    x, ident, gate, mods = sb["x"], sb["ident"], sb["gateB0"], sb["mods"]
    gate_w, gate_b, iota8, b1, b3 = (sb[n] for n in ("gate_w", "gate_b", "iota8", "b1", "b3"))
    R_LOW = 64
    R_ROWS = R_LOW + ALL_EXP
    with ExitStack() as ctx:
        def tile(name, shape, dt=F32):
            return ctx.enter_context(nc.sbuf_tensor(f"ex_{name}", shape, dt))

        raw = {n: tile(n, [P, HPAD]) for n in ("w1", "w3")}
        hi = {n: tile(f"{n}_hi", [P, HPAD], F32R) for n in ("w1", "w3")}
        lo = {n: tile(f"{n}_lo", [P, HPAD], F32R) for n in ("w1", "w3")}
        sel = tile("sel", [R_ROWS, HPAD])
        selr = tile("selr", [R_ROWS, HPAD], F32R)
        w2 = tile("w2", [P, HTILES, D])
        b2x2 = tile("b2x2", [ALL_EXP, D])
        st = tile("st", [P, TILES, 6])
        mv = tile("mv", [P, TILES, 2])
        ve = tile("ve", [P, TILES])
        rstd = tile("rstd", [P, TILES])
        xn = tile("xn", [P, TILES, P])
        hT = tile("hT", [P, SEQ])
        h_hi = tile("h_hi", [P, 2, SEQ], F32R)
        h_lo = tile("h_lo", [P, 2, SEQ], F32R)
        top = tile("top", [P, TILES])
        lg = tile("lg", [P, TILES, EXPERTS])
        ex = tile("ex", [P, TILES, EXPERTS])
        sm = tile("sm", [P, TILES])
        rs = tile("rs", [P, TILES])
        sc = tile("sc", [P, TILES, EXPERTS])
        bi = tile("bi", [P, TILES, EXPERTS])
        m8 = tile("m8", [P, TILES, 8])
        i8 = tile("i8", [P, TILES, 8], U32)
        i8f = tile("i8f", [P, TILES, 8])
        k1 = tile("k1", [P, TILES, EXPERTS])
        k2 = tile("k2", [P, TILES, EXPERTS])
        k12 = tile("k12", [P, TILES, EXPERTS])
        rw = tile("rw", [P, TILES, ALL_EXP])
        rwT = tile("rwT", [ALL_EXP, 2, SEQ])
        rwr = tile("rwr", [P, 2, SEQ], F32R)
        up3 = tile("up3", [P, 2, SEQ])
        z = tile("z", [P, 2, SEQ])
        th = tile("th", [P, 2, SEQ])
        zr = tile("zr", [P, 2, SEQ])
        hh = tile("hh", [P, 2, SEQ])
        t1 = tile("t1", [P, SEQ])

        def bank(name, n=1):
            return ctx.enter_context(nc.psum_tensor(f"ex_{name}", [P, n, 512], F32))

        Ab, Bb, Rb, Yb, Tb = bank("Ab", 2), bank("Bb", 2), bank("Rb", 2), bank("Yb"), bank("Tb")
        s = semaphores(nc, ctx, "ex", "load load2 zero hi1 lo1 hi3 lo3 selr b2 stats aggr veps rstd norm fill free hT hhi hlo "
                 "ch exp rwT rhi rlo up u3 z th zr hh down y t1 xup apart")
        block = ctx.enter_context(nc.Block())
        N = HTILES
        last_b = NBATCH - 1

        def is_int(b, k):
            return isinstance(b, int) and b == k

        CH_PER = 14

        LN, LOGITS, RW = range(3)

        def pairs(eng, body):
            body(0, 0)
            body(1, 1)
            with eng.Fori(1, NBATCH // 2 - 1) as pair:
                body(pair * 2, 0)
                body(pair * 2 + 1, 1)
            body(last_b - 1, 0)
            body(last_b, 1)

        @block.sync
        def _(sp):
            sp.dma_start(raw["w1"][:], dram["w1"]).then_inc(s["load"], 16)
            sp.dma_start(raw["w3"][:], dram["w3"]).then_inc(s["load"], 16)
            sp.dma_start(sel[:], dram["sel"]).then_inc(s["load"], 16)
            sp.dma_start(w2[:], dram["w2"]).then_inc(s["load2"], 16)

        @block.gpsimd
        def _(p):
            def powers(bn):
                p.wait_ge(s["veps"], bn + 1)
                p.tensor_tensor(rstd[:], ve[:], sb["mhalf"][:], ALU.pow).then_inc(s["rstd"], 1)

            def split(bn, half):
                if not (isinstance(bn, int) and bn < 2):
                    p.wait_ge(s["up"], N * bn - N)
                wait_apart(s, p, s["hT"], bn + 1)
                p.tensor_scalar(h_hi[:, half, :], hT[:], 1.0, None, ALU.mult).then_inc(s["hhi"], 1)
                p.wait_ge(s["hhi"], bn + 1)
                p.tensor_tensor(h_lo[:, half, :], hT[:], h_hi[:, half, :].bitcast(F32), ALU.subtract)\
                 .then_inc(s["hlo"], 1)

            def update_x(b):
                xb = x[:, bass.ds(b * SEQ, SEQ)]
                wait_apart(s, p, s["t1"], b + 1)
                p.tensor_tensor(xb, xb, t1[:], ALU.add).then_inc(s["xup"], 1)

            def body(b, half):
                if not is_int(b, last_b):
                    powers(b + 1)
                    split(b + 1, 1 - half)
                if not is_int(b, 0):
                    update_x(b - 1)

            p.memset(rwr[:].bitcast(F32), 0.0).then_inc(s["zero"], 1)
            powers(0)
            split(0, 0)
            p.wait_ge(s["load"], 48)
            p.wait_ge(s["hi3"], 1)
            p.tensor_tensor(lo["w3"][:], raw["w3"][:], hi["w3"][:].bitcast(F32), ALU.subtract).then_inc(s["lo3"], 1)
            pairs(p, body)
            update_x(last_b)

        @block.scalar
        def _(a):
            def read_hT(bn):
                a.wait_ge(s["fill"], 3 * bn + (LN + 1))
                if not is_int(bn, 0):
                    a.wait_ge(s["hlo"], bn)
                nc.scalar.activation(hT[:], Tb[:, 0, :], ACT.Identity, bias=mods[:, 0, 2, bass.ds(bn, 1)],
                                     scale=mods[:, 0, 3, bass.ds(bn, 1)]).then_inc(s["hT"], 1)
                a.wait_ge(s["hT"], bn + 1)
                a.sem_inc(s["free"], 1)

            def route_exp(bn):
                a.wait_ge(s["ch"], CH_PER * bn + 2)
                nc.scalar.activation(ex[:], lg[:], ACT.Exp).then_inc(s["exp"], 1)

            def read_rw(bn, half):
                a.wait_ge(s["fill"], 3 * bn + (RW + 1))
                if not (isinstance(bn, int) and bn < 2):
                    a.wait_ge(s["y"], bn - 1)
                nc.scalar.activation(rwT[:, half, :], Tb[0:ALL_EXP, 0, :], ACT.Copy).then_inc(s["rwT"], 1)

            def up_bias(b, j, n):
                q = (13 * (n % 2) + j) % 2
                a.wait_ge(s["up"], N * b + (j + 1))
                if not (is_int(b, 0) and j < 2):
                    a.wait_ge(s["z"], N * b + (j - 1))
                nc.scalar.activation(up3[:, q, :], Bb[:, q, :], ACT.Identity, bias=b3[:, j:j + 1]).then_inc(s["u3"], 1)

            def tanh(b, j, n):
                q = (13 * (n % 2) + j) % 2
                a.wait_ge(s["z"], N * b + (j + 1))
                if not (is_int(b, 0) and j < 2):
                    a.wait_ge(s["hh"], N * b + (j - 1))
                nc.scalar.activation(th[:, q, :], z[:, q, :], ACT.Tanh, scale=0.5).then_inc(s["th"], 1)

            def body(b, half):
                for j in range(N):
                    up_bias(b, j, half)
                    if j > 0:
                        tanh(b, j - 1, half)
                    elif not is_int(b, 0):
                        tanh(b - 1, N - 1, 1 - half)
                    if not is_int(b, last_b):
                        if j == 3:
                            read_hT(b + 1)
                        if j == 6:
                            route_exp(b + 1)
                        if j == 10:
                            read_rw(b + 1, 1 - half)

            a.wait_ge(s["load"], 48)
            nc.scalar.activation(hi["w3"][:], raw["w3"][:], ACT.Copy).then_inc(s["hi3"], 1)
            read_hT(0)
            nc.scalar.activation(selr[:], sel[:], ACT.Copy).then_inc(s["selr"], 1)
            route_exp(0)
            read_rw(0, 0)
            pairs(a, body)
            tanh(last_b, N - 1, 1)

        @block.vector
        def _(v):
            def stats(bn):
                for t in range(TILES):
                    last = v.bn_stats(st[:, t, :], x[:, bass.ds(bn * SEQ + t * P, P)])
                last.then_inc(s["stats"], 1)
                wait_apart(s, v, s["stats"], bn + 1)
                for t in range(TILES):
                    last = v.bn_aggr(mv[:, t, :], st[:, t, :])
                last.then_inc(s["aggr"], 1)
                v.wait_ge(s["aggr"], bn + 1)
                v.tensor_scalar(ve[:], mv[:, :, 1], EPS, None, ALU.add).then_inc(s["veps"], 1)

            def normalise(bn):
                v.wait_ge(s["rstd"], bn + 1)
                if not is_int(bn, 0):
                    v.wait_ge(s["hT"], bn)
                for t in range(TILES):
                    last = v.tensor_scalar(xn[:, t, :], x[:, bass.ds(bn * SEQ + t * P, P)], mv[:, t, 0:1],
                                           rstd[:, t:t + 1], ALU.subtract, ALU.mult)
                last.then_inc(s["norm"], 1)

            def route(bn):
                def step(ins, k):
                    ins.then_inc(s["ch"], 1)
                    if k in (6, 7):
                        wait_apart(s, v, s["ch"], CH_PER * bn + k)
                    else:
                        v.wait_ge(s["ch"], CH_PER * bn + k)

                logits = Tb[:, 0, 0:TILES * EXPERTS].rearrange("p (t e) -> p t e", t=TILES)
                v.wait_ge(s["fill"], 3 * bn + (LOGITS + 1))
                if not is_int(bn, 0):
                    v.wait_ge(s["exp"], bn)
                step(v.tensor_reduce(top[:], logits, AX.X, ALU.max), 1)
                step(v.tensor_tensor(lg[:], logits, each(top[:], EXPERTS), ALU.subtract), 2)
                v.sem_inc(s["free"], 1)
                v.wait_ge(s["exp"], bn + 1)
                step(v.tensor_reduce(sm[:], ex[:], AX.X, ALU.add), 3)
                step(v.reciprocal(rs[:], sm[:]), 4)
                step(v.tensor_tensor(sc[:], ex[:], each(rs[:], EXPERTS), ALU.mult), 5)
                step(v.tensor_tensor(bi[:], sc[:], both(gate_b[:], TILES), ALU.add), 6)
                for t in range(TILES):
                    last = v.max(m8[:, t, :], bi[:, t, :])
                step(last, 7)
                for t in range(TILES):
                    last = v.max_index(i8[:, t, :], m8[:, t, :], bi[:, t, :])
                step(last, 8)
                step(v.tensor_copy(i8f[:], i8[:]), 9)
                step(v.tensor_tensor(k1[:], both(iota8[:], TILES), i8f[:, :, 0:1].to_broadcast([P, TILES, EXPERTS]),
                                     ALU.is_equal), 10)
                step(v.tensor_tensor(k2[:], both(iota8[:], TILES), i8f[:, :, 1:2].to_broadcast([P, TILES, EXPERTS]),
                                     ALU.is_equal), 11)
                step(v.tensor_tensor(k12[:], k1[:], k2[:], ALU.add), 12)
                step(v.memset(rw[:, :, EXPERTS:ALL_EXP], 0.5), 13)
                step(v.scalar_tensor_tensor(rw[:, :, 0:EXPERTS], sc[:], 0.5, k12[:], ALU.mult, ALU.mult), 14)

            def split_rw(bn, half):
                v.wait_ge(s["fill"], 3 * bn + (RW + 1))
                v.wait_ge(s["rwT"], bn + 1)
                if not (isinstance(bn, int) and bn < 2):
                    v.wait_ge(s["up"], N * bn - N)
                v.tensor_scalar(rwr[0:ALL_EXP, half, :], Tb[0:ALL_EXP, 0, :], 1.0, None, ALU.mult).then_inc(s["rhi"], 1)
                v.wait_ge(s["rhi"], bn + 1)
                v.tensor_tensor(rwr[R_LOW:R_ROWS, half, :], Tb[0:ALL_EXP, 0, :],
                                rwr[0:ALL_EXP, half, :].bitcast(F32), ALU.subtract).then_inc(s["rlo"], 1)
                v.wait_ge(s["rlo"], bn + 1)
                v.sem_inc(s["free"], 1)

            def product(b, j, n):
                q = (13 * (n % 2) + j) % 2
                v.wait_ge(s["u3"], N * b + (j + 1))
                if not (is_int(b, 0) and j < 2):
                    v.wait_ge(s["th"], N * b + (j - 1))
                v.scalar_tensor_tensor(z[:, q, :], Ab[:, q, :], b1[:, j:j + 1], up3[:, q, :],
                                       ALU.add, ALU.mult).then_inc(s["z"], 1)
                v.wait_ge(s["z"], N * b + (j + 1))
                v.tensor_tensor(zr[:, q, :], Rb[:, q, :], z[:, q, :], ALU.mult).then_inc(s["zr"], 1)

            def hidden(b, j, n):
                q = (13 * (n % 2) + j) % 2
                v.wait_ge(s["th"], N * b + (j + 1))
                v.wait_ge(s["zr"], N * b + (j + 1))
                if not (is_int(b, 0) and j < 2):
                    v.wait_ge(s["down"], N * b + (j - 1))
                v.scalar_tensor_tensor(hh[:, q, :], th[:, q, :], 1.0, zr[:, q, :], ALU.add, ALU.mult)\
                 .then_inc(s["hh"], 1)

            def gated(b):
                v.wait_ge(s["y"], b + 1)
                if not is_int(b, 0):
                    v.wait_ge(s["xup"], b)
                v.tensor_tensor(t1[:].rearrange("p (t d) -> p t d", t=TILES),
                                Yb[:, 0, :].rearrange("p (t d) -> p t d", t=TILES),
                                gate[:, bass.ds(b, 1), :].to_broadcast([P, TILES, P]), ALU.mult).then_inc(s["t1"], 1)

            def body(b, half):
                for j in range(N):
                    product(b, j, half)
                    if j > 0:
                        hidden(b, j - 1, half)
                    elif not is_int(b, 0):
                        hidden(b - 1, N - 1, 1 - half)
                    if j == 1 and not is_int(b, 0):
                        gated(b - 1)
                    if not is_int(b, last_b):
                        if j == 0:
                            stats(b + 1)
                        if j == 2:
                            normalise(b + 1)
                        if j == 6:
                            route(b + 1)
                        if j == 10:
                            split_rw(b + 1, 1 - half)

            stats(0)
            v.wait_ge(s["load"], 48)
            v.tensor_scalar(hi["w1"][:], raw["w1"][:], 1.0, None, ALU.mult).then_inc(s["hi1"], 1)
            normalise(0)
            v.wait_ge(s["hi1"], 1)
            v.tensor_tensor(lo["w1"][:], raw["w1"][:], hi["w1"][:].bitcast(F32), ALU.subtract).then_inc(s["lo1"], 1)
            v.tensor_scalar(b2x2[:], sb["b2"][:], 2.0, None, ALU.mult).then_inc(s["b2"], 1)
            route(0)
            v.wait_ge(s["zero"], 1)
            split_rw(0, 0)
            pairs(v, body)
            hidden(last_b, N - 1, 1)
            gated(last_b)

        @block.tensor
        def _(pe):
            def norm_T(bn):
                if not is_int(bn, 0):
                    pe.wait_ge(s["free"], 3 * bn + LN)
                pe.wait_ge(s["norm"], bn + 1)
                for t in range(TILES):
                    last = pe.transpose(Tb[:, 0, t * P:(t + 1) * P], xn[:, t, :], ident[:])
                last.then_inc(s["fill"], 1)

            def logits(bn):
                pe.wait_ge(s["free"], 3 * bn + LOGITS)
                pe.wait_ge(s["hT"], bn + 1)
                for t in range(TILES):
                    last = pe.matmul(Tb[:, 0, t * EXPERTS:(t + 1) * EXPERTS], hT[:, t * P:(t + 1) * P], gate_w[:],
                                     start=True, stop=True)
                last.then_inc(s["fill"], 1)

            def rw_T(bn):
                pe.wait_ge(s["free"], 3 * bn + RW)
                pe.wait_ge(s["ch"], CH_PER * (bn + 1))
                for t in range(TILES):
                    last = pe.transpose(Tb[0:ALL_EXP, 0, t * P:(t + 1) * P], rw[:, t, :], ident[:])
                last.then_inc(s["fill"], 1)

            def up(b, j, half):
                q = (13 * half + j) % 2
                if j == 0:
                    pe.wait_ge(s["hlo"], b + 1)
                    pe.wait_ge(s["rlo"], b + 1)
                if not (is_int(b, 0) and j < 2):
                    pe.wait_ge(s["zr"], N * b + (j - 1))
                cols = slice(j * P, (j + 1) * P)
                for bankk, w in ((Ab, "w1"), (Bb, "w3")):
                    pe.matmul(bankk[:, q, :], hi[w][:, cols], h_hi[:, half, :], start=True, stop=False)
                    pe.matmul(bankk[:, q, :], hi[w][:, cols], h_lo[:, half, :], start=False, stop=False)
                    pe.matmul(bankk[:, q, :], lo[w][:, cols], h_hi[:, half, :], start=False, stop=True)
                pe.matmul(Rb[:, q, :], selr[:, cols], rwr[0:R_ROWS, half, :], start=True, stop=True)\
                  .then_inc(s["up"], 1)

            def down(b, j, half):
                q = (13 * half + j) % 2
                pe.wait_ge(s["hh"], N * b + (j + 1))
                if j == 0:
                    if not is_int(b, 0):
                        pe.wait_ge(s["t1"], b)
                    for t in range(TILES):
                        pe.matmul(Yb[:, 0, t * P:(t + 1) * P], rwT[:, half, t * P:(t + 1) * P], b2x2[:],
                                  start=(t == 0), stop=False, skip_group_check=True)
                for t in range(TILES):
                    last = pe.matmul(Yb[:, 0, t * P:(t + 1) * P], hh[:, q, t * P:(t + 1) * P], w2[:, j, :],
                                     start=False, stop=(j == N - 1), skip_group_check=True)
                last.then_inc(s["down"], 1)
                if j == N - 1:
                    pe.wait_ge(s["down"], N * b + N)
                    pe.sem_inc(s["y"], 1)

            def body(b, half):
                for j in range(N):
                    up(b, j, half)
                    if j >= 2:
                        down(b, j - 2, half)
                    elif not is_int(b, 0):
                        down(b - 1, N - 2 + j, 1 - half)
                    if not is_int(b, last_b):
                        if j == 3:
                            norm_T(b + 1)
                        if j == 5:
                            logits(b + 1)
                        if j == 9:
                            rw_T(b + 1)

            norm_T(0)
            logits(0)
            rw_T(0)
            pe.wait_ge(s["load2"], 16)
            pe.wait_ge(s["selr"], 1)
            pe.wait_ge(s["b2"], 1)
            pe.wait_ge(s["lo1"], 1)
            pe.wait_ge(s["lo3"], 1)
            pairs(pe, body)
            down(last_b, N - 2, 1)
            down(last_b, N - 1, 1)


def spike_phase(nc, dram, sb, out):
    x, ident, gate, mods = (sb[n] for n in ("x", "ident", "gateB1", "mods"))
    FT = FFN // P
    last_b = NBATCH - 1
    with ExitStack() as ctx:
        def tile(name, shape, dt=F32):
            return ctx.enter_context(nc.sbuf_tensor(f"sp_{name}", shape, dt))

        wfc = tile("wfc", [P, FFN])
        wproj = tile("wproj", [P, FFN // P, D])

        st = tile("st", [P, TILES, 6])
        mv = tile("mv", [P, TILES, 2])
        ve = tile("ve", [P, TILES])
        rstd = tile("rstd", [P, TILES])
        xn = tile("xn", [P, TILES, P])
        hT = tile("hT", [P, SEQ])
        relu = tile("relu", [P, 2, SEQ])
        sq = tile("sq", [P, 2, SEQ])
        y = tile("y", [P, SEQ])
        drive = tile("drive", [P, SEQ])
        nmem = tile("nmem", [P, 2, SEQ])
        cnt = tile("cnt", [P, 2, SEQ])
        t1 = tile("t1", [P, SEQ])

        def bank(name, n=1):
            return ctx.enter_context(nc.psum_tensor(f"sp_{name}", [P, n, 512], F32))

        Ub, Yb, Tb = bank("Ub", 2), bank("Yb", 2), bank("Tb")
        s = semaphores(nc, ctx, "sp", "load stats aggr veps rstd norm fill hT up relu sq down y yread ch t1 xup store apart")
        block = ctx.enter_context(nc.Block())

        def is_int(b, k):
            return isinstance(b, int) and b == k

        def loop(eng, body):
            body(0)
            with eng.Fori(1, last_b) as b:
                body(b)
            body(last_b)

        @block.gpsimd
        def _(p):
            def powers(bn):
                p.wait_ge(s["veps"], bn + 1)
                p.tensor_tensor(rstd[:], ve[:], sb["mhalf"][:], ALU.pow).then_inc(s["rstd"], 1)

            def update_x(b):
                xb = x[:, bass.ds(b * SEQ, SEQ)]
                wait_apart(s, p, s["t1"], b + 1)
                p.tensor_tensor(xb, xb, t1[:], ALU.add).then_inc(s["xup"], 1)

            def body(b):
                if not is_int(b, last_b):
                    powers(b + 1)
                update_x(b)

            powers(0)
            loop(p, body)

        @block.sync
        def _(sp):
            def body(b):
                sp.wait_ge(s["xup"], b + 1)
                sp.dma_start(out[bass.ds(b, 1)].rearrange("b (t p) d -> p (b t) d", p=P),
                             x[:, bass.ds(b * SEQ, SEQ)].rearrange("p (t d) -> p t d", t=TILES)).then_inc(s["store"], 16)
            sp.dma_start(wfc[:], dram["wfc"]).then_inc(s["load"], 16)
            sp.dma_start(wproj[:], dram["wproj"]).then_inc(s["load"], 16)
            loop(sp, body)
            sp.wait_ge(s["store"], 16 * NBATCH)

        @block.tensor
        def _(pe):
            def norm_T(bn):
                if not is_int(bn, 0):
                    pe.wait_ge(s["hT"], bn)
                pe.wait_ge(s["norm"], bn + 1)
                for t in range(TILES):
                    last = pe.transpose(Tb[:, 0, t * P:(t + 1) * P], xn[:, t, :], ident[:])
                last.then_inc(s["fill"], 1)

            def down(b, f):
                pe.wait_ge(s["sq"], FT * b + (f + 1))
                if f == 0 and not is_int(b, 0):
                    pe.wait_ge(s["yread"], b)
                for t in range(TILES):
                    last = pe.matmul(Yb[:, 0, t * P:(t + 1) * P], sq[:, f % 2, t * P:(t + 1) * P], wproj[:, f, :],
                                     start=(f == 0 and t == 0), stop=(f == FT - 1), skip_group_check=True)
                last.then_inc(s["down"], 1)

            def body(b):
                pe.wait_ge(s["hT"], b + 1)
                for f in range(FT):
                    if not (is_int(b, 0) and f < 2):
                        pe.wait_ge(s["relu"], FT * b + (f - 1))
                    pe.matmul(Ub[:, f % 2, :], wfc[:, f * P:(f + 1) * P], hT[:], start=True, stop=True)\
                      .then_inc(s["up"], 1)
                    if f == FT - 1 and not is_int(b, last_b):
                        norm_T(b + 1)
                    if f >= 1:
                        down(b, f - 1)
                down(b, FT - 1)

            norm_T(0)
            pe.wait_ge(s["load"], 32)
            loop(pe, body)

        @block.scalar
        def _(a):
            def read_hT(bn):
                a.wait_ge(s["fill"], bn + 1)
                if not is_int(bn, 0):
                    a.wait_ge(s["up"], FT * bn)
                nc.scalar.activation(hT[:], Tb[:, 0, :], ACT.Identity, bias=mods[:, 1, 2, bass.ds(bn, 1)],
                                     scale=mods[:, 1, 3, bass.ds(bn, 1)]).then_inc(s["hT"], 1)

            def body(b):
                for f in range(FT):
                    a.wait_ge(s["up"], FT * b + (f + 1))
                    nc.scalar.activation(relu[:, f % 2, :], Ub[:, f % 2, :], ACT.Relu).then_inc(s["relu"], 1)
                    a.wait_ge(s["relu"], FT * b + (f + 1))
                    if not (is_int(b, 0) and f < 2):
                        a.wait_ge(s["down"], FT * b + (f - 1))
                    nc.scalar.activation(sq[:, f % 2, :], relu[:, f % 2, :], ACT.Square).then_inc(s["sq"], 1)
                if not is_int(b, last_b):
                    read_hT(b + 1)

            read_hT(0)
            loop(a, body)

        @block.vector
        def _(v):
            CH = 3 * (STEPS - 1) + 2

            def stats(bn):
                for t in range(TILES):
                    last = v.bn_stats(st[:, t, :], x[:, bass.ds(bn * SEQ + t * P, P)])
                last.then_inc(s["stats"], 1)
                wait_apart(s, v, s["stats"], bn + 1)
                for t in range(TILES):
                    last = v.bn_aggr(mv[:, t, :], st[:, t, :])
                last.then_inc(s["aggr"], 1)
                v.wait_ge(s["aggr"], bn + 1)
                v.tensor_scalar(ve[:], mv[:, :, 1], EPS, None, ALU.add).then_inc(s["veps"], 1)

            def normalise(bn):
                v.wait_ge(s["rstd"], bn + 1)
                if not is_int(bn, 0):
                    v.wait_ge(s["fill"], bn)
                for t in range(TILES):
                    last = v.tensor_scalar(xn[:, t, :], x[:, bass.ds(bn * SEQ + t * P, P)], mv[:, t, 0:1],
                                           rstd[:, t:t + 1], ALU.subtract, ALU.mult)
                last.then_inc(s["norm"], 1)

            def spikes(b):
                k = [0]

                def step(ins):
                    k[0] += 1
                    ins.then_inc(s["ch"], 1)
                    v.wait_ge(s["ch"], CH * b + k[0])

                v.wait_ge(s["down"], FT * b + FT)
                step(v.tensor_copy(y[:], Yb[:, 0, :]))
                v.sem_inc(s["yread"], 1)
                v.tensor_scalar(nmem[:, 0, :], y[:], -1.0, None, ALU.mult).then_inc(s["y"], 1)
                step(v.tensor_scalar(cnt[:, 0, :], y[:], 1.0, None, ALU.is_gt))
                v.wait_ge(s["y"], b + 1)
                for i in range(1, STEPS):
                    old, new = (i - 1) % 2, i % 2
                    step(v.scalar_tensor_tensor(drive[:], nmem[:, old, :], -BETA, y[:], ALU.mult, ALU.add))
                    step(v.scalar_tensor_tensor(nmem[:, new, :], nmem[:, old, :], -1.0, drive[:],
                                                ALU.is_lt, ALU.subtract))
                    step(v.scalar_tensor_tensor(cnt[:, new, :], nmem[:, new, :], -1.0, cnt[:, old, :],
                                                ALU.is_lt, ALU.add))
                if not is_int(b, 0):
                    v.wait_ge(s["xup"], b)
                v.scalar_tensor_tensor(t1[:].rearrange("p (t d) -> p t d", t=TILES),
                                       cnt[:, (STEPS - 1) % 2, :].rearrange("p (t d) -> p t d", t=TILES), 1.0 / STEPS,
                                       gate[:, bass.ds(b, 1), :].to_broadcast([P, TILES, P]),
                                       ALU.mult, ALU.mult).then_inc(s["t1"], 1)

            def body(b):
                if not is_int(b, last_b):
                    stats(b + 1)
                    normalise(b + 1)
                spikes(b)

            stats(0)
            normalise(0)
            loop(v, body)


def build(nc, dram, out, stop=4):
    with ExitStack() as ctx:
        sb = {}

        def tile(name, shape, dt=F32):
            sb[name] = ctx.enter_context(nc.sbuf_tensor(name, shape, dt))

        tile("x", [P, NBATCH * SEQ])
        tile("ident", [P, P])
        tile("mhalf", [P, TILES])
        tile("mods", [P, 2, 4, NBATCH])
        for layer in range(2):
            for n in (f"gateA{layer}", f"gateB{layer}"):
                tile(n, [P, NBATCH, P])
            tile(f"wqkv{layer}", [P, 3 * D])
            tile(f"bqk{layer}", [P, 2])
            tile(f"bv{layer}", [P, D])
            tile(f"bo{layer}", [P, D])
            tile(f"wo{layer}", [P, D])
        tile("gate_w", [P, EXPERTS])
        tile("gate_b", [P, EXPERTS])
        tile("iota8", [P, EXPERTS])
        tile("b1", [P, HTILES])
        tile("b3", [P, HTILES])
        tile("b2", [ALL_EXP, D])
        setup_phase(nc, dram, sb)
        if stop >= 1:
            attention_phase(nc, dram, sb, 0)
        if stop >= 2:
            expert_phase(nc, dram, sb)
        if stop >= 3:
            attention_phase(nc, dram, sb, 1)
        if stop >= 4:
            spike_phase(nc, dram, sb, out)
        else:
            with nc.semaphore("dbg") as q, nc.Block() as blk:
                @blk.sync
                def _(sp):
                    for b in range(NBATCH):
                        sp.dma_start(out[b].rearrange("(t p) d -> p t d", p=P),
                                     sb["x"][:, b * SEQ:(b + 1) * SEQ].rearrange("p (t d) -> p t d", t=TILES)).then_inc(q, 16)
                    sp.wait_ge(q, 16 * NBATCH)


def _bf16_parts(np, a, n):
    out, rest = [], a.astype(np.float64)
    for _ in range(n):
        part = rest.astype(np.float32).astype("bfloat16")
        out.append(part)
        rest = rest - part.astype(np.float64)
    return out


def constants(np):
    slopes = (2.0 ** -0.5) ** np.arange(1, HEADS + 1)
    slopes = slopes.astype(np.float32).astype(np.float64)
    pos = np.arange(SEQ)
    c = {}
    zero = np.zeros((N_ALIBI, HEADS, SEQ), "bfloat16")
    c["aliq0"], c["alik0"] = zero, zero
    sj = _bf16_parts(np, slopes[:, None] * pos[None], 3)
    si = _bf16_parts(np, -slopes[:, None] * pos[None], 3)
    q, k = zero.copy(), zero.copy()
    for kt in range(TILES - 1):
        after = (pos >= (kt + 1) * P)[None]
        inside = ((pos >= kt * P) & (pos < (kt + 1) * P))[None]
        for part in range(3):
            r = 6 * kt + part
            q[r] = after
            k[r] = sj[part] * inside
            q[r + 3] = si[part] * after
            k[r + 3] = np.broadcast_to(inside, k[r].shape)
    c["aliq1"], c["alik1"] = q, k
    c["shiftq0"] = np.zeros((1, HEADS, SEQ), "bfloat16")
    c["shiftq1"] = np.full((1, HEADS, SEQ), ALIBI_SHIFT, "bfloat16")
    c["ones3"] = np.ones((3, HEADS, SEQ), "bfloat16")
    p = np.arange(P)
    c["mask0"] = np.where(p[None] > p[:, None], -1e30, 0.0).astype("bfloat16")
    bias = slopes[None, :, None] * np.minimum(p[None, None] - p[:, None, None], 0)
    c["mask1"] = bias.astype(np.float32).astype("bfloat16")
    c["alibi"] = np.ascontiguousarray(bias.transpose(2, 1, 0)).astype(np.float32)
    sel = np.zeros((64 + ALL_EXP, HPAD), np.float32)
    unit = np.arange(ALL_EXP * HID)
    sel[unit // HID, unit] = 1.0
    sel[64 + unit // HID, unit] = 1.0
    c["sel"] = sel
    c["iota8"] = np.arange(EXPERTS, dtype=np.float32)[None]
    return c


def layout(np, i):
    def f(a):
        return np.ascontiguousarray(a)

    def heads(w):
        n = w.shape[0]
        return w.reshape(n, HEADS, DK).transpose(0, 2, 1).reshape(n, D)

    def by_strip(w):
        return w.reshape(GROUPS, GROUP, DK, D).transpose(1, 2, 0, 3).reshape(D, D)

    d = {"x": f(i["L0_attn_embeddings"])}
    wq, wk, wv = (np.asarray(i[f"L0_attn_W{n}"]).transpose(1, 0, 2).reshape(D, D) for n in "qkv")
    d["wqkv0"] = f(np.concatenate([heads(wq), heads(wk), wv], 1))
    bq, bk, bv = (np.asarray(i[f"L0_attn_b{n}"]).reshape(1, D) for n in "qkv")
    d["bqk0"] = f(np.concatenate([heads(bq), heads(bk)], 0).T)
    d["bv0"] = f(bv)
    w, b = np.asarray(i["L1_attn_W_qkv"]), np.asarray(i["L1_attn_b_qkv"]).reshape(1, 3 * D)
    d["wqkv1"] = f(np.concatenate([heads(w[:, 0:D]), heads(w[:, D:2 * D]), w[:, 2 * D:]], 1))
    d["bqk1"] = f(np.concatenate([heads(b[:, 0:D]), heads(b[:, D:2 * D])], 0).T)
    d["bv1"] = f(b[:, 2 * D:])
    d["wo0"], d["wo1"] = (f(by_strip(np.asarray(i[n]))) for n in ("L0_attn_Wo", "L1_attn_W_proj"))
    d["bo0"], d["bo1"] = f(np.asarray(i["L0_attn_bo"])[None]), f(np.asarray(i["L1_attn_b_proj"])[None])
    for layer in range(2):
        d[f"c{layer}"] = f(np.asarray(i[f"L{layer}_c"]).T)
        d[f"wmod{layer}"] = f(i[f"L{layer}_wmod"])
    d["gate_w"] = f(np.asarray(i["L0_ffn_gate_w"]).T)
    d["gate_b"] = f(np.asarray(i["L0_ffn_gate_b"])[None])
    pad = HPAD - ALL_EXP * HID
    for n in ("1", "3"):
        up = np.asarray(i[f"L0_ffn_w{n}"]).transpose(1, 0, 2).reshape(D, EXPERTS * HID)
        d[f"w{n}"] = f(np.pad(np.concatenate([up, np.asarray(i[f"L0_ffn_sw{n}"])], 1), ((0, 0), (0, pad))))
        bb = np.concatenate([np.asarray(i[f"L0_ffn_b{n}"]).reshape(-1), np.asarray(i[f"L0_ffn_sb{n}"])])
        d[f"b{n}"] = f(np.pad(bb, (0, pad)).reshape(HTILES, P).T)
    w2 = np.concatenate([np.asarray(i["L0_ffn_w2"]).reshape(-1, D), np.asarray(i["L0_ffn_sw2"])])
    d["w2"] = f(np.pad(w2, ((0, pad), (0, 0))).reshape(HTILES, P, D).transpose(1, 0, 2))
    d["b2"] = f(np.concatenate([np.asarray(i["L0_ffn_b2"]), np.asarray(i["L0_ffn_sb2"])[None]]))
    d["wfc"] = f(np.asarray(i["L1_ffn_W_fc"]).T)
    d["wproj"] = f(np.asarray(i["L1_ffn_W_proj"]).T.reshape(FFN // P, P, D).transpose(1, 0, 2))
    return d


def kernel(**inputs):
    import numpy as np
    import concourse.bacc as bacc
    from concourse.bass_utils import run_bass_kernel_spmd

    arrays = {**layout(np, {k: np.asarray(v) for k, v in inputs.items()}), **constants(np)}
    nc = bacc.Bacc("TRN2", target_bir_lowering=False, num_devices=1)
    dram = {n: nc.dram_tensor(f"in_{n}", a.shape, mybir.dt.from_np(a.dtype), kind="ExternalInput").ap()
            for n, a in arrays.items()}
    out = nc.dram_tensor("out", (NBATCH, SEQ, D), F32, kind="ExternalOutput").ap()
    build(nc, dram, out)
    r = run_bass_kernel_spmd(nc, [{f"in_{n}": a for n, a in arrays.items()}], core_ids=[0])
    return r.results[0]["out"]
```

```python
from contextlib import ExitStack

import concourse.bass as bass
from concourse import mybir

F32 = mybir.dt.float32
F32R = mybir.dt.float32r
BF16 = mybir.dt.bfloat16
U32 = mybir.dt.uint32
ALU = mybir.AluOpType
ACT = mybir.ActivationFunctionType
AX = mybir.AxisListType

P = 128
NBATCH, SEQ, D = 8, 512, 128
HEADS, DK = 16, 8
TILES = SEQ // P
GROUP = 4
GROUPS = HEADS // GROUP
EPS = 1e-5
EXPERTS, HID = 8, 176
ALL_EXP = EXPERTS + 1
HTILES = -(-ALL_EXP * HID // P)
HPAD = HTILES * P
FFN = 512
STEPS, BETA = 5, 0.9
GATE_MIN = 0.25
CH_SA, CH_CA, CH_GA, CH_SB, CH_CB, CH_GB = range(6)

Q_PARTS = (0, 0, 1, 1, 0, 2)
K_PARTS = (0, 1, 0, 1, 2, 0)
R_ALIBI = 8 * len(Q_PARTS)
N_ALIBI = 6 * (TILES - 1)
R_SHIFT = R_ALIBI + N_ALIBI
R_ALL = R_SHIFT + 3
ALIBI_SHIFT = -20.0
DENS = DK
VW = 32


def both(ap, n):
    return ap.unsqueeze(1).to_broadcast([ap.shape[0], n, ap.shape[1]])


def each(ap, n):
    return ap.unsqueeze(2).to_broadcast([ap.shape[0], ap.shape[1], n])


def semaphores(nc, ctx, phase, names):
    return {n: ctx.enter_context(nc.semaphore(f"{phase}_{n}")) for n in names.split()}


def wait_apart(s, eng, sem, value):
    eng.wait_ge(sem, value)
    if not isinstance(value, int):
        eng.sem_inc(s["apart"], 1)


def setup_phase(nc, dram, sb):
    x, ident = sb["x"], sb["ident"]
    with ExitStack() as ctx:
        def tile(name, shape, dt=F32):
            return ctx.enter_context(nc.sbuf_tensor(name, shape, dt))

        cT = tile("cT", [P, 2, NBATCH])
        half = tile("c_tanh", [P, 2, NBATCH])
        sil2 = tile("c_silu2", [P, 2, NBATCH])
        sil = tile("c_silu", [P, 2, NBATCH])
        silB = tile("c_siluB", [P, 2, NBATCH, P])
        wmod = tile("wmod", [P, 2, 6 * D])
        graw = tile("gate_sign", [P, 4, P])
        gabs = tile("gate_abs", [P, 4, P])
        gmax = tile("gate_max", [P, 4, P])
        ps = ctx.enter_context(nc.psum_tensor("setup_ps", [P, 8, 512], F32))
        s = semaphores(nc, ctx, "su", "load xload zero ident tanh sil2 sil silB mm gsign gabs gmax gate mods free bo")
        block = ctx.enter_context(nc.Block())

        small = ["wqkv0", "bqk0", "wo0", "wqkv1", "bqk1", "wo1", "bv0", "bv1", "bo0", "bo1",
                 "gate_w", "gate_b", "b1", "b3", "b2", "iota8"]

        @block.sync
        def _(sp):
            sp.dma_start(cT[:, 0, :], dram["c0"]).then_inc(s["load"], 16)
            sp.dma_start(cT[:, 1, :], dram["c1"]).then_inc(s["load"], 16)
            for layer in range(2):
                sp.dma_start(wmod[:, layer, :], dram[f"wmod{layer}"]).then_inc(s["load"], 16)
            for b in range(NBATCH):
                sp.dma_start(x[:, b * SEQ:(b + 1) * SEQ].rearrange("p (t d) -> p t d", t=TILES),
                             dram["x"][b].rearrange("(t p) d -> p t d", p=P)).then_inc(s["xload"], 16)
            n_other = 0
            for n in small:
                src = dram[n]
                if n in ("bv0", "bv1", "bo0", "bo1", "gate_b", "iota8"):
                    src = src.partition_broadcast(P)
                sp.dma_start(sb[n][:], src).then_inc(s["xload"], 16)
                n_other += 1
            sp.wait_ge(s["xload"], 16 * (NBATCH + n_other))

        @block.gpsimd
        def _(g):
            g.memset(ident[:], 0.0).then_inc(s["zero"], 1)
            g.memset(sb["mhalf"][:], -0.5)
            g.wait_ge(s["zero"], 1)
            g.affine_select(out=ident[:], in_=ident[:], compare_op=ALU.not_equal, fill=1.0, base=0,
                            pattern=[[-1, P]], channel_multiplier=1).then_inc(s["ident"], 1)

        @block.scalar
        def _(a):
            a.wait_ge(s["load"], 64)
            nc.scalar.activation(half[:], cT[:], ACT.Tanh, scale=0.5).then_inc(s["tanh"], 1)

        @block.tensor
        def _(t):
            t.wait_ge(s["sil"], 1)
            for layer in range(2):
                for i, ch in enumerate((CH_SA, CH_CA, CH_SB, CH_CB)):
                    last = t.matmul(ps[:, 0, (layer * 4 + i) * 8:(layer * 4 + i) * 8 + 8],
                                    wmod[:, layer, ch * D:(ch + 1) * D], sil[:, layer, :], start=True, stop=True)
            last.then_inc(s["mm"], 1)
            t.wait_ge(s["silB"], 1)
            n = 0
            for layer in range(2):
                for ch in (CH_GA, CH_GB):
                    for h in range(2):
                        if n >= 7:
                            t.wait_ge(s["gabs"], n - 6)
                        for b in range(4):
                            last = t.matmul(ps[:, 1 + n % 7, b * P:(b + 1) * P], silB[:, layer, 4 * h + b, :],
                                            wmod[:, layer, ch * D:(ch + 1) * D], start=True, stop=True)
                        last.then_inc(s["mm"], 1)
                        n += 1

        @block.vector
        def _(v):
            v.wait_ge(s["tanh"], 1)
            v.scalar_tensor_tensor(sil2[:], half[:], 1.0, cT[:], ALU.add, ALU.mult).then_inc(s["sil2"], 1)
            v.wait_ge(s["sil2"], 1)
            v.tensor_scalar(sil[:], sil2[:], 0.5, None, ALU.mult).then_inc(s["sil"], 1)
            v.wait_ge(s["sil"], 1)
            v.tensor_copy(silB[:], sil[:].unsqueeze(3).to_broadcast([P, 2, NBATCH, P])).then_inc(s["silB"], 1)
            v.wait_ge(s["mm"], 1)
            for layer in range(2):
                for i in range(4):
                    v.tensor_scalar(sb["mods"][:, layer, i, :], ps[:, 0, (layer * 4 + i) * 8:(layer * 4 + i) * 8 + 8],
                                    float(i % 2), None, ALU.add)
            n = 0
            for layer in range(2):
                for ch in ("A", "B"):
                    for h in range(2):
                        src = ps[:, 1 + n % 7, :].rearrange("p (b d) -> p b d", b=4)
                        v.wait_ge(s["mm"], n + 2)
                        if n:
                            v.wait_ge(s["gate"], n)
                        v.tensor_scalar(graw[:], src, 0.0, 2.0, ALU.is_ge, ALU.mult).then_inc(s["gsign"], 1)
                        v.wait_ge(s["gsign"], n + 1)
                        v.scalar_tensor_tensor(gabs[:], graw[:], -1.0, src, ALU.add, ALU.mult).then_inc(s["gabs"], 1)
                        v.wait_ge(s["gabs"], n + 1)
                        v.tensor_scalar(gmax[:], gabs[:], GATE_MIN, None, ALU.max).then_inc(s["gmax"], 1)
                        v.wait_ge(s["gmax"], n + 1)
                        v.scalar_tensor_tensor(sb[f"gate{ch}{layer}"][:, 4 * h:4 * h + 4, :], graw[:], -1.0, gmax[:],
                                               ALU.add, ALU.mult).then_inc(s["gate"], 1)
                        n += 1


def attention_phase(nc, dram, sb, layer):
    causal = layer == 0
    ph = f"at{layer}"
    x, ident, gate, mods = sb["x"], sb["ident"], sb[f"gateA{layer}"], sb["mods"]
    wqkv, bqk, wo, bv, bo_row = (sb[f"{n}{layer}"] for n in ("wqkv", "bqk", "wo", "bv", "bo"))
    with ExitStack() as ctx:
        def tile(name, shape, dt=F32):
            return ctx.enter_context(nc.sbuf_tensor(f"{ph}_{name}", shape, dt))

        QP = tile("QP", [R_ALL, 2, HEADS, SEQ], BF16)
        KP = tile("KP", [R_ALL, 2, HEADS, SEQ], BF16)
        E = tile("E", [P, TILES, GROUP, SEQ])
        VP = tile("VP", [P, 2, TILES, HEADS, VW])
        xn = tile("xn", [P, TILES, P])
        hT = tile("hT", [P, SEQ])
        parts = {n: tile(n, [P, SEQ], BF16) for n in ("q0", "q1", "q2", "k0", "k1", "k2")}
        rest = {n: tile(f"rest_{n}", [P, SEQ]) for n in "qk"}
        Oev = tile("Oev", [P, GROUPS, SEQ])
        ctxN = tile("ctxN", [P, SEQ])
        den = tile("den", [P, SEQ // 8])
        rden = tile("rden", [P, SEQ // 8])
        rden4 = tile("rden4", [GROUP, GROUPS * SEQ])
        denB = tile("denB", [P, SEQ])
        ctxT = tile("ctxT", [P, SEQ])
        gbo = tile("gbo", [P, P])
        t1 = tile("t1", [P, SEQ])
        st = tile("st", [P, TILES, 6])
        mv = tile("mv", [P, TILES, 2])
        ve = tile("ve", [P, TILES])
        rstd = tile("rstd", [P, TILES])
        mx = tile("mx", [P, 2, GROUP * TILES])
        nmx = tile("nmx", [P, 2, 2, GROUP * TILES], BF16)
        nrow = tile("nrow", [2 * GROUP * TILES, 2, P], BF16)
        idb = tile("idb", [P, P], BF16)
        wq_s = tile("wq_s", [P, D])
        bq_s = tile("bq_s", [P, 1])
        if causal:
            mask = tile("mask", [P, P], BF16)
        else:
            mask = tile("mask", [P, HEADS, P], BF16)
            factor = tile("factor", [P, HEADS, P])

        def bank(name, n=1):
            return ctx.enter_context(nc.psum_tensor(f"{ph}_{name}", [P, n, 512], F32))

        Mb, Sb, Ob, Tb = bank("Mb", 3), bank("Sb", 3), bank("Ob"), bank("Tb")

        s = semaphores(nc, ctx, ph, "const table zero ones wscale fac stats aggr veps rstd norm fill free hT p0 p1 p2 "
                 "rest maxs maxd nr0 nr1 nrow score exp diag vp pv oev gath compact rden rden4 dden ctx t1 gbo xup xbo apart")
        pk, = ([ctx.enter_context(nc.semaphore(f"{ph}_{n}{g}")) for g in range(2)] for n in ("stacked",))
        mrow = [ctx.enter_context(nc.semaphore(f"{ph}_shift_rows{g}")) for g in range(GROUPS)]
        block = ctx.enter_context(nc.Block())

        scale = float(DK) ** -0.5

        FILLS = {(0, 0): "ln", (0, 3): "m1", (1, 1): "q", (2, 1): "k", (3, 1): "v", (4, 3): "m2", (8, 3): "m3",
                 (11, 3): "ctx", (12, 3): "m0"}

        def fill(b, name):
            if isinstance(b, int) and b == -1:
                return ["ln", "q", "k", "v", "m0"].index(name)
            order = list(FILLS.values())
            if isinstance(b, int) and b == 0:
                order.remove("ctx")
                return 5 + order.index(name)
            if isinstance(b, int) and b == NBATCH - 1:
                order = ["m1", "m2", "m3", "ctx", "ctx_last"]
            return b * 9 + (4 + order.index(name))

        def filled(b, u, i, later=0):
            name = FILLS.get(divmod(u * GROUP + i - later, GROUP))
            if is_first(b) and name == "ctx" or is_last(b) and name in ("ln", "q", "k", "v", "m0"):
                return None
            return name

        def group_of(b, name):
            g = int(name[1])
            return (b + 1, 0) if g == 0 else (b, g)

        PER_M = GROUPS * GROUP * TILES
        UNITS = GROUPS * TILES
        KEY_TILES = (0, 3, 1, 2) if causal else (0, 1, 2, 3)
        VLAG = 2

        def before(n):
            return n - 3 if n >= 3 else (-1, -3, -2)[n]

        def groups_of(b, g):
            return (b, g + 2) if g < 2 else (b + 1, g - 2)

        last_b = NBATCH - 1

        def pairs(eng, steps):
            steps(0, 0)
            steps(1, 1)
            with eng.Fori(1, NBATCH // 2 - 1) as pair:
                steps(pair * 2, 0)
                steps(pair * 2 + 1, 1)
            steps(last_b - 1, 0)
            steps(last_b, 1)

        def is_last(b):
            return isinstance(b, int) and b == last_b

        def is_first(b):
            return isinstance(b, int) and b == 0

        @block.tensor
        def _(pe):
            def fill_wait(k):
                if not (isinstance(k, int) and k == 0):
                    pe.wait_ge(s["free"], k)

            def norm_T(bn, k):
                fill_wait(k)
                pe.wait_ge(s["norm"], bn + 1)
                for t in range(TILES):
                    last = pe.transpose(Tb[:, 0, t * P:(t + 1) * P], xn[:, t, :], ident[:])
                last.then_inc(s["fill"], 1)

            def project(which, bn, k):
                fill_wait(k)
                pe.wait_ge(s["hT"], bn + 1)
                if which == "v":
                    for t in range(TILES):
                        last = pe.matmul(Tb[:, 0, t * P:(t + 1) * P], hT[:, t * P:(t + 1) * P],
                                         wqkv[:, 2 * D:3 * D], start=True, stop=True)
                else:
                    w = wq_s[:] if which == "q" else wqkv[:, D:2 * D]
                    last = pe.matmul(Tb[:, 0, :], w, hT[:], start=True, stop=True)
                last.then_inc(s["fill"], 1)

            def max_score(bm, gm, i, qt, half):
                h = GROUP * gm + i
                n = h * TILES + qt
                if n == 0:
                    for which in range(2):
                        pe.wait_ge(pk[which], 96 * (bm + 1))
                if not (is_first(bm) and n < 3):
                    pe.wait_ge(s["maxd"], bm * PER_M + (before(n) + 1))
                width = (qt + 1) * P if causal else SEQ
                out = Mb[:, n % 3, :]
                pe.matmul(out[:, 0:width], QP[0:R_SHIFT, half, h, qt * P:(qt + 1) * P],
                          KP[0:R_SHIFT, half, h, 0:width],
                          start=True, stop=True)
                pe.matmul(out[:, qt * P:(qt + 1) * P], idb[:], mask[:] if causal else mask[:, h, :],
                          start=False, stop=True, skip_group_check=True).then_inc(s["maxs"], 1)

            def max_T(bm, gm, k):
                fill_wait(k)
                pe.wait_ge(s["nr1"], GROUPS * bm + (gm + 1))
                pe.transpose(Tb[0:32, 0, 0:P // 2].bitcast(BF16), nmx[:, gm % 2].rearrange("p a c -> p (a c)"),
                             idb[:]).then_inc(s["fill"], 1)

            def key_score(b, g, kt, i, half):
                if kt == 0 and i == 0:
                    pe.wait_ge(mrow[g], 16 * (b + 1))
                h = GROUP * g + i
                n = (GROUP * g + kt) * GROUP + i
                if not (is_first(b) and n < 3):
                    pe.wait_ge(s["exp"], b * PER_M + (before(n) + 1))
                kt = KEY_TILES[kt]
                q0 = kt * P if causal else 0
                pe.matmul(Sb[:, n % 3, q0:SEQ], KP[:, half, h, kt * P:(kt + 1) * P], QP[:, half, h, q0:SEQ],
                          start=True, stop=True).then_inc(s["score"], 1)

            def values(bp, gp, kt, half):
                pe.wait_ge(s["diag"], UNITS * bp + (TILES * gp + kt + 1))
                if kt == 0:
                    if gp == 0:
                        pe.wait_ge(s["vp"], bp + 1)
                    if not (is_first(bp) and gp == 0):
                        pe.wait_ge(s["oev"], GROUPS * bp + gp)
                opens, closes = kt == 0, kt == TILES - 1
                kt = KEY_TILES[kt]
                q0 = kt * P if causal else 0
                for i in range(GROUP):
                    last = pe.matmul(Ob[VW * i:VW * (i + 1), 0, q0:SEQ], VP[:, half, kt, GROUP * gp + i, :],
                                     E[:, kt, i, q0:SEQ], start=opens, stop=closes)
                last.then_inc(s["pv"], 1)

            def out_proj(bo, k):
                fill_wait(k)
                pe.wait_ge(s["ctx"], bo + 1)
                for t in range(TILES):
                    last = pe.matmul(Tb[:, 0, t * P:(t + 1) * P], ctxT[:, t * P:(t + 1) * P], wo[:],
                                     start=True, stop=True)
                last.then_inc(s["fill"], 1)

            def steps(b, half):
                for u in range(UNITS):
                    g, kt = divmod(u, TILES)
                    bm, gm = groups_of(b, g)
                    gp, ktp = divmod((u - VLAG) % UNITS, TILES)
                    bp, halfp = (b, half) if u >= VLAG else (b - 1, 1 - half)
                    for i in range(GROUP):
                        if not (is_last(b) and g >= 2):
                            max_score(bm, gm, kt, i, half if g < 2 else 1 - half)
                        key_score(b, g, kt, i, half)
                        if i == GROUP - 1 and not (is_first(b) and u < VLAG):
                            values(bp, gp, ktp, halfp)
                        name = filled(b, u, i)
                        if name == "ln":
                            norm_T(b + 1, fill(b, name))
                        elif name in ("q", "k", "v"):
                            project(name, b + 1, fill(b, name))
                        elif name == "ctx":
                            out_proj(b - 1, fill(b, name))
                        elif name:
                            max_T(*group_of(b, name), fill(b, name))

            pe.wait_ge(s["wscale"], 1)
            pe.wait_ge(s["const"], 144)
            norm_T(0, 0)
            for k, which in enumerate("qkv"):
                project(which, 0, k + 1)
            for gm in range(2):
                for i in range(GROUP):
                    for qt in range(TILES):
                        max_score(0, gm, i, qt, 0)
                if gm == 0:
                    max_T(0, 0, fill(-1, "m0"))
            pairs(pe, steps)
            for u in range(UNITS - VLAG, UNITS):
                values(last_b, u // TILES, u % TILES, 1)
            out_proj(last_b, fill(last_b, "ctx_last"))

        @block.scalar
        def _(a):
            def read_hT(bn, k):
                a.wait_ge(s["fill"], k + 1)
                nc.scalar.activation(hT[:], Tb[:, 0, :], ACT.Identity, bias=mods[:, layer, 0, bass.ds(bn, 1)],
                                     scale=mods[:, layer, 1, bass.ds(bn, 1)]).then_inc(s["hT"], 1)
                a.wait_ge(s["hT"], bn + 1)
                a.sem_inc(s["free"], 1)

            def part0(which, bn, k):
                a.wait_ge(s["fill"], k + 1)
                if not (isinstance(bn, int) and bn == 0):
                    a.wait_ge(pk[0 if which == "q" else 1], 96 * bn)
                    a.wait_ge(s["p2"], 2 * bn)
                bias = bq_s[:] if which == "q" else bqk[:, 1:2]
                nc.scalar.activation(parts[f"{which}0"][:], Tb[:, 0, :], ACT.Identity, bias=bias)
                nc.scalar.activation(rest[which][:], Tb[:, 0, :], ACT.Identity, bias=bias).then_inc(s["p0"], 1)
                a.wait_ge(s["p0"], 2 * bn + (1 if which == "q" else 2))
                a.sem_inc(s["free"], 1)

            def shift_rows(bm, gm, k):
                a.wait_ge(s["fill"], k + 1)
                if not (isinstance(bm, int) and bm == 0 and gm < 2):
                    a.wait_ge(mrow[(gm - 2) % GROUPS], 16 * (bm + (1 if gm >= 2 else 0)))
                nc.scalar.activation(nrow[:, gm % 2, :], Tb[0:32, 0, 0:P // 2].bitcast(BF16), ACT.Copy)\
                  .then_inc(s["nrow"], 1)
                a.wait_ge(s["nrow"], GROUPS * bm + (gm + 1))
                a.sem_inc(s["free"], 1)

            def exp(b, g, kt, i):
                n = (GROUP * g + kt) * GROUP + i
                a.wait_ge(s["score"], b * PER_M + (n + 1))
                if i == 0 and not (is_first(b) and g == 0):
                    a.wait_ge(s["pv"], UNITS * b + (TILES * (g - 1) + kt + 1))
                kt = KEY_TILES[kt]
                q0 = kt * P if causal else 0
                nc.scalar.activation(E[:, kt, i, q0:SEQ], Sb[:, n % 3, q0:SEQ], ACT.Exp).then_inc(s["exp"], 1)

            def read_O(bp, gp):
                a.wait_ge(s["pv"], UNITS * bp + TILES * (gp + 1))
                if gp == 0 and not (isinstance(bp, int) and bp == 0):
                    a.wait_ge(s["gath"], 64 * bp)
                    a.wait_ge(s["compact"], 16 * bp)
                nc.scalar.activation(Oev[:, gp, :], Ob[:, 0, :], ACT.Copy).then_inc(s["oev"], 1)

            def steps(b, half):
                for u in range(UNITS):
                    g, kt = divmod(u, TILES)
                    for i in range(GROUP):
                        exp(b, g, kt, i)
                        if kt == VLAG and i == 0 and not (is_first(b) and g == 0):
                            read_O(*((b, g - 1) if g else (b - 1, GROUPS - 1)))
                        name = filled(b, u, i, 1)
                        if name == "ln":
                            read_hT(b + 1, fill(b, name))
                        elif name in ("q", "k"):
                            part0(name, b + 1, fill(b, name))
                        elif name and name[0] == "m":
                            shift_rows(*group_of(b, name), fill(b, name))

            if not causal:
                a.wait_ge(s["table"], 16)
                nc.scalar.activation(factor[:], factor[:], ACT.Exp).then_inc(s["fac"], 1)
            a.wait_ge(s["wscale"], 1)
            read_hT(0, 0)
            part0("q", 0, 1)
            part0("k", 0, 2)
            shift_rows(0, 0, 4)
            pairs(a, steps)
            read_O(last_b, GROUPS - 1)

        @block.vector
        def _(v):
            def stats(bn, t):
                last = v.bn_stats(st[:, t, :], x[:, bass.ds(bn * SEQ + t * P, P)])
                if t == TILES - 1:
                    last.then_inc(s["stats"], 1)

            def aggregate(bn):
                wait_apart(s, v, s["stats"], bn + 1)
                for t in range(TILES):
                    last = v.bn_aggr(mv[:, t, :], st[:, t, :])
                last.then_inc(s["aggr"], 1)
                v.wait_ge(s["aggr"], bn + 1)
                v.tensor_scalar(ve[:], mv[:, :, 1], EPS, None, ALU.add).then_inc(s["veps"], 1)

            def normalise(bn, t):
                if t == 0:
                    v.wait_ge(s["rstd"], bn + 1)
                    if not is_first(bn):
                        v.wait_ge(s["hT"], bn)
                last = v.tensor_scalar(xn[:, t, :], x[:, bass.ds(bn * SEQ + t * P, P)], mv[:, t, 0:1],
                                       rstd[:, t:t + 1], ALU.subtract, ALU.mult)
                if t == TILES - 1:
                    last.then_inc(s["norm"], 1)

            def remainder(which, bn):
                wait_apart(s, v, s["p0"], 2 * bn + (1 if which == "q" else 2))
                v.tensor_tensor(rest[which][:], rest[which][:], parts[f"{which}0"][:], ALU.subtract)\
                 .then_inc(s["rest"], 1)

            def read_V(bn, half, k):
                v.wait_ge(s["fill"], k + 1)
                if not (isinstance(bn, int) and bn < 2):
                    v.wait_ge(s["pv"], UNITS * bn - UNITS)
                v.tensor_tensor(VP[:, half, :, :, 0:DK], Tb[:, 0, :].rearrange("p (t h d) -> p t h d", t=TILES, h=HEADS),
                                both(bv[:], TILES).rearrange("p t (h d) -> p t h d", h=HEADS), ALU.add).then_inc(s["vp"], 1)
                v.wait_ge(s["vp"], bn + 1)
                v.sem_inc(s["free"], 1)

            def reduce_max(bm, gm, i, qt):
                n = (GROUP * gm + i) * TILES + qt
                v.wait_ge(s["maxs"], bm * PER_M + (n + 1))
                if i == 0 and qt == 0 and not (is_first(bm) and gm < 2):
                    v.wait_ge(s["nrow"], GROUPS * bm + (gm - 1))
                width = (qt + 1) * P if causal else SEQ
                v.tensor_reduce(mx[:, gm % 2, i * TILES + qt:i * TILES + qt + 1], Mb[:, n % 3, 0:width],
                                AX.X, ALU.max).then_inc(s["maxd"], 1)

            def negate(bm, gm):
                v.wait_ge(s["maxd"], bm * PER_M + 16 * (gm + 1))
                v.tensor_scalar(nmx[:, gm % 2, 0, :], mx[:, gm % 2, :], -1.0, None, ALU.mult).then_inc(s["nr0"], 1)
                v.wait_ge(s["nr0"], GROUPS * bm + (gm + 1))
                v.scalar_tensor_tensor(nmx[:, gm % 2, 1, :], mx[:, gm % 2, :], -1.0, nmx[:, gm % 2, 0, :],
                                       ALU.mult, ALU.subtract).then_inc(s["nr1"], 1)

            def recip(bo):
                v.wait_ge(s["compact"], 16 * (bo + 1))
                if not (isinstance(bo, int) and bo == 0):
                    v.wait_ge(s["rden4"], 16 * bo)
                v.reciprocal(rden[:], den[:]).then_inc(s["rden"], 1)

            def context(bo):
                v.wait_ge(s["gath"], 64 * (bo + 1))
                v.wait_ge(s["dden"], 64 * (bo + 1))
                if not (isinstance(bo, int) and bo == 0):
                    v.wait_ge(s["t1"], bo)
                v.tensor_tensor(ctxT[:], ctxN[:], denB[:], ALU.mult).then_inc(s["ctx"], 1)

            def gated(bo, k):
                v.wait_ge(s["fill"], k + 1)
                if not (isinstance(bo, int) and bo == 0):
                    v.wait_ge(s["xup"], bo)
                v.tensor_tensor(t1[:].rearrange("p (t d) -> p t d", t=TILES),
                                Tb[:, 0, :].rearrange("p (t d) -> p t d", t=TILES),
                                gate[:, bass.ds(bo, 1), :].to_broadcast([P, TILES, P]), ALU.mult).then_inc(s["t1"], 1)
                v.wait_ge(s["t1"], bo + 1)
                v.sem_inc(s["free"], 1)

            def steps(b, half):
                for u in range(UNITS):
                    g, kt = divmod(u, TILES)
                    bm, gm = groups_of(b, g)
                    maxima = not (is_last(b) and g >= 2)
                    for i in range(GROUP):
                        if maxima:
                            reduce_max(bm, gm, kt, i)
                        name = filled(b, u, i, 2)
                        if name in ("q", "k"):
                            remainder(name, b + 1)
                        elif name == "v":
                            read_V(b + 1, 1 - half, fill(b, name))
                        elif name == "ctx":
                            gated(b - 1, fill(b, name))
                        if u == 6 and i == 1 and not is_first(b):
                            recip(b - 1)
                        if u == 11 and i == 0 and not is_first(b):
                            context(b - 1)
                        if not (isinstance(b, int) and b >= last_b - 1):
                            if u == 11:
                                stats(b + 2, i)
                            if u == 12 and i == 0:
                                aggregate(b + 2)
                            if u == 14:
                                normalise(b + 2, i)
                    if maxima and kt == TILES - 1:
                        negate(bm, gm)

            for t in range(TILES):
                stats(0, t)
            aggregate(0)
            v.tensor_scalar(wq_s[:], wqkv[:, 0:D], scale, None, ALU.mult)
            v.tensor_copy(idb[:], ident[:])
            v.tensor_scalar(bq_s[:], bqk[:, 0:1], scale, None, ALU.mult).then_inc(s["wscale"], 1)
            v.wait_ge(s["wscale"], 1)
            for t in range(TILES):
                normalise(0, t)
            remainder("q", 0)
            remainder("k", 0)
            v.wait_ge(s["zero"], 2)
            read_V(0, 0, 3)
            for t in range(TILES):
                stats(1, t)
            aggregate(1)
            for t in range(TILES):
                normalise(1, t)
            for gm in range(2):
                for i in range(GROUP):
                    for qt in range(TILES):
                        reduce_max(0, gm, i, qt)
                negate(0, gm)
            pairs(v, steps)
            recip(last_b)
            context(last_b)
            gated(last_b, fill(last_b, "ctx_last"))

        @block.gpsimd
        def _(p):
            def powers(bn):
                p.wait_ge(s["veps"], bn + 1)
                p.tensor_tensor(rstd[:], ve[:], sb["mhalf"][:], ALU.pow).then_inc(s["rstd"], 1)

            def split(which, bn):
                k = 2 * bn + (1 if which == "q" else 2)
                if not (isinstance(bn, int) and bn == 0):
                    p.wait_ge(pk[0 if which == "q" else 1], 96 * bn)
                wait_apart(s, p, s["rest"], k)
                p.tensor_scalar(parts[f"{which}1"][:], rest[which][:], 1.0, None, ALU.mult).then_inc(s["p1"], 1)
                wait_apart(s, p, s["p1"], k)
                p.tensor_tensor(parts[f"{which}2"][:], rest[which][:], parts[f"{which}1"][:],
                                ALU.subtract).then_inc(s["p2"], 1)

            def diagonal(b, g, kt):
                wait_apart(s, p, s["exp"], b * PER_M + (GROUP * g + kt + 1) * GROUP)
                kt = KEY_TILES[kt]
                blocks = E[:, kt, :, kt * P:(kt + 1) * P]
                if causal:
                    p.affine_select(out=blocks, in_=blocks, compare_op=ALU.is_ge, fill=0.0, base=0,
                                    pattern=[[0, GROUP], [1, P]], channel_multiplier=-1).then_inc(s["diag"], 1)
                else:
                    p.tensor_tensor(blocks, blocks, factor[:, GROUP * g:GROUP * (g + 1), :],
                                    ALU.mult).then_inc(s["diag"], 1)

            def update_x(bo):
                xb = x[:, bass.ds(bo * SEQ, SEQ)]
                if not is_first(bo):
                    wait_apart(s, p, s["xbo"], bo)
                p.tensor_tensor(gbo[:].unsqueeze(1), gate[:, bass.ds(bo, 1), :], bo_row[:].unsqueeze(1),
                                ALU.mult).then_inc(s["gbo"], 1)
                wait_apart(s, p, s["t1"], bo + 1)
                p.tensor_tensor(xb, xb, t1[:], ALU.add).then_inc(s["xup"], 1)
                p.wait_ge(s["xup"], bo + 1)
                wait_apart(s, p, s["gbo"], bo + 1)
                xv = xb.rearrange("p (t d) -> p t d", t=TILES)
                p.tensor_tensor(xv, xv, both(gbo[:], TILES), ALU.add).then_inc(s["xbo"], 1)

            def steps(b, half):
                for u in range(UNITS):
                    diagonal(b, *divmod(u, TILES))
                    if u in (1, 2) and not is_last(b):
                        split("qk"[u - 1], b + 1)
                    if u == 13 and not is_first(b):
                        update_x(b - 1)
                    if u == 12 and not (isinstance(b, int) and b >= last_b - 1):
                        powers(b + 2)

            p.memset(VP[:], 0.0).then_inc(s["zero"], 1)
            p.wait_ge(s["zero"], 1)
            p.memset(VP[:, :, :, :, DENS:DENS + 1], 1.0).then_inc(s["zero"], 1)
            if not causal:
                p.wait_ge(s["fac"], 1)
            powers(0)
            split("q", 0)
            split("k", 0)
            powers(1)
            pairs(p, steps)
            update_x(last_b)

        @block.sync
        def _(sp):
            def stack(bn, half, which):
                if not (isinstance(bn, int) and bn < 2):
                    wait_apart(s, sp, s["score"], PER_M * bn - PER_M)
                k = 2 * bn + (1 + which)
                sp.wait_ge(s["p2"], k)
                sp.wait_ge(s["p0"], k)
                for r in range(6):
                    dst = (QP, KP)[which]
                    part = parts["qk"[which] + str((Q_PARTS, K_PARTS)[which][r])]
                    sp.dma_start(dst[8 * r:8 * r + 8, half, :, :], part[:]).then_inc(pk[which], 16)

            def send_rows(bm, gm, half):
                sp.wait_ge(s["nrow"], GROUPS * bm + (gm + 1))
                sp.dma_start(QP[R_SHIFT + 1:R_ALL, half, GROUP * gm:GROUP * (gm + 1), :],
                             nrow[:, gm % 2, :]).then_inc(mrow[gm], 16)

            def gather(bo):
                wait_apart(s, sp, s["oev"], GROUPS * (bo + 1))
                if not (isinstance(bo, int) and bo == 0):
                    sp.wait_ge(s["ctx"], bo)
                sp.dma_start(den[:], Oev[DENS::VW, :, :]).then_inc(s["compact"], 16)
                for i in range(GROUP):
                    sp.dma_start(ctxN[32 * i:32 * i + 32, :], Oev[VW * i:VW * i + DK, :, :]).then_inc(s["gath"], 16)

            def spread(bo):
                sp.wait_ge(s["rden"], bo + 1)
                sp.dma_start(rden4[:], rden[:]).then_inc(s["rden4"], 16)
                sp.wait_ge(s["rden4"], 16 * (bo + 1))
                for g in range(GROUPS):
                    sp.dma_start(denB[g::GROUPS, :],
                                 rden4[:, g * SEQ:(g + 1) * SEQ].unsqueeze(1).to_broadcast([GROUP, DK, SEQ]))\
                      .then_inc(s["dden"], 16)

            def steps(b, half):
                for g in range(GROUPS):
                    if g < 3:
                        send_rows(b, g + 1, half)
                    elif not is_last(b):
                        send_rows(b + 1, 0, 1 - half)
                    if g < 2 and not is_last(b):
                        stack(b + 1, 1 - half, g)
                    if g == 0 and not is_first(b):
                        gather(b - 1)
                    if g == 1 and not is_first(b):
                        spread(b - 1)

            for half in range(2):
                sp.dma_start(QP[R_ALIBI:R_SHIFT, half], dram[f"aliq{layer}"]).then_inc(s["const"], 16)
                sp.dma_start(KP[R_ALIBI:R_SHIFT, half], dram[f"alik{layer}"]).then_inc(s["const"], 16)
                sp.dma_start(QP[R_SHIFT:R_SHIFT + 1, half], dram[f"shiftq{layer}"]).then_inc(s["const"], 16)
                sp.dma_start(KP[R_SHIFT:R_ALL, half], dram["ones3"]).then_inc(s["const"], 16)
            sp.dma_start(mask[:], dram[f"mask{layer}"]).then_inc(s["const"], 16)
            if not causal:
                sp.dma_start(factor[:], dram["alibi"]).then_inc(s["table"], 16)
            stack(0, 0, 0)
            stack(0, 0, 1)
            send_rows(0, 0, 0)
            pairs(sp, steps)
            gather(last_b)
            spread(last_b)


def expert_phase(nc, dram, sb):
    x, ident, gate, mods = sb["x"], sb["ident"], sb["gateB0"], sb["mods"]
    gate_w, gate_b, iota8, b1, b3 = (sb[n] for n in ("gate_w", "gate_b", "iota8", "b1", "b3"))
    R_LOW = 64
    R_ROWS = R_LOW + ALL_EXP
    with ExitStack() as ctx:
        def tile(name, shape, dt=F32):
            return ctx.enter_context(nc.sbuf_tensor(f"ex_{name}", shape, dt))

        raw = {n: tile(n, [P, HPAD]) for n in ("w1", "w3")}
        hi = {n: tile(f"{n}_hi", [P, HPAD], F32R) for n in ("w1", "w3")}
        lo = {n: tile(f"{n}_lo", [P, HPAD], F32R) for n in ("w1", "w3")}
        sel = tile("sel", [R_ROWS, HPAD])
        selr = tile("selr", [R_ROWS, HPAD], F32R)
        w2 = tile("w2", [P, HTILES, D])
        st = tile("st", [P, TILES, 6])
        mv = tile("mv", [P, TILES, 2])
        ve = tile("ve", [P, TILES])
        rstd = tile("rstd", [P, TILES])
        xn = tile("xn", [P, TILES, P])
        hT = tile("hT", [P, SEQ])
        h_hi = tile("h_hi", [P, 2, SEQ], F32R)
        h_lo = tile("h_lo", [P, 2, SEQ], F32R)
        top = tile("top", [P, TILES])
        lg = tile("lg", [P, TILES, EXPERTS])
        ex = tile("ex", [P, TILES, EXPERTS])
        sm = tile("sm", [P, TILES])
        rs = tile("rs", [P, TILES])
        sc = tile("sc", [P, TILES, EXPERTS])
        bi = tile("bi", [P, TILES, EXPERTS])
        m8 = tile("m8", [P, TILES, 8])
        i8 = tile("i8", [P, TILES, 8], U32)
        i8f = tile("i8f", [P, TILES, 8])
        k1 = tile("k1", [P, TILES, EXPERTS])
        k2 = tile("k2", [P, TILES, EXPERTS])
        k12 = tile("k12", [P, TILES, EXPERTS])
        rw = tile("rw", [P, TILES, ALL_EXP])
        rwT = tile("rwT", [ALL_EXP, 2, SEQ])
        rwr = tile("rwr", [P, 2, SEQ], F32R)
        up3 = tile("up3", [P, 2, SEQ])
        z = tile("z", [P, 2, SEQ])
        th = tile("th", [P, 2, SEQ])
        hh = tile("hh", [P, 2, SEQ])
        t1 = tile("t1", [P, SEQ])

        def bank(name, n=1):
            return ctx.enter_context(nc.psum_tensor(f"ex_{name}", [P, n, 512], F32))

        Ab, Bb, Rb, Yb, Tb = bank("Ab", 2), bank("Bb", 2), bank("Rb", 2), bank("Yb"), bank("Tb")
        s = semaphores(nc, ctx, "ex", "load load2 zero hi1 lo1 hi3 lo3 selr stats aggr veps rstd norm fill free hT hhi hlo "
                 "ch exp rwT rhi rlo up u3 z th hh down y t1 xup apart")
        block = ctx.enter_context(nc.Block())
        N = HTILES
        last_b = NBATCH - 1

        def is_int(b, k):
            return isinstance(b, int) and b == k

        CH_PER = 14

        LN, LOGITS, RW = range(3)

        def pairs(eng, body):
            body(0, 0)
            body(1, 1)
            with eng.Fori(1, NBATCH // 2 - 1) as pair:
                body(pair * 2, 0)
                body(pair * 2 + 1, 1)
            body(last_b - 1, 0)
            body(last_b, 1)

        @block.sync
        def _(sp):
            sp.dma_start(raw["w1"][:], dram["w1"]).then_inc(s["load"], 16)
            sp.dma_start(raw["w3"][:], dram["w3"]).then_inc(s["load"], 16)
            sp.dma_start(sel[:], dram["sel"]).then_inc(s["load"], 16)
            sp.dma_start(w2[:], dram["w2"]).then_inc(s["load2"], 16)

        @block.gpsimd
        def _(p):
            def powers(bn):
                p.wait_ge(s["veps"], bn + 1)
                p.tensor_tensor(rstd[:], ve[:], sb["mhalf"][:], ALU.pow).then_inc(s["rstd"], 1)

            def split(bn, half):
                if not (isinstance(bn, int) and bn < 2):
                    p.wait_ge(s["up"], N * bn - N)
                wait_apart(s, p, s["hT"], bn + 1)
                p.tensor_scalar(h_hi[:, half, :], hT[:], 1.0, None, ALU.mult).then_inc(s["hhi"], 1)
                p.wait_ge(s["hhi"], bn + 1)
                p.tensor_tensor(h_lo[:, half, :], hT[:], h_hi[:, half, :].bitcast(F32), ALU.subtract)\
                 .then_inc(s["hlo"], 1)

            def update_x(b):
                xb = x[:, bass.ds(b * SEQ, SEQ)]
                wait_apart(s, p, s["t1"], b + 1)
                p.tensor_tensor(xb, xb, t1[:], ALU.add).then_inc(s["xup"], 1)

            def body(b, half):
                if not is_int(b, last_b):
                    powers(b + 1)
                    split(b + 1, 1 - half)
                if not is_int(b, 0):
                    update_x(b - 1)

            p.memset(rwr[:].bitcast(F32), 0.0).then_inc(s["zero"], 1)
            powers(0)
            split(0, 0)
            p.wait_ge(s["load"], 48)
            p.wait_ge(s["hi3"], 1)
            p.tensor_tensor(lo["w3"][:], raw["w3"][:], hi["w3"][:].bitcast(F32), ALU.subtract).then_inc(s["lo3"], 1)
            pairs(p, body)
            update_x(last_b)

        @block.scalar
        def _(a):
            def read_hT(bn):
                a.wait_ge(s["fill"], 3 * bn + (LN + 1))
                if not is_int(bn, 0):
                    a.wait_ge(s["hlo"], bn)
                nc.scalar.activation(hT[:], Tb[:, 0, :], ACT.Identity, bias=mods[:, 0, 2, bass.ds(bn, 1)],
                                     scale=mods[:, 0, 3, bass.ds(bn, 1)]).then_inc(s["hT"], 1)
                a.wait_ge(s["hT"], bn + 1)
                a.sem_inc(s["free"], 1)

            def route_exp(bn):
                a.wait_ge(s["ch"], CH_PER * bn + 2)
                nc.scalar.activation(ex[:], lg[:], ACT.Exp).then_inc(s["exp"], 1)

            def read_rw(bn, half):
                a.wait_ge(s["fill"], 3 * bn + (RW + 1))
                if not (isinstance(bn, int) and bn < 2):
                    a.wait_ge(s["y"], bn - 1)
                nc.scalar.activation(rwT[:, half, :], Tb[0:ALL_EXP, 0, :], ACT.Copy).then_inc(s["rwT"], 1)

            def up_bias(b, j, n):
                q = (13 * (n % 2) + j) % 2
                a.wait_ge(s["up"], N * b + (j + 1))
                if not (is_int(b, 0) and j < 2):
                    a.wait_ge(s["z"], N * b + (j - 1))
                nc.scalar.activation(up3[:, q, :], Bb[:, q, :], ACT.Identity, bias=b3[:, j:j + 1]).then_inc(s["u3"], 1)

            def silu(b, j, n):
                q = (13 * (n % 2) + j) % 2
                a.wait_ge(s["z"], N * b + (j + 1))
                if not (is_int(b, 0) and j < 2):
                    a.wait_ge(s["hh"], N * b + (j - 1))
                nc.scalar.activation(th[:, q, :], z[:, q, :], ACT.Silu).then_inc(s["th"], 1)

            def body(b, half):
                for j in range(N):
                    up_bias(b, j, half)
                    if j > 0:
                        silu(b, j - 1, half)
                    elif not is_int(b, 0):
                        silu(b - 1, N - 1, 1 - half)
                    if not is_int(b, last_b):
                        if j == 3:
                            read_hT(b + 1)
                        if j == 6:
                            route_exp(b + 1)
                        if j == 11:
                            read_rw(b + 1, 1 - half)

            a.wait_ge(s["load"], 48)
            nc.scalar.activation(hi["w3"][:], raw["w3"][:], ACT.Copy).then_inc(s["hi3"], 1)
            read_hT(0)
            nc.scalar.activation(selr[:], sel[:], ACT.Copy).then_inc(s["selr"], 1)
            route_exp(0)
            read_rw(0, 0)
            pairs(a, body)
            silu(last_b, N - 1, 1)

        @block.vector
        def _(v):
            def stats(bn):
                for t in range(TILES):
                    last = v.bn_stats(st[:, t, :], x[:, bass.ds(bn * SEQ + t * P, P)])
                last.then_inc(s["stats"], 1)
                wait_apart(s, v, s["stats"], bn + 1)
                for t in range(TILES):
                    last = v.bn_aggr(mv[:, t, :], st[:, t, :])
                last.then_inc(s["aggr"], 1)
                v.wait_ge(s["aggr"], bn + 1)
                v.tensor_scalar(ve[:], mv[:, :, 1], EPS, None, ALU.add).then_inc(s["veps"], 1)

            def normalise(bn):
                v.wait_ge(s["rstd"], bn + 1)
                if not is_int(bn, 0):
                    v.wait_ge(s["hT"], bn)
                for t in range(TILES):
                    last = v.tensor_scalar(xn[:, t, :], x[:, bass.ds(bn * SEQ + t * P, P)], mv[:, t, 0:1],
                                           rstd[:, t:t + 1], ALU.subtract, ALU.mult)
                last.then_inc(s["norm"], 1)

            def route_step(bn, k, ins):
                ins.then_inc(s["ch"], 1)
                if k in (6, 7):
                    wait_apart(s, v, s["ch"], CH_PER * bn + k)
                else:
                    v.wait_ge(s["ch"], CH_PER * bn + k)

            def route_shift(bn):
                logits = Tb[:, 0, 0:TILES * EXPERTS].rearrange("p (t e) -> p t e", t=TILES)
                v.wait_ge(s["fill"], 3 * bn + (LOGITS + 1))
                if not is_int(bn, 0):
                    v.wait_ge(s["exp"], bn)
                route_step(bn, 1, v.tensor_reduce(top[:], logits, AX.X, ALU.max))
                route_step(bn, 2, v.tensor_tensor(lg[:], logits, each(top[:], EXPERTS), ALU.subtract))
                v.sem_inc(s["free"], 1)

            def route_softmax(bn):
                v.wait_ge(s["exp"], bn + 1)
                route_step(bn, 3, v.tensor_reduce(sm[:], ex[:], AX.X, ALU.add))
                route_step(bn, 4, v.reciprocal(rs[:], sm[:]))
                route_step(bn, 5, v.tensor_tensor(sc[:], ex[:], each(rs[:], EXPERTS), ALU.mult))
                route_step(bn, 6, v.tensor_tensor(bi[:], sc[:], both(gate_b[:], TILES), ALU.add))

            def route_top(bn):
                for t in range(TILES):
                    last = v.max(m8[:, t, :], bi[:, t, :])
                route_step(bn, 7, last)
                for t in range(TILES):
                    last = v.max_index(i8[:, t, :], m8[:, t, :], bi[:, t, :])
                route_step(bn, 8, last)

            def route_weights(bn):
                def chosen(r):
                    return i8f[:, :, r:r + 1].to_broadcast([P, TILES, EXPERTS])

                numbers = both(iota8[:], TILES)
                route_step(bn, 9, v.tensor_copy(i8f[:], i8[:]))
                route_step(bn, 10, v.tensor_tensor(k1[:], numbers, chosen(0), ALU.is_equal))
                route_step(bn, 11, v.tensor_tensor(k2[:], numbers, chosen(1), ALU.is_equal))
                route_step(bn, 12, v.tensor_tensor(k12[:], k1[:], k2[:], ALU.add))
                route_step(bn, 13, v.memset(rw[:, :, EXPERTS:ALL_EXP], 1.0))
                route_step(bn, 14, v.tensor_tensor(rw[:, :, 0:EXPERTS], sc[:], k12[:], ALU.mult))

            def split_rw(bn, half):
                v.wait_ge(s["fill"], 3 * bn + (RW + 1))
                v.wait_ge(s["rwT"], bn + 1)
                if not (isinstance(bn, int) and bn < 2):
                    v.wait_ge(s["up"], N * bn - N)
                v.tensor_scalar(rwr[0:ALL_EXP, half, :], Tb[0:ALL_EXP, 0, :], 1.0, None, ALU.mult).then_inc(s["rhi"], 1)
                v.wait_ge(s["rhi"], bn + 1)
                v.tensor_tensor(rwr[R_LOW:R_ROWS, half, :], Tb[0:ALL_EXP, 0, :],
                                rwr[0:ALL_EXP, half, :].bitcast(F32), ALU.subtract).then_inc(s["rlo"], 1)
                v.wait_ge(s["rlo"], bn + 1)
                v.sem_inc(s["free"], 1)

            def product(b, j, n):
                q = (13 * (n % 2) + j) % 2
                v.wait_ge(s["u3"], N * b + (j + 1))
                if not (is_int(b, 0) and j < 2):
                    v.wait_ge(s["th"], N * b + (j - 1))
                v.scalar_tensor_tensor(z[:, q, :], Ab[:, q, :], b1[:, j:j + 1], up3[:, q, :],
                                       ALU.add, ALU.mult).then_inc(s["z"], 1)

            def hidden(b, j, n):
                q = (13 * (n % 2) + j) % 2
                v.wait_ge(s["th"], N * b + (j + 1))
                if not (is_int(b, 0) and j < 2):
                    v.wait_ge(s["down"], N * b + (j - 1))
                v.tensor_tensor(hh[:, q, :], Rb[:, q, :], th[:, q, :], ALU.mult).then_inc(s["hh"], 1)

            def gated(b):
                v.wait_ge(s["y"], b + 1)
                if not is_int(b, 0):
                    v.wait_ge(s["xup"], b)
                v.tensor_tensor(t1[:].rearrange("p (t d) -> p t d", t=TILES),
                                Yb[:, 0, :].rearrange("p (t d) -> p t d", t=TILES),
                                gate[:, bass.ds(b, 1), :].to_broadcast([P, TILES, P]), ALU.mult).then_inc(s["t1"], 1)

            def body(b, half):
                for j in range(N):
                    product(b, j, half)
                    if j > 0:
                        hidden(b, j - 1, half)
                    elif not is_int(b, 0):
                        hidden(b - 1, N - 1, 1 - half)
                    if j == 1 and not is_int(b, 0):
                        gated(b - 1)
                    if not is_int(b, last_b):
                        if j == 0:
                            stats(b + 1)
                        if j == 2:
                            normalise(b + 1)
                        if j == 6:
                            route_shift(b + 1)
                        if j == 7:
                            route_softmax(b + 1)
                        if j == 8:
                            route_top(b + 1)
                        if j == 9:
                            route_weights(b + 1)
                        if j == 11:
                            split_rw(b + 1, 1 - half)

            stats(0)
            v.wait_ge(s["load"], 48)
            v.tensor_scalar(hi["w1"][:], raw["w1"][:], 1.0, None, ALU.mult).then_inc(s["hi1"], 1)
            normalise(0)
            v.wait_ge(s["hi1"], 1)
            v.tensor_tensor(lo["w1"][:], raw["w1"][:], hi["w1"][:].bitcast(F32), ALU.subtract).then_inc(s["lo1"], 1)
            for stage in (route_shift, route_softmax, route_top, route_weights):
                stage(0)
            v.wait_ge(s["zero"], 1)
            split_rw(0, 0)
            pairs(v, body)
            hidden(last_b, N - 1, 1)
            gated(last_b)

        @block.tensor
        def _(pe):
            def norm_T(bn):
                if not is_int(bn, 0):
                    pe.wait_ge(s["free"], 3 * bn + LN)
                pe.wait_ge(s["norm"], bn + 1)
                for t in range(TILES):
                    last = pe.transpose(Tb[:, 0, t * P:(t + 1) * P], xn[:, t, :], ident[:])
                last.then_inc(s["fill"], 1)

            def logits(bn):
                pe.wait_ge(s["free"], 3 * bn + LOGITS)
                pe.wait_ge(s["hT"], bn + 1)
                for t in range(TILES):
                    last = pe.matmul(Tb[:, 0, t * EXPERTS:(t + 1) * EXPERTS], hT[:, t * P:(t + 1) * P], gate_w[:],
                                     start=True, stop=True)
                last.then_inc(s["fill"], 1)

            def rw_T(bn):
                pe.wait_ge(s["free"], 3 * bn + RW)
                pe.wait_ge(s["ch"], CH_PER * (bn + 1))
                for t in range(TILES):
                    last = pe.transpose(Tb[0:ALL_EXP, 0, t * P:(t + 1) * P], rw[:, t, :], ident[:])
                last.then_inc(s["fill"], 1)

            def up(b, j, half):
                q = (13 * half + j) % 2
                if j == 0:
                    pe.wait_ge(s["hlo"], b + 1)
                    pe.wait_ge(s["rlo"], b + 1)
                if not (is_int(b, 0) and j < 2):
                    pe.wait_ge(s["z"], N * b + (j - 1))
                cols = slice(j * P, (j + 1) * P)
                for bankk, w in ((Ab, "w1"), (Bb, "w3")):
                    pe.matmul(bankk[:, q, :], hi[w][:, cols], h_hi[:, half, :], start=True, stop=False)
                    pe.matmul(bankk[:, q, :], hi[w][:, cols], h_lo[:, half, :], start=False, stop=False)
                    pe.matmul(bankk[:, q, :], lo[w][:, cols], h_hi[:, half, :], start=False, stop=True)
                if not (is_int(b, 0) and j < 2):
                    pe.wait_ge(s["hh"], N * b + (j - 1))
                pe.matmul(Rb[:, q, :], selr[:, cols], rwr[0:R_ROWS, half, :], start=True, stop=True)\
                  .then_inc(s["up"], 1)

            def down(b, j, half):
                q = (13 * half + j) % 2
                pe.wait_ge(s["hh"], N * b + (j + 1))
                if j == 0:
                    if not is_int(b, 0):
                        pe.wait_ge(s["t1"], b)
                    for t in range(TILES):
                        pe.matmul(Yb[:, 0, t * P:(t + 1) * P], rwT[:, half, t * P:(t + 1) * P], sb["b2"][:],
                                  start=(t == 0), stop=False, skip_group_check=True)
                for t in range(TILES):
                    last = pe.matmul(Yb[:, 0, t * P:(t + 1) * P], hh[:, q, t * P:(t + 1) * P], w2[:, j, :],
                                     start=False, stop=(j == N - 1), skip_group_check=True)
                last.then_inc(s["down"], 1)
                if j == N - 1:
                    pe.wait_ge(s["down"], N * b + N)
                    pe.sem_inc(s["y"], 1)

            def body(b, half):
                for j in range(N):
                    up(b, j, half)
                    if j >= 2:
                        down(b, j - 2, half)
                    elif not is_int(b, 0):
                        down(b - 1, N - 2 + j, 1 - half)
                    if not is_int(b, last_b):
                        if j == 3:
                            norm_T(b + 1)
                        if j == 5:
                            logits(b + 1)
                        if j == 10:
                            rw_T(b + 1)

            norm_T(0)
            logits(0)
            rw_T(0)
            pe.wait_ge(s["load2"], 16)
            pe.wait_ge(s["selr"], 1)
            pe.wait_ge(s["lo1"], 1)
            pe.wait_ge(s["lo3"], 1)
            pairs(pe, body)
            down(last_b, N - 2, 1)
            down(last_b, N - 1, 1)


def spike_phase(nc, dram, sb, out):
    x, ident, gate, mods = (sb[n] for n in ("x", "ident", "gateB1", "mods"))
    FT = FFN // P
    last_b = NBATCH - 1
    with ExitStack() as ctx:
        def tile(name, shape, dt=F32):
            return ctx.enter_context(nc.sbuf_tensor(f"sp_{name}", shape, dt))

        wfc = tile("wfc", [P, FFN])
        wproj = tile("wproj", [P, FFN // P, D])

        st = tile("st", [P, TILES, 6])
        mv = tile("mv", [P, TILES, 2])
        ve = tile("ve", [P, TILES])
        rstd = tile("rstd", [P, TILES])
        xn = tile("xn", [P, TILES, P])
        hT = tile("hT", [P, SEQ])
        relu = tile("relu", [P, 2, SEQ])
        sq = tile("sq", [P, 2, SEQ])
        y = tile("y", [P, SEQ])
        drive = tile("drive", [P, SEQ])
        nmem = tile("nmem", [P, 2, SEQ])
        cnt = tile("cnt", [P, 2, SEQ])
        t1 = tile("t1", [P, SEQ])

        def bank(name, n=1):
            return ctx.enter_context(nc.psum_tensor(f"sp_{name}", [P, n, 512], F32))

        Ub, Yb, Tb = bank("Ub", 2), bank("Yb", 2), bank("Tb")
        s = semaphores(nc, ctx, "sp", "load stats aggr veps rstd norm fill hT up relu sq down y yread ch t1 xup store apart")
        block = ctx.enter_context(nc.Block())

        def is_int(b, k):
            return isinstance(b, int) and b == k

        def loop(eng, body):
            body(0)
            with eng.Fori(1, last_b) as b:
                body(b)
            body(last_b)

        @block.gpsimd
        def _(p):
            def powers(bn):
                p.wait_ge(s["veps"], bn + 1)
                p.tensor_tensor(rstd[:], ve[:], sb["mhalf"][:], ALU.pow).then_inc(s["rstd"], 1)

            def update_x(b):
                xb = x[:, bass.ds(b * SEQ, SEQ)]
                wait_apart(s, p, s["t1"], b + 1)
                p.tensor_tensor(xb, xb, t1[:], ALU.add).then_inc(s["xup"], 1)

            def body(b):
                if not is_int(b, last_b):
                    powers(b + 1)
                update_x(b)

            powers(0)
            loop(p, body)

        @block.sync
        def _(sp):
            def body(b):
                sp.wait_ge(s["xup"], b + 1)
                sp.dma_start(out[bass.ds(b, 1)].rearrange("b (t p) d -> p (b t) d", p=P),
                             x[:, bass.ds(b * SEQ, SEQ)].rearrange("p (t d) -> p t d", t=TILES)).then_inc(s["store"], 16)
            sp.dma_start(wfc[:], dram["wfc"]).then_inc(s["load"], 16)
            sp.dma_start(wproj[:], dram["wproj"]).then_inc(s["load"], 16)
            loop(sp, body)
            sp.wait_ge(s["store"], 16 * NBATCH)

        @block.tensor
        def _(pe):
            def norm_T(bn):
                if not is_int(bn, 0):
                    pe.wait_ge(s["hT"], bn)
                pe.wait_ge(s["norm"], bn + 1)
                for t in range(TILES):
                    last = pe.transpose(Tb[:, 0, t * P:(t + 1) * P], xn[:, t, :], ident[:])
                last.then_inc(s["fill"], 1)

            def down(b, f):
                pe.wait_ge(s["sq"], FT * b + (f + 1))
                if f == 0 and not is_int(b, 0):
                    pe.wait_ge(s["yread"], b)
                for t in range(TILES):
                    last = pe.matmul(Yb[:, 0, t * P:(t + 1) * P], sq[:, f % 2, t * P:(t + 1) * P], wproj[:, f, :],
                                     start=(f == 0 and t == 0), stop=(f == FT - 1), skip_group_check=True)
                last.then_inc(s["down"], 1)

            def body(b):
                pe.wait_ge(s["hT"], b + 1)
                for f in range(FT):
                    if not (is_int(b, 0) and f < 2):
                        pe.wait_ge(s["relu"], FT * b + (f - 1))
                    pe.matmul(Ub[:, f % 2, :], wfc[:, f * P:(f + 1) * P], hT[:], start=True, stop=True)\
                      .then_inc(s["up"], 1)
                    if f == FT - 1 and not is_int(b, last_b):
                        norm_T(b + 1)
                    if f >= 1:
                        down(b, f - 1)
                down(b, FT - 1)

            norm_T(0)
            pe.wait_ge(s["load"], 32)
            loop(pe, body)

        @block.scalar
        def _(a):
            def read_hT(bn):
                a.wait_ge(s["fill"], bn + 1)
                if not is_int(bn, 0):
                    a.wait_ge(s["up"], FT * bn)
                nc.scalar.activation(hT[:], Tb[:, 0, :], ACT.Identity, bias=mods[:, 1, 2, bass.ds(bn, 1)],
                                     scale=mods[:, 1, 3, bass.ds(bn, 1)]).then_inc(s["hT"], 1)

            def body(b):
                for f in range(FT):
                    a.wait_ge(s["up"], FT * b + (f + 1))
                    nc.scalar.activation(relu[:, f % 2, :], Ub[:, f % 2, :], ACT.Relu).then_inc(s["relu"], 1)
                    a.wait_ge(s["relu"], FT * b + (f + 1))
                    if not (is_int(b, 0) and f < 2):
                        a.wait_ge(s["down"], FT * b + (f - 1))
                    nc.scalar.activation(sq[:, f % 2, :], relu[:, f % 2, :], ACT.Square).then_inc(s["sq"], 1)
                if not is_int(b, last_b):
                    read_hT(b + 1)

            read_hT(0)
            loop(a, body)

        @block.vector
        def _(v):
            CH = 3 * (STEPS - 1) + 2

            def stats(bn):
                for t in range(TILES):
                    last = v.bn_stats(st[:, t, :], x[:, bass.ds(bn * SEQ + t * P, P)])
                last.then_inc(s["stats"], 1)
                wait_apart(s, v, s["stats"], bn + 1)
                for t in range(TILES):
                    last = v.bn_aggr(mv[:, t, :], st[:, t, :])
                last.then_inc(s["aggr"], 1)
                v.wait_ge(s["aggr"], bn + 1)
                v.tensor_scalar(ve[:], mv[:, :, 1], EPS, None, ALU.add).then_inc(s["veps"], 1)

            def normalise(bn):
                v.wait_ge(s["rstd"], bn + 1)
                if not is_int(bn, 0):
                    v.wait_ge(s["fill"], bn)
                for t in range(TILES):
                    last = v.tensor_scalar(xn[:, t, :], x[:, bass.ds(bn * SEQ + t * P, P)], mv[:, t, 0:1],
                                           rstd[:, t:t + 1], ALU.subtract, ALU.mult)
                last.then_inc(s["norm"], 1)

            def spikes(b):
                k = [0]

                def step(ins):
                    k[0] += 1
                    ins.then_inc(s["ch"], 1)
                    v.wait_ge(s["ch"], CH * b + k[0])

                v.wait_ge(s["down"], FT * b + FT)
                step(v.tensor_copy(y[:], Yb[:, 0, :]))
                v.sem_inc(s["yread"], 1)
                v.tensor_scalar(nmem[:, 0, :], y[:], -1.0, None, ALU.mult).then_inc(s["y"], 1)
                step(v.tensor_scalar(cnt[:, 0, :], y[:], 1.0, None, ALU.is_gt))
                v.wait_ge(s["y"], b + 1)
                for i in range(1, STEPS):
                    old, new = (i - 1) % 2, i % 2
                    step(v.scalar_tensor_tensor(drive[:], nmem[:, old, :], -BETA, y[:], ALU.mult, ALU.add))
                    step(v.scalar_tensor_tensor(nmem[:, new, :], nmem[:, old, :], -1.0, drive[:],
                                                ALU.is_lt, ALU.subtract))
                    step(v.scalar_tensor_tensor(cnt[:, new, :], nmem[:, new, :], -1.0, cnt[:, old, :],
                                                ALU.is_lt, ALU.add))
                if not is_int(b, 0):
                    v.wait_ge(s["xup"], b)
                v.scalar_tensor_tensor(t1[:].rearrange("p (t d) -> p t d", t=TILES),
                                       cnt[:, (STEPS - 1) % 2, :].rearrange("p (t d) -> p t d", t=TILES), 1.0 / STEPS,
                                       gate[:, bass.ds(b, 1), :].to_broadcast([P, TILES, P]),
                                       ALU.mult, ALU.mult).then_inc(s["t1"], 1)

            def body(b):
                if not is_int(b, last_b):
                    stats(b + 1)
                    normalise(b + 1)
                spikes(b)

            stats(0)
            normalise(0)
            loop(v, body)


def build(nc, dram, out, stop=4):
    with ExitStack() as ctx:
        sb = {}

        def tile(name, shape, dt=F32):
            sb[name] = ctx.enter_context(nc.sbuf_tensor(name, shape, dt))

        tile("x", [P, NBATCH * SEQ])
        tile("ident", [P, P])
        tile("mhalf", [P, TILES])
        tile("mods", [P, 2, 4, NBATCH])
        for layer in range(2):
            for n in (f"gateA{layer}", f"gateB{layer}"):
                tile(n, [P, NBATCH, P])
            tile(f"wqkv{layer}", [P, 3 * D])
            tile(f"bqk{layer}", [P, 2])
            tile(f"bv{layer}", [P, D])
            tile(f"bo{layer}", [P, D])
            tile(f"wo{layer}", [P, D])
        tile("gate_w", [P, EXPERTS])
        tile("gate_b", [P, EXPERTS])
        tile("iota8", [P, EXPERTS])
        tile("b1", [P, HTILES])
        tile("b3", [P, HTILES])
        tile("b2", [ALL_EXP, D])
        setup_phase(nc, dram, sb)
        if stop >= 1:
            attention_phase(nc, dram, sb, 0)
        if stop >= 2:
            expert_phase(nc, dram, sb)
        if stop >= 3:
            attention_phase(nc, dram, sb, 1)
        if stop >= 4:
            spike_phase(nc, dram, sb, out)
        else:
            with nc.semaphore("dbg") as q, nc.Block() as blk:
                @blk.sync
                def _(sp):
                    for b in range(NBATCH):
                        sp.dma_start(out[b].rearrange("(t p) d -> p t d", p=P),
                                     sb["x"][:, b * SEQ:(b + 1) * SEQ].rearrange("p (t d) -> p t d", t=TILES)).then_inc(q, 16)
                    sp.wait_ge(q, 16 * NBATCH)


def _bf16_parts(np, a, n):
    out, rest = [], a.astype(np.float64)
    for _ in range(n):
        part = rest.astype(np.float32).astype("bfloat16")
        out.append(part)
        rest = rest - part.astype(np.float64)
    return out


def constants(np):
    slopes = (2.0 ** -0.5) ** np.arange(1, HEADS + 1)
    slopes = slopes.astype(np.float32).astype(np.float64)
    pos = np.arange(SEQ)
    c = {}
    zero = np.zeros((N_ALIBI, HEADS, SEQ), "bfloat16")
    c["aliq0"], c["alik0"] = zero, zero
    sj = _bf16_parts(np, slopes[:, None] * pos[None], 3)
    si = _bf16_parts(np, -slopes[:, None] * pos[None], 3)
    q, k = zero.copy(), zero.copy()
    for kt in range(TILES - 1):
        after = (pos >= (kt + 1) * P)[None]
        inside = ((pos >= kt * P) & (pos < (kt + 1) * P))[None]
        for part in range(3):
            r = 6 * kt + part
            q[r] = after
            k[r] = sj[part] * inside
            q[r + 3] = si[part] * after
            k[r + 3] = np.broadcast_to(inside, k[r].shape)
    c["aliq1"], c["alik1"] = q, k
    c["shiftq0"] = np.zeros((1, HEADS, SEQ), "bfloat16")
    c["shiftq1"] = np.full((1, HEADS, SEQ), ALIBI_SHIFT, "bfloat16")
    c["ones3"] = np.ones((3, HEADS, SEQ), "bfloat16")
    p = np.arange(P)
    c["mask0"] = np.where(p[None] > p[:, None], -1e30, 0.0).astype("bfloat16")
    bias = slopes[None, :, None] * np.minimum(p[None, None] - p[:, None, None], 0)
    c["mask1"] = bias.astype(np.float32).astype("bfloat16")
    c["alibi"] = np.ascontiguousarray(bias.transpose(2, 1, 0)).astype(np.float32)
    sel = np.zeros((64 + ALL_EXP, HPAD), np.float32)
    unit = np.arange(ALL_EXP * HID)
    sel[unit // HID, unit] = 1.0
    sel[64 + unit // HID, unit] = 1.0
    c["sel"] = sel
    c["iota8"] = np.arange(EXPERTS, dtype=np.float32)[None]
    return c


def layout(np, i):
    def f(a):
        return np.ascontiguousarray(a)

    def heads(w):
        n = w.shape[0]
        return w.reshape(n, HEADS, DK).transpose(0, 2, 1).reshape(n, D)

    def by_strip(w):
        return w.reshape(GROUPS, GROUP, DK, D).transpose(1, 2, 0, 3).reshape(D, D)

    d = {"x": f(i["L0_attn_embeddings"])}
    wq, wk, wv = (np.asarray(i[f"L0_attn_W{n}"]).transpose(1, 0, 2).reshape(D, D) for n in "qkv")
    d["wqkv0"] = f(np.concatenate([heads(wq), heads(wk), wv], 1))
    bq, bk, bv = (np.asarray(i[f"L0_attn_b{n}"]).reshape(1, D) for n in "qkv")
    d["bqk0"] = f(np.concatenate([heads(bq), heads(bk)], 0).T)
    d["bv0"] = f(bv)
    w, b = np.asarray(i["L1_attn_W_qkv"]), np.asarray(i["L1_attn_b_qkv"]).reshape(1, 3 * D)
    d["wqkv1"] = f(np.concatenate([heads(w[:, 0:D]), heads(w[:, D:2 * D]), w[:, 2 * D:]], 1))
    d["bqk1"] = f(np.concatenate([heads(b[:, 0:D]), heads(b[:, D:2 * D])], 0).T)
    d["bv1"] = f(b[:, 2 * D:])
    d["wo0"], d["wo1"] = (f(by_strip(np.asarray(i[n]))) for n in ("L0_attn_Wo", "L1_attn_W_proj"))
    d["bo0"], d["bo1"] = f(np.asarray(i["L0_attn_bo"])[None]), f(np.asarray(i["L1_attn_b_proj"])[None])
    for layer in range(2):
        d[f"c{layer}"] = f(np.asarray(i[f"L{layer}_c"]).T)
        d[f"wmod{layer}"] = f(i[f"L{layer}_wmod"])
    d["gate_w"] = f(np.asarray(i["L0_ffn_gate_w"]).T)
    d["gate_b"] = f(np.asarray(i["L0_ffn_gate_b"])[None])
    pad = HPAD - ALL_EXP * HID
    for n in ("1", "3"):
        up = np.asarray(i[f"L0_ffn_w{n}"]).transpose(1, 0, 2).reshape(D, EXPERTS * HID)
        d[f"w{n}"] = f(np.pad(np.concatenate([up, np.asarray(i[f"L0_ffn_sw{n}"])], 1), ((0, 0), (0, pad))))
        bb = np.concatenate([np.asarray(i[f"L0_ffn_b{n}"]).reshape(-1), np.asarray(i[f"L0_ffn_sb{n}"])])
        d[f"b{n}"] = f(np.pad(bb, (0, pad)).reshape(HTILES, P).T)
    w2 = np.concatenate([np.asarray(i["L0_ffn_w2"]).reshape(-1, D), np.asarray(i["L0_ffn_sw2"])])
    d["w2"] = f(np.pad(w2, ((0, pad), (0, 0))).reshape(HTILES, P, D).transpose(1, 0, 2))
    d["b2"] = f(np.concatenate([np.asarray(i["L0_ffn_b2"]), np.asarray(i["L0_ffn_sb2"])[None]]))
    d["wfc"] = f(np.asarray(i["L1_ffn_W_fc"]).T)
    d["wproj"] = f(np.asarray(i["L1_ffn_W_proj"]).T.reshape(FFN // P, P, D).transpose(1, 0, 2))
    return d


def kernel(**inputs):
    import numpy as np
    import concourse.bacc as bacc
    from concourse.bass_utils import run_bass_kernel_spmd

    arrays = {**layout(np, {k: np.asarray(v) for k, v in inputs.items()}), **constants(np)}
    nc = bacc.Bacc("TRN2", target_bir_lowering=False, num_devices=1)
    dram = {n: nc.dram_tensor(f"in_{n}", a.shape, mybir.dt.from_np(a.dtype), kind="ExternalInput").ap()
            for n, a in arrays.items()}
    out = nc.dram_tensor("out", (NBATCH, SEQ, D), F32, kind="ExternalOutput").ap()
    build(nc, dram, out)
    r = run_bass_kernel_spmd(nc, [{f"in_{n}": a for n, a in arrays.items()}], core_ids=[0])
    return r.results[0]["out"]
```

```python
from contextlib import ExitStack

import concourse.bass as bass
from concourse import mybir

F32 = mybir.dt.float32
F32R = mybir.dt.float32r
BF16 = mybir.dt.bfloat16
U32 = mybir.dt.uint32
ALU = mybir.AluOpType
ACT = mybir.ActivationFunctionType
AX = mybir.AxisListType

P = 128
NBATCH, SEQ, D = 8, 512, 128
HEADS, DK = 16, 8
TILES = SEQ // P
GROUP = 4
GROUPS = HEADS // GROUP
EPS = 1e-5
EXPERTS, HID = 8, 176
ALL_EXP = EXPERTS + 1
HTILES = -(-ALL_EXP * HID // P)
HPAD = HTILES * P
FFN = 512
STEPS, BETA = 5, 0.9
GATE_MIN = 0.25
CH_SA, CH_CA, CH_GA, CH_SB, CH_CB, CH_GB = range(6)

Q_PARTS = (0, 0, 1, 1, 0, 2)
K_PARTS = (0, 1, 0, 1, 2, 0)
R_ALIBI = 8 * len(Q_PARTS)
N_ALIBI = 6 * (TILES - 1)
R_SHIFT = R_ALIBI + N_ALIBI
R_ALL = R_SHIFT + 3
ALIBI_SHIFT = -20.0
DENS = DK
VW = 32


def offsets(*widths):
    at, where = 0, {}
    for name, width in widths:
        where[name] = at
        at += width
    where["end"] = at
    return where


COLUMNS = offsets(("wqkv0", 3 * D), ("wo0", D), ("wqkv1", 3 * D), ("wo1", D), ("bqk0", 2), ("bqk1", 2),
                  ("gate_w", EXPERTS), ("b1", HTILES), ("b3", HTILES))
ROWS = offsets(("bv0", D), ("bo0", D), ("bv1", D), ("bo1", D), ("gate_b", EXPERTS), ("iota8", EXPERTS))


def both(ap, n):
    return ap.unsqueeze(1).to_broadcast([ap.shape[0], n, ap.shape[1]])


def each(ap, n):
    return ap.unsqueeze(2).to_broadcast([ap.shape[0], ap.shape[1], n])


def semaphores(nc, ctx, phase, names):
    return {n: ctx.enter_context(nc.semaphore(f"{phase}_{n}")) for n in names.split()}


def wait_apart(s, eng, sem, value):
    eng.wait_ge(sem, value)
    if not isinstance(value, int):
        eng.sem_inc(s["apart"], 1)


def setup_phase(nc, dram, sb):
    x, ident = sb["x"], sb["ident"]
    with ExitStack() as ctx:
        def tile(name, shape, dt=F32):
            return ctx.enter_context(nc.sbuf_tensor(name, shape, dt))

        cT = tile("cT", [P, 2, NBATCH])
        half = tile("c_tanh", [P, 2, NBATCH])
        sil2 = tile("c_silu2", [P, 2, NBATCH])
        sil = tile("c_silu", [P, 2, NBATCH])
        wmod = tile("wmod", [P, 2, 6 * D])
        gsign = tile("gate_sign", [NBATCH, 4 * P])
        gabs = tile("gate_abs", [NBATCH, 4 * P])
        gmax = tile("gate_max", [NBATCH, 4 * P])
        ps = ctx.enter_context(nc.psum_tensor("setup_ps", [P, 2, 512], F32))
        s = semaphores(nc, ctx, "su", "c wmod load zero ident tanh sil mm chain")
        s["apart"] = sb["apart"]
        block = ctx.enter_context(nc.Block())

        @block.sync
        def _(sp):
            sp.dma_start(cT[:], dram["c"]).then_inc(s["c"], 16)
            sp.dma_start(x[:, 0:SEQ].rearrange("p (t d) -> p t d", t=TILES),
                         dram["x"][0].rearrange("(t p) d -> p t d", p=P)).then_inc(s["load"], 16)
            sp.dma_start(wmod[:], dram["wmod"]).then_inc(s["wmod"], 16)
            sp.dma_start(sb["columns"][:], dram["columns"]).then_inc(s["load"], 16)
            sp.dma_start(sb["rows"][:], dram["rows"].partition_broadcast(P)).then_inc(s["load"], 16)
            sp.dma_start(sb["b2"][:], dram["b2"]).then_inc(s["load"], 16)
            sp.dma_start(x[:, SEQ:].rearrange("p (m d) -> p m d", d=D),
                         dram["x"][1:].rearrange("b (t p) d -> p (b t) d", p=P)).then_inc(sb["x_rest"], 16)
            sp.wait_ge(s["load"], 64)

        @block.gpsimd
        def _(g):
            g.memset(ident[:], 0.0).then_inc(s["zero"], 1)
            g.memset(sb["mhalf"][:], -0.5)
            g.wait_ge(s["zero"], 1)
            g.affine_select(out=ident[:], in_=ident[:], compare_op=ALU.not_equal, fill=1.0, base=0,
                            pattern=[[-1, P]], channel_multiplier=1).then_inc(s["ident"], 1)

        @block.scalar
        def _(a):
            a.wait_ge(s["c"], 16)
            nc.scalar.activation(half[:], cT[:], ACT.Tanh, scale=0.5).then_inc(s["tanh"], 1)

        @block.tensor
        def _(t):
            t.wait_ge(s["sil"], 1)
            t.wait_ge(s["wmod"], 16)
            for layer in range(2):
                for i, ch in enumerate((CH_GA, CH_GB)):
                    k = 2 * layer + i
                    last = t.matmul(ps[0:NBATCH, 0, k * P:(k + 1) * P], sil[:, layer, :],
                                    wmod[:, layer, ch * D:(ch + 1) * D], start=True, stop=True)
            last.then_inc(s["mm"], 1)
            for layer in range(2):
                for i, ch in enumerate((CH_SA, CH_CA, CH_SB, CH_CB)):
                    k = layer * 4 + i
                    last = t.matmul(ps[:, 1, k * NBATCH:(k + 1) * NBATCH], wmod[:, layer, ch * D:(ch + 1) * D],
                                    sil[:, layer, :], start=True, stop=True)
            last.then_inc(s["mm"], 1)

        @block.vector
        def _(v):
            v.wait_ge(s["tanh"], 1)
            v.scalar_tensor_tensor(sil2[:], half[:], 1.0, cT[:], ALU.add, ALU.mult).then_inc(s["chain"], 1)
            v.wait_ge(s["chain"], 1)
            v.tensor_scalar(sil[:], sil2[:], 0.5, None, ALU.mult).then_inc(s["sil"], 1)
            v.wait_ge(s["mm"], 1)
            src = ps[0:NBATCH, 0, :]
            v.tensor_scalar(gsign[:], src, 0.0, 2.0, ALU.is_ge, ALU.mult).then_inc(s["chain"], 1)
            v.wait_ge(s["chain"], 2)
            v.scalar_tensor_tensor(gabs[:], gsign[:], -1.0, src, ALU.add, ALU.mult).then_inc(s["chain"], 1)
            v.wait_ge(s["chain"], 3)
            v.tensor_scalar(gmax[:], gabs[:], GATE_MIN, None, ALU.max).then_inc(s["chain"], 1)
            v.wait_ge(s["chain"], 4)
            v.scalar_tensor_tensor(sb["gate_rows"][:], gsign[:], -1.0, gmax[:], ALU.add, ALU.mult)\
             .then_inc(s["chain"], 1)
            v.wait_ge(s["mm"], 2)
            for layer in range(2):
                for i in range(4):
                    k = layer * 4 + i
                    v.tensor_scalar(sb["mods"][:, layer, i, :], ps[:, 1, k * NBATCH:(k + 1) * NBATCH],
                                    float(i % 2), None, ALU.add)


def finish_gather(sp, sb, s, b):
    wait_apart(s, sp, s["oev"], GROUPS * (b + 1))
    if not (isinstance(b, int) and b == 0):
        sp.wait_ge(s["ctx"], b)
    sp.dma_start(sb["den"][:], sb["Oev"][DENS::VW, :, :]).then_inc(s["compact"], 16)
    for i in range(GROUP):
        sp.dma_start(sb["ctxN"][32 * i:32 * i + 32, :], sb["Oev"][VW * i:VW * i + DK, :, :]).then_inc(s["gath"], 16)


def finish_recip(v, sb, s, b):
    v.wait_ge(s["compact"], 16 * (b + 1))
    if not (isinstance(b, int) and b == 0):
        v.wait_ge(s["rden16"], 16 * b)
    v.reciprocal(sb["rden"][:], sb["den"][:]).then_inc(s["rden"], 1)


def finish_spread(sp, sb, s, b):
    sp.wait_ge(s["rden"], b + 1)
    sp.dma_start(sb["rden16"][:], sb["rden"][:]).then_inc(s["rden16"], 16)
    sp.wait_ge(s["rden16"], 16 * (b + 1))
    for g in range(GROUPS):
        sp.dma_start(sb["denB"][g::GROUPS, :],
                     sb["rden16"][g::GROUPS, :].unsqueeze(1).to_broadcast([GROUP, DK, SEQ])).then_inc(s["dden"], 16)


def finish_context(v, sb, s, b):
    v.wait_ge(s["gath"], 64 * (b + 1))
    v.wait_ge(s["dden"], 64 * (b + 1))
    if not (isinstance(b, int) and b == 0):
        v.wait_ge(s["t1"], b)
    v.tensor_tensor(sb["ctxT"][:], sb["ctxN"][:], sb["denB"][:], ALU.mult).then_inc(s["ctx"], 1)


def finish_project(pe, sb, s, layer, b, bank):
    pe.wait_ge(s["ctx"], b + 1)
    for t in range(TILES):
        last = pe.matmul(bank[:, t * P:(t + 1) * P], sb["ctxT"][:, t * P:(t + 1) * P], sb[f"wo{layer}"][:],
                         start=True, stop=True)
    return last


def finish_gated(v, sb, s, layer, b, bank):
    if isinstance(b, int) and b == 0 and layer == 0:
        v.wait_ge(sb["gates_ready"], 16 * NBATCH)
    if not (isinstance(b, int) and b == 0):
        v.wait_ge(s["xup"], b)
    v.tensor_tensor(sb["t1"][:].rearrange("p (t d) -> p t d", t=TILES), bank.rearrange("p (t d) -> p t d", t=TILES),
                    sb[f"gateA{layer}"][:, bass.ds(b, 1), :].to_broadcast([P, TILES, P]), ALU.mult)\
     .then_inc(s["t1"], 1)


def finish_x(p, sb, s, layer, b):
    xb = sb["x"][:, bass.ds(b * SEQ, SEQ)]
    if isinstance(b, int) and b == 0:
        if layer == 0:
            p.wait_ge(sb["gates_ready"], 16 * NBATCH)
    else:
        wait_apart(s, p, s["bias"], 2 * b)
    p.tensor_tensor(sb["gbo"][:].unsqueeze(1), sb[f"gateA{layer}"][:, bass.ds(b, 1), :],
                    sb[f"bo{layer}"][:].unsqueeze(1), ALU.mult).then_inc(s["bias"], 1)
    wait_apart(s, p, s["t1"], b + 1)
    p.tensor_tensor(xb, xb, sb["t1"][:], ALU.add).then_inc(s["xup"], 1)
    p.wait_ge(s["xup"], b + 1)
    wait_apart(s, p, s["bias"], 2 * b + 1)
    xv = xb.rearrange("p (t d) -> p t d", t=TILES)
    p.tensor_tensor(xv, xv, both(sb["gbo"][:], TILES), ALU.add).then_inc(s["bias"], 1)


def attention_phase(nc, dram, sb, layer):
    causal = layer == 0
    ph = f"at{layer}"
    x, ident, mods = sb["x"], sb["ident"], sb["mods"]
    wqkv, bqk, bv = (sb[f"{n}{layer}"] for n in ("wqkv", "bqk", "bv"))
    Oev = sb["Oev"]
    with ExitStack() as ctx:
        def tile(name, shape, dt=F32):
            return ctx.enter_context(nc.sbuf_tensor(f"{ph}_{name}", shape, dt))

        QP = tile("QP", [R_ALL, 2, HEADS, SEQ], BF16)
        KP = tile("KP", [R_ALL, 2, HEADS, SEQ], BF16)
        E = tile("E", [P, TILES, GROUP, SEQ])
        VP = tile("VP", [P, 2, TILES, HEADS, VW])
        xn = tile("xn", [P, TILES, P])
        hT = tile("hT", [P, SEQ])
        parts = {n: tile(n, [P, SEQ], BF16) for n in ("q0", "q1", "q2", "k0", "k1", "k2")}
        rest = {n: tile(f"rest_{n}", [P, SEQ]) for n in "qk"}
        st = tile("st", [P, TILES, 6])
        mv = tile("mv", [P, TILES, 2])
        ve = tile("ve", [P, TILES])
        rstd = tile("rstd", [P, TILES])
        mx = tile("mx", [P, 2, GROUP * TILES])
        nmx = tile("nmx", [P, 2, 2, GROUP * TILES], BF16)
        nrow = tile("nrow", [2 * GROUP * TILES, 2, P], BF16)
        idb = tile("idb", [P, P], BF16)
        if causal:
            mask = tile("mask", [P, P], BF16)
        else:
            mask = tile("mask", [P, HEADS, P], BF16)
            factor = tile("factor", [P, HEADS, P])

        def bank(name, n=1):
            return ctx.enter_context(nc.psum_tensor(f"{ph}_{name}", [P, n, 512], F32))

        Mb, Sb, Ob, Tb = bank("Mb", 3), bank("Sb", 3), bank("Ob"), bank("Tb")

        s = sb["attention"] = semaphores(
            nc, sb["keep"], ph, "const const2 table zero wscale fac stats veps rstd norm fill free hT p0 p1 p2 "
            "rest maxs maxd nr0 nr1 nrow score exp diag vp pv oev gath compact rden rden16 dden ctx t1 bias xup k_first")
        pk = [ctx.enter_context(nc.semaphore(f"{ph}_stacked{which}")) for which in range(2)]
        mrow = [ctx.enter_context(nc.semaphore(f"{ph}_shift_rows{g}")) for g in range(GROUPS)]
        s["apart"] = sb["apart"]
        block = ctx.enter_context(nc.Block())

        scale = float(DK) ** -0.5

        FILLS = {(0, 0): "ln", (0, 3): "m1", (1, 2): "q", (2, 2): "k", (3, 2): "v", (4, 3): "m2", (8, 3): "m3",
                 (11, 3): "ctx", (12, 3): "m0"}

        def fill(b, name):
            if isinstance(b, int) and b == -1:
                return ["ln", "q", "k", "v", "m0"].index(name)
            order = list(FILLS.values())
            if isinstance(b, int) and b == 0:
                order.remove("ctx")
                return 5 + order.index(name)
            if isinstance(b, int) and b == NBATCH - 1:
                order = ["m1", "m2", "m3", "ctx"]
            return b * 9 + (4 + order.index(name))

        def filled(b, u, i, later=0):
            name = FILLS.get(divmod(u * GROUP + i - later, GROUP))
            if is_first(b) and name == "ctx" or is_last(b) and name in ("ln", "q", "k", "v", "m0"):
                return None
            return name

        def group_of(b, name):
            g = int(name[1])
            return (b + 1, 0) if g == 0 else (b, g)

        PER_M = GROUPS * GROUP * TILES
        UNITS = GROUPS * TILES
        KEY_TILES = (0, 3, 1, 2) if causal else (0, 1, 2, 3)
        VLAG = 2

        def before(n):
            return n - 3 if n >= 3 else (-1, -3, -2)[n]

        def groups_of(b, g):
            return (b, g + 2) if g < 2 else (b + 1, g - 2)

        last_b = NBATCH - 1

        def pairs(eng, steps):
            steps(0, 0)
            steps(1, 1)
            with eng.Fori(1, NBATCH // 2 - 1) as pair:
                steps(pair * 2, 0)
                steps(pair * 2 + 1, 1)
            steps(last_b - 1, 0)
            steps(last_b, 1)

        def is_last(b):
            return isinstance(b, int) and b == last_b

        def is_first(b):
            return isinstance(b, int) and b == 0

        @block.tensor
        def _(pe):
            def fill_wait(k):
                if not (isinstance(k, int) and k == 0):
                    pe.wait_ge(s["free"], k)

            def norm_T(bn, k):
                fill_wait(k)
                pe.wait_ge(s["norm"], bn + 1)
                for t in range(TILES):
                    last = pe.transpose(Tb[:, 0, t * P:(t + 1) * P], xn[:, t, :], ident[:])
                last.then_inc(s["fill"], 1)

            def project(which, bn, k):
                bank = Tb[:, 0, :]
                if is_first(bn):
                    bank = Mb[:, "qkv".index(which), :]
                else:
                    fill_wait(k)
                pe.wait_ge(s["hT"], bn + 1)
                if which == "v":
                    for t in range(TILES):
                        last = pe.matmul(bank[:, t * P:(t + 1) * P], hT[:, t * P:(t + 1) * P],
                                         wqkv[:, 2 * D:3 * D], start=True, stop=True)
                else:
                    w = wqkv[:, 0:D] if which == "q" else wqkv[:, D:2 * D]
                    last = pe.matmul(bank, w, hT[:], start=True, stop=True)
                last.then_inc(s["fill"], 1)

            def max_score(bm, gm, i, qt, half):
                h = GROUP * gm + i
                n = h * TILES + qt
                if n == 0:
                    if isinstance(bm, int) and bm == 1:
                        pe.wait_ge(s["const2"], 64)
                    for which in range(2):
                        pe.wait_ge(pk[which], 96 * (bm + 1))
                if is_first(bm) and n < 3:
                    pe.wait_ge(s["p0" if n < 2 else "vp"], (1, 2, 1)[n])
                else:
                    pe.wait_ge(s["maxd"], bm * PER_M + (before(n) + 1))
                width = (qt + 1) * P if causal else SEQ
                out = Mb[:, n % 3, :]
                pe.matmul(out[:, 0:width], QP[0:R_SHIFT, half, h, qt * P:(qt + 1) * P],
                          KP[0:R_SHIFT, half, h, 0:width],
                          start=True, stop=True)
                pe.matmul(out[:, qt * P:(qt + 1) * P], idb[:], mask[:] if causal else mask[:, h, :],
                          start=False, stop=True, skip_group_check=True).then_inc(s["maxs"], 1)

            def max_T(bm, gm, k):
                fill_wait(k)
                pe.wait_ge(s["nr1"], GROUPS * bm + (gm + 1))
                pe.transpose(Tb[0:32, 0, 0:P // 2].bitcast(BF16), nmx[:, gm % 2].rearrange("p a c -> p (a c)"),
                             idb[:]).then_inc(s["fill"], 1)

            def key_score(b, g, kt, i, half):
                if kt == 0 and i == 0:
                    pe.wait_ge(mrow[g], 16 * (b + 1))
                h = GROUP * g + i
                n = (GROUP * g + kt) * GROUP + i
                if not (is_first(b) and n < 3):
                    pe.wait_ge(s["exp"], b * PER_M + (before(n) + 1))
                kt = KEY_TILES[kt]
                q0 = kt * P if causal else 0
                pe.matmul(Sb[:, n % 3, q0:SEQ], KP[:, half, h, kt * P:(kt + 1) * P], QP[:, half, h, q0:SEQ],
                          start=True, stop=True).then_inc(s["score"], 1)

            def values(bp, gp, kt, half):
                pe.wait_ge(s["diag"], UNITS * bp + (TILES * gp + kt + 1))
                if kt == 0:
                    if gp == 0:
                        pe.wait_ge(s["vp"], bp + 1)
                    if not (is_first(bp) and gp == 0):
                        pe.wait_ge(s["oev"], GROUPS * bp + gp)
                opens, closes = kt == 0, kt == TILES - 1
                kt = KEY_TILES[kt]
                q0 = kt * P if causal else 0
                for i in range(GROUP):
                    last = pe.matmul(Ob[VW * i:VW * (i + 1), 0, q0:SEQ], VP[:, half, kt, GROUP * gp + i, :],
                                     E[:, kt, i, q0:SEQ], start=opens, stop=closes)
                last.then_inc(s["pv"], 1)

            def out_proj(bo, k):
                fill_wait(k)
                finish_project(pe, sb, s, layer, bo, Tb[:, 0, :]).then_inc(s["fill"], 1)

            def steps(b, half):
                for u in range(UNITS):
                    g, kt = divmod(u, TILES)
                    bm, gm = groups_of(b, g)
                    gp, ktp = divmod((u - VLAG) % UNITS, TILES)
                    bp, halfp = (b, half) if u >= VLAG else (b - 1, 1 - half)
                    for i in range(GROUP):
                        if not (is_last(b) and g >= 2):
                            max_score(bm, gm, kt, i, half if g < 2 else 1 - half)
                        key_score(b, g, kt, i, half)
                        if i == GROUP - 1 and not (is_first(b) and u < VLAG):
                            values(bp, gp, ktp, halfp)
                        name = filled(b, u, i)
                        if name == "ln":
                            norm_T(b + 1, fill(b, name))
                        elif name in ("q", "k", "v"):
                            project(name, b + 1, fill(b, name))
                        elif name == "ctx":
                            out_proj(b - 1, fill(b, name))
                        elif name:
                            max_T(*group_of(b, name), fill(b, name))

            pe.wait_ge(s["wscale"], 1)
            norm_T(0, 0)
            for k, which in enumerate("qkv"):
                project(which, 0, k + 1)
            pe.wait_ge(s["const"], 80)
            for gm in range(2):
                for i in range(GROUP):
                    for qt in range(TILES):
                        max_score(0, gm, i, qt, 0)
                if gm == 0:
                    max_T(0, 0, fill(-1, "m0"))
            pairs(pe, steps)
            for u in range(UNITS - VLAG, UNITS):
                values(last_b, u // TILES, u % TILES, 1)

        @block.scalar
        def _(a):
            def read_hT(bn, k):
                a.wait_ge(s["fill"], k + 1)
                nc.scalar.activation(hT[:], Tb[:, 0, :], ACT.Identity, bias=mods[:, layer, 0, bass.ds(bn, 1)],
                                     scale=mods[:, layer, 1, bass.ds(bn, 1)]).then_inc(s["hT"], 1)
                a.wait_ge(s["hT"], bn + 1)
                a.sem_inc(s["free"], 1)

            def part0(which, bn, k):
                a.wait_ge(s["fill"], k + 1)
                if not (isinstance(bn, int) and bn == 0):
                    a.wait_ge(pk[0 if which == "q" else 1], 96 * bn)
                    a.wait_ge(s["p2"], 2 * bn)
                bias = bqk[:, 0:1] if which == "q" else bqk[:, 1:2]
                bank = Mb[:, "qkv".index(which), :] if is_first(bn) else Tb[:, 0, :]
                nc.scalar.activation(parts[f"{which}0"][:], bank, ACT.Identity, bias=bias)
                nc.scalar.activation(rest[which][:], bank, ACT.Identity, bias=bias).then_inc(s["p0"], 1)
                a.wait_ge(s["p0"], 2 * bn + (1 if which == "q" else 2))
                a.sem_inc(s["free"], 1)

            def shift_rows(bm, gm, k):
                a.wait_ge(s["fill"], k + 1)
                if not (isinstance(bm, int) and bm == 0 and gm < 2):
                    a.wait_ge(mrow[(gm - 2) % GROUPS], 16 * (bm + (1 if gm >= 2 else 0)))
                nc.scalar.activation(nrow[:, gm % 2, :], Tb[0:32, 0, 0:P // 2].bitcast(BF16), ACT.Copy)\
                  .then_inc(s["nrow"], 1)
                a.wait_ge(s["nrow"], GROUPS * bm + (gm + 1))
                a.sem_inc(s["free"], 1)

            def exp(b, g, kt, i):
                n = (GROUP * g + kt) * GROUP + i
                a.wait_ge(s["score"], b * PER_M + (n + 1))
                if i == 0 and not (is_first(b) and g == 0):
                    a.wait_ge(s["pv"], UNITS * b + (TILES * (g - 1) + kt + 1))
                kt = KEY_TILES[kt]
                q0 = kt * P if causal else 0
                nc.scalar.activation(E[:, kt, i, q0:SEQ], Sb[:, n % 3, q0:SEQ], ACT.Exp).then_inc(s["exp"], 1)

            def read_O(bp, gp):
                a.wait_ge(s["pv"], UNITS * bp + TILES * (gp + 1))
                if gp == 0 and not (isinstance(bp, int) and bp == 0):
                    a.wait_ge(s["gath"], 64 * bp)
                    a.wait_ge(s["compact"], 16 * bp)
                nc.scalar.activation(Oev[:, gp, :], Ob[:, 0, :], ACT.Copy).then_inc(s["oev"], 1)

            def steps(b, half):
                for u in range(UNITS):
                    g, kt = divmod(u, TILES)
                    for i in range(GROUP):
                        exp(b, g, kt, i)
                        if kt == VLAG and i == 0 and not (is_first(b) and g == 0):
                            read_O(*((b, g - 1) if g else (b - 1, GROUPS - 1)))
                        name = filled(b, u, i, 1)
                        if name == "ln":
                            read_hT(b + 1, fill(b, name))
                        elif name in ("q", "k"):
                            part0(name, b + 1, fill(b, name))
                        elif name and name[0] == "m":
                            shift_rows(*group_of(b, name), fill(b, name))

            a.wait_ge(s["wscale"], 1)
            read_hT(0, 0)
            part0("q", 0, 1)
            part0("k", 0, 2)
            if not causal:
                a.wait_ge(s["table"], 16)
                nc.scalar.activation(factor[:], factor[:], ACT.Exp).then_inc(s["fac"], 1)
            shift_rows(0, 0, 4)
            pairs(a, steps)
            read_O(last_b, GROUPS - 1)

        @block.vector
        def _(v):
            def stats(bn, t):
                last = v.bn_stats(st[:, t, :], x[:, bass.ds(bn * SEQ + t * P, P)])
                if t == TILES - 1:
                    last.then_inc(s["stats"], 1)

            def aggregate(bn):
                wait_apart(s, v, s["stats"], 2 * bn + 1)
                for t in range(TILES):
                    last = v.bn_aggr(mv[:, t, :], st[:, t, :])
                last.then_inc(s["stats"], 1)
                v.wait_ge(s["stats"], 2 * bn + 2)
                v.tensor_scalar(ve[:], mv[:, :, 1], EPS, None, ALU.add).then_inc(s["veps"], 1)

            def normalise(bn, t):
                if t == 0:
                    v.wait_ge(s["rstd"], bn + 1)
                    if not is_first(bn):
                        v.wait_ge(s["hT"], bn)
                last = v.tensor_scalar(xn[:, t, :], x[:, bass.ds(bn * SEQ + t * P, P)], mv[:, t, 0:1],
                                       rstd[:, t:t + 1], ALU.subtract, ALU.mult)
                if t == TILES - 1:
                    last.then_inc(s["norm"], 1)

            def remainder(which, bn):
                wait_apart(s, v, s["p0"], 2 * bn + (1 if which == "q" else 2))
                v.tensor_tensor(rest[which][:], rest[which][:], parts[f"{which}0"][:], ALU.subtract)\
                 .then_inc(s["rest"], 1)

            def read_V(bn, half, k):
                v.wait_ge(s["fill"], k + 1)
                if not (isinstance(bn, int) and bn < 2):
                    v.wait_ge(s["pv"], UNITS * bn - UNITS)
                bank = Mb[:, 2, :] if is_first(bn) else Tb[:, 0, :]
                v.tensor_tensor(VP[:, half, :, :, 0:DK], bank.rearrange("p (t h d) -> p t h d", t=TILES, h=HEADS),
                                both(bv[:], TILES).rearrange("p t (h d) -> p t h d", h=HEADS), ALU.add).then_inc(s["vp"], 1)
                v.wait_ge(s["vp"], bn + 1)
                v.sem_inc(s["free"], 1)

            def reduce_max(bm, gm, i, qt):
                n = (GROUP * gm + i) * TILES + qt
                v.wait_ge(s["maxs"], bm * PER_M + (n + 1))
                if i == 0 and qt == 0 and not (is_first(bm) and gm < 2):
                    v.wait_ge(s["nrow"], GROUPS * bm + (gm - 1))
                width = (qt + 1) * P if causal else SEQ
                v.tensor_reduce(mx[:, gm % 2, i * TILES + qt:i * TILES + qt + 1], Mb[:, n % 3, 0:width],
                                AX.X, ALU.max).then_inc(s["maxd"], 1)

            def negate(bm, gm):
                v.wait_ge(s["maxd"], bm * PER_M + 16 * (gm + 1))
                v.tensor_scalar(nmx[:, gm % 2, 0, :], mx[:, gm % 2, :], -1.0, None, ALU.mult).then_inc(s["nr0"], 1)
                v.wait_ge(s["nr0"], GROUPS * bm + (gm + 1))
                v.scalar_tensor_tensor(nmx[:, gm % 2, 1, :], mx[:, gm % 2, :], -1.0, nmx[:, gm % 2, 0, :],
                                       ALU.mult, ALU.subtract).then_inc(s["nr1"], 1)

            def gated(bo, k):
                v.wait_ge(s["fill"], k + 1)
                finish_gated(v, sb, s, layer, bo, Tb[:, 0, :])
                v.wait_ge(s["t1"], bo + 1)
                v.sem_inc(s["free"], 1)

            def steps(b, half):
                for u in range(UNITS):
                    g, kt = divmod(u, TILES)
                    bm, gm = groups_of(b, g)
                    maxima = not (is_last(b) and g >= 2)
                    for i in range(GROUP):
                        if maxima:
                            reduce_max(bm, gm, kt, i)
                        name = filled(b, u, i, 2)
                        if name in ("q", "k"):
                            remainder(name, b + 1)
                        elif name == "v":
                            read_V(b + 1, 1 - half, fill(b, name))
                        elif name == "ctx":
                            gated(b - 1, fill(b, name))
                        if u == 6 and i == 1 and not is_first(b):
                            finish_recip(v, sb, s, b - 1)
                        if u == 11 and i == 0 and not is_first(b):
                            finish_context(v, sb, s, b - 1)
                        if not (isinstance(b, int) and b >= last_b - 1):
                            if u == 10:
                                stats(b + 2, i)
                            if u == 11 and i == 0:
                                aggregate(b + 2)
                            if u == 14:
                                normalise(b + 2, i)
                    if maxima and kt == TILES - 1:
                        negate(bm, gm)

            for t in range(TILES):
                stats(0, t)
            aggregate(0)
            v.tensor_scalar(wqkv[:, 0:D], wqkv[:, 0:D], scale, None, ALU.mult)
            v.tensor_copy(idb[:], ident[:])
            v.tensor_scalar(bqk[:, 0:1], bqk[:, 0:1], scale, None, ALU.mult).then_inc(s["wscale"], 1)
            v.wait_ge(s["wscale"], 1)
            for t in range(TILES):
                normalise(0, t)
            remainder("q", 0)
            remainder("k", 0)
            v.wait_ge(s["rest"], 2)
            v.tensor_copy(parts["k1"][:], rest["k"][:]).then_inc(s["k_first"], 1)
            v.wait_ge(s["k_first"], 1)
            v.wait_ge(s["p2"], 1)
            v.tensor_tensor(parts["k2"][:], rest["k"][:], parts["k1"][:], ALU.subtract).then_inc(s["p2"], 1)
            v.wait_ge(s["zero"], 2)
            read_V(0, 0, 3)
            if causal:
                v.wait_ge(sb["x_rest"], 16)
            for t in range(TILES):
                stats(1, t)
            aggregate(1)
            for t in range(TILES):
                normalise(1, t)
            for gm in range(2):
                for i in range(GROUP):
                    for qt in range(TILES):
                        reduce_max(0, gm, i, qt)
                negate(0, gm)
            pairs(v, steps)

        @block.gpsimd
        def _(p):
            def powers(bn):
                p.wait_ge(s["veps"], bn + 1)
                p.tensor_tensor(rstd[:], ve[:], sb["mhalf"][:], ALU.pow).then_inc(s["rstd"], 1)

            def split(which, bn):
                k = 2 * bn + (1 if which == "q" else 2)
                if not (isinstance(bn, int) and bn == 0):
                    p.wait_ge(pk[0 if which == "q" else 1], 96 * bn)
                wait_apart(s, p, s["rest"], k)
                p.tensor_scalar(parts[f"{which}1"][:], rest[which][:], 1.0, None, ALU.mult).then_inc(s["p1"], 1)
                wait_apart(s, p, s["p1"], k if is_first(bn) else k - 1)
                p.tensor_tensor(parts[f"{which}2"][:], rest[which][:], parts[f"{which}1"][:],
                                ALU.subtract).then_inc(s["p2"], 1)

            def diagonal(b, g, kt):
                wait_apart(s, p, s["exp"], b * PER_M + (GROUP * g + kt + 1) * GROUP)
                kt = KEY_TILES[kt]
                blocks = E[:, kt, :, kt * P:(kt + 1) * P]
                if causal:
                    p.affine_select(out=blocks, in_=blocks, compare_op=ALU.is_ge, fill=0.0, base=0,
                                    pattern=[[0, GROUP], [1, P]], channel_multiplier=-1).then_inc(s["diag"], 1)
                else:
                    p.tensor_tensor(blocks, blocks, factor[:, GROUP * g:GROUP * (g + 1), :],
                                    ALU.mult).then_inc(s["diag"], 1)

            def steps(b, half):
                for u in range(UNITS):
                    diagonal(b, *divmod(u, TILES))
                    if u in (1, 2) and not is_last(b):
                        split("qk"[u - 1], b + 1)
                    if u == 13 and not is_first(b):
                        finish_x(p, sb, s, layer, b - 1)
                    if u == 12 and not (isinstance(b, int) and b >= last_b - 1):
                        powers(b + 2)

            powers(0)
            p.memset(VP[:], 0.0).then_inc(s["zero"], 1)
            p.wait_ge(s["zero"], 1)
            p.memset(VP[:, :, :, :, DENS:DENS + 1], 1.0).then_inc(s["zero"], 1)
            split("q", 0)
            powers(1)
            if not causal:
                p.wait_ge(s["fac"], 1)
            pairs(p, steps)

        @block.sync
        def _(sp):
            def stack(bn, half, which):
                if not (isinstance(bn, int) and bn < 2):
                    wait_apart(s, sp, s["score"], PER_M * bn - PER_M)
                k = 2 * bn + (1 + which)
                for part in range(3):
                    if part == 0:
                        sp.wait_ge(s["p0"], k)
                    elif part == 1 and is_first(bn):
                        sp.wait_ge(s["p1"] if which == 0 else s["k_first"], 1)
                    elif part == 1:
                        sp.wait_ge(s["p1"], k - 1)
                    else:
                        sp.wait_ge(s["p2"], k)
                    for r in range(6):
                        if (Q_PARTS, K_PARTS)[which][r] == part:
                            sp.dma_start((QP, KP)[which][8 * r:8 * r + 8, half, :, :],
                                         parts["qk"[which] + str(part)][:]).then_inc(pk[which], 16)

            def send_rows(bm, gm, half):
                sp.wait_ge(s["nrow"], GROUPS * bm + (gm + 1))
                sp.dma_start(QP[R_SHIFT + 1:R_ALL, half, GROUP * gm:GROUP * (gm + 1), :],
                             nrow[:, gm % 2, :]).then_inc(mrow[gm], 16)

            def steps(b, half):
                for g in range(GROUPS):
                    if g < 3:
                        send_rows(b, g + 1, half)
                    elif not is_last(b):
                        send_rows(b + 1, 0, 1 - half)
                    if g == 0 and not is_first(b):
                        finish_gather(sp, sb, s, b - 1)
                    if g == 0 and not is_last(b):
                        stack(b + 1, 1 - half, 0)
                        stack(b + 1, 1 - half, 1)
                    if g == 1 and not is_first(b):
                        finish_spread(sp, sb, s, b - 1)

            def constant_rows(half, sem):
                sp.dma_start(QP[R_ALIBI:R_SHIFT, half], dram[f"aliq{layer}"]).then_inc(sem, 16)
                sp.dma_start(KP[R_ALIBI:R_SHIFT, half], dram[f"alik{layer}"]).then_inc(sem, 16)
                sp.dma_start(QP[R_SHIFT:R_SHIFT + 1, half], dram[f"shiftq{layer}"]).then_inc(sem, 16)
                sp.dma_start(KP[R_SHIFT:R_ALL, half], dram["ones3"]).then_inc(sem, 16)

            constant_rows(0, s["const"])
            sp.dma_start(mask[:], dram[f"mask{layer}"]).then_inc(s["const"], 16)
            stack(0, 0, 0)
            stack(0, 0, 1)
            if not causal:
                sp.dma_start(factor[:], dram["alibi"]).then_inc(s["table"], 16)
            constant_rows(1, s["const2"])
            if causal:
                for b in range(NBATCH):
                    sp.dma_start(sb["gates"][:, b, :], sb["gate_rows"][b:b + 1, :].unsqueeze(1).to_broadcast([1, P, 4 * P]))\
                      .then_inc(sb["gates_ready"], 16)
            send_rows(0, 0, 0)
            if causal:
                for dst, src in ((sb["w_raw"]["w1"], "w1"), (sb["w_raw"]["w3"], "w3"), (sb["w2"], "w2")):
                    sp.dma_start(dst[:], dram[src]).then_inc(sb["experts_loaded"], 16)
            pairs(sp, steps)


def expert_phase(nc, dram, sb):
    x, ident, gate, mods = sb["x"], sb["ident"], sb["gateB0"], sb["mods"]
    gate_w, gate_b, iota8, b1, b3 = (sb[n] for n in ("gate_w", "gate_b", "iota8", "b1", "b3"))
    R_LOW = 64
    R_ROWS = R_LOW + ALL_EXP
    with ExitStack() as ctx:
        def tile(name, shape, dt=F32):
            return ctx.enter_context(nc.sbuf_tensor(f"ex_{name}", shape, dt))

        raw, w2, loaded = sb["w_raw"], sb["w2"], sb["experts_loaded"]
        hi = {n: tile(f"{n}_hi", [P, HPAD], F32R) for n in ("w1", "w3")}
        lo = {n: tile(f"{n}_lo", [P, HPAD], F32R) for n in ("w1", "w3")}
        sel = tile("sel", [R_ROWS, HPAD])
        selr = tile("selr", [R_ROWS, HPAD], F32R)
        st = tile("st", [P, TILES, 6])
        mv = tile("mv", [P, TILES, 2])
        ve = tile("ve", [P, TILES])
        rstd = tile("rstd", [P, TILES])
        xn = tile("xn", [P, TILES, P])
        hT = tile("hT", [P, SEQ])
        h_hi = tile("h_hi", [P, 2, SEQ], F32R)
        h_lo = tile("h_lo", [P, 2, SEQ], F32R)
        top = tile("top", [P, TILES])
        lg = tile("lg", [P, TILES, EXPERTS])
        ex = tile("ex", [P, TILES, EXPERTS])
        sm = tile("sm", [P, TILES])
        rs = tile("rs", [P, TILES])
        sc = tile("sc", [P, TILES, EXPERTS])
        bi = tile("bi", [P, TILES, EXPERTS])
        m8 = tile("m8", [P, TILES, 8])
        i8 = tile("i8", [P, TILES, 8], U32)
        i8f = tile("i8f", [P, TILES, 8])
        k1 = tile("k1", [P, TILES, EXPERTS])
        k2 = tile("k2", [P, TILES, EXPERTS])
        k12 = tile("k12", [P, TILES, EXPERTS])
        rw = tile("rw", [P, TILES, ALL_EXP])
        rwT = tile("rwT", [ALL_EXP, 2, SEQ])
        rwr = tile("rwr", [P, 2, SEQ], F32R)
        up3 = tile("up3", [P, 2, SEQ])
        z = tile("z", [P, 2, SEQ])
        th = tile("th", [P, 2, SEQ])
        hh = tile("hh", [P, 2, SEQ])
        t1 = tile("t1", [P, SEQ])

        def bank(name, n=1):
            return ctx.enter_context(nc.psum_tensor(f"ex_{name}", [P, n, 512], F32))

        Ab, Bb, Rb, Yb, Tb = bank("Ab", 2), bank("Bb", 2), bank("Rb", 2), bank("Yb"), bank("Tb")
        s = semaphores(nc, ctx, "ex", "sel zero hi1 lo1 hi3 lo3 selr stats veps rstd norm fill free hT hhi hlo "
                 "proj ch exp rwT rhi rlo up u3 z th hh down y t1 xup")
        at = sb["attention"]
        s["apart"] = sb["apart"]
        block = ctx.enter_context(nc.Block())
        N = HTILES
        last_b = NBATCH - 1

        def is_int(b, k):
            return isinstance(b, int) and b == k

        CH_PER = 14

        LN, LOGITS, RW = range(3)

        def pairs(eng, body):
            body(0, 0)
            body(1, 1)
            with eng.Fori(1, NBATCH // 2 - 1) as pair:
                body(pair * 2, 0)
                body(pair * 2 + 1, 1)
            body(last_b - 1, 0)
            body(last_b, 1)

        @block.sync
        def _(sp):
            sp.dma_start(sel[:], dram["sel"]).then_inc(s["sel"], 16)
            finish_gather(sp, sb, at, last_b)
            finish_spread(sp, sb, at, last_b)

        @block.gpsimd
        def _(p):
            def powers(bn):
                p.wait_ge(s["veps"], bn + 1)
                p.tensor_tensor(rstd[:], ve[:], sb["mhalf"][:], ALU.pow).then_inc(s["rstd"], 1)

            def split(bn, half):
                if not (isinstance(bn, int) and bn < 2):
                    p.wait_ge(s["up"], N * bn - N)
                wait_apart(s, p, s["hT"], bn + 1)
                p.tensor_scalar(h_hi[:, half, :], hT[:], 1.0, None, ALU.mult).then_inc(s["hhi"], 1)
                p.wait_ge(s["hhi"], bn + 1)
                p.tensor_tensor(h_lo[:, half, :], hT[:], h_hi[:, half, :].bitcast(F32), ALU.subtract)\
                 .then_inc(s["hlo"], 1)

            def update_x(b):
                xb = x[:, bass.ds(b * SEQ, SEQ)]
                wait_apart(s, p, s["t1"], b + 1)
                p.tensor_tensor(xb, xb, t1[:], ALU.add).then_inc(s["xup"], 1)

            def body(b, half):
                if not is_int(b, last_b):
                    powers(b + 1)
                    split(b + 1, 1 - half)
                if is_int(b, 0):
                    finish_x(p, sb, at, 0, last_b)
                if not is_int(b, 0):
                    update_x(b - 1)

            powers(0)
            p.memset(rwr[:].bitcast(F32), 0.0).then_inc(s["zero"], 1)
            split(0, 0)
            p.wait_ge(loaded, 48)
            p.wait_ge(s["hi3"], 1)
            p.tensor_tensor(lo["w3"][:], raw["w3"][:], hi["w3"][:].bitcast(F32), ALU.subtract).then_inc(s["lo3"], 1)
            pairs(p, body)
            update_x(last_b)

        @block.scalar
        def _(a):
            def read_hT(bn):
                a.wait_ge(s["fill"], 3 * bn + (LN + 1))
                if not is_int(bn, 0):
                    a.wait_ge(s["hlo"], bn)
                nc.scalar.activation(hT[:], Tb[:, 0, :], ACT.Identity, bias=mods[:, 0, 2, bass.ds(bn, 1)],
                                     scale=mods[:, 0, 3, bass.ds(bn, 1)]).then_inc(s["hT"], 1)
                a.wait_ge(s["hT"], bn + 1)
                a.sem_inc(s["free"], 1)

            def route_exp(bn):
                a.wait_ge(s["ch"], CH_PER * bn + 2)
                nc.scalar.activation(ex[:], lg[:], ACT.Exp).then_inc(s["exp"], 1)

            def read_rw(bn, half):
                a.wait_ge(s["fill"], 3 * bn + (RW + 1))
                if not (isinstance(bn, int) and bn < 2):
                    a.wait_ge(s["y"], bn - 1)
                nc.scalar.activation(rwT[:, half, :], Tb[0:ALL_EXP, 0, :], ACT.Copy).then_inc(s["rwT"], 1)

            def up_bias(b, j, n):
                q = (13 * (n % 2) + j) % 2
                a.wait_ge(s["up"], N * b + (j + 1))
                if not (is_int(b, 0) and j < 2):
                    a.wait_ge(s["z"], N * b + (j - 1))
                nc.scalar.activation(up3[:, q, :], Bb[:, q, :], ACT.Identity, bias=b3[:, j:j + 1]).then_inc(s["u3"], 1)

            def silu(b, j, n):
                q = (13 * (n % 2) + j) % 2
                a.wait_ge(s["z"], N * b + (j + 1))
                if not (is_int(b, 0) and j < 2):
                    a.wait_ge(s["hh"], N * b + (j - 1))
                nc.scalar.activation(th[:, q, :], z[:, q, :], ACT.Silu).then_inc(s["th"], 1)

            def body(b, half):
                for j in range(N):
                    up_bias(b, j, half)
                    if not is_int(b, last_b):
                        if j == 3:
                            read_hT(b + 1)
                        if j == 6:
                            route_exp(b + 1)
                        if j == 11:
                            read_rw(b + 1, 1 - half)
                    silu(b, j, half)

            a.wait_ge(loaded, 48)
            nc.scalar.activation(hi["w3"][:], raw["w3"][:], ACT.Copy).then_inc(s["hi3"], 1)
            read_hT(0)
            a.wait_ge(s["sel"], 16)
            nc.scalar.activation(selr[:], sel[:], ACT.Copy).then_inc(s["selr"], 1)
            route_exp(0)
            read_rw(0, 0)
            pairs(a, body)

        @block.vector
        def _(v):
            def stats(bn):
                if is_int(bn, last_b):
                    v.wait_ge(at["bias"], 2 * NBATCH)
                for t in range(TILES):
                    last = v.bn_stats(st[:, t, :], x[:, bass.ds(bn * SEQ + t * P, P)])
                last.then_inc(s["stats"], 1)
                wait_apart(s, v, s["stats"], 2 * bn + 1)
                for t in range(TILES):
                    last = v.bn_aggr(mv[:, t, :], st[:, t, :])
                last.then_inc(s["stats"], 1)
                v.wait_ge(s["stats"], 2 * bn + 2)
                v.tensor_scalar(ve[:], mv[:, :, 1], EPS, None, ALU.add).then_inc(s["veps"], 1)

            def normalise(bn):
                v.wait_ge(s["rstd"], bn + 1)
                if not is_int(bn, 0):
                    v.wait_ge(s["hT"], bn)
                for t in range(TILES):
                    last = v.tensor_scalar(xn[:, t, :], x[:, bass.ds(bn * SEQ + t * P, P)], mv[:, t, 0:1],
                                           rstd[:, t:t + 1], ALU.subtract, ALU.mult)
                last.then_inc(s["norm"], 1)

            def route_step(bn, k, ins):
                ins.then_inc(s["ch"], 1)
                if k in (6, 7):
                    wait_apart(s, v, s["ch"], CH_PER * bn + k)
                else:
                    v.wait_ge(s["ch"], CH_PER * bn + k)

            def route_shift(bn):
                logits = Tb[:, 0, 0:TILES * EXPERTS].rearrange("p (t e) -> p t e", t=TILES)
                v.wait_ge(s["fill"], 3 * bn + (LOGITS + 1))
                if not is_int(bn, 0):
                    v.wait_ge(s["exp"], bn)
                route_step(bn, 1, v.tensor_reduce(top[:], logits, AX.X, ALU.max))
                route_step(bn, 2, v.tensor_tensor(lg[:], logits, each(top[:], EXPERTS), ALU.subtract))
                v.sem_inc(s["free"], 1)

            def route_softmax(bn):
                v.wait_ge(s["exp"], bn + 1)
                route_step(bn, 3, v.tensor_reduce(sm[:], ex[:], AX.X, ALU.add))
                route_step(bn, 4, v.reciprocal(rs[:], sm[:]))
                route_step(bn, 5, v.tensor_tensor(sc[:], ex[:], each(rs[:], EXPERTS), ALU.mult))
                route_step(bn, 6, v.tensor_tensor(bi[:], sc[:], both(gate_b[:], TILES), ALU.add))

            def route_top(bn):
                for t in range(TILES):
                    last = v.max(m8[:, t, :], bi[:, t, :])
                route_step(bn, 7, last)
                for t in range(TILES):
                    last = v.max_index(i8[:, t, :], m8[:, t, :], bi[:, t, :])
                route_step(bn, 8, last)

            def route_weights(bn):
                def chosen(r):
                    return i8f[:, :, r:r + 1].to_broadcast([P, TILES, EXPERTS])

                numbers = both(iota8[:], TILES)
                route_step(bn, 9, v.tensor_copy(i8f[:], i8[:]))
                route_step(bn, 10, v.tensor_tensor(k1[:], numbers, chosen(0), ALU.is_equal))
                route_step(bn, 11, v.tensor_tensor(k2[:], numbers, chosen(1), ALU.is_equal))
                route_step(bn, 12, v.tensor_tensor(k12[:], k1[:], k2[:], ALU.add))
                route_step(bn, 13, v.memset(rw[:, :, EXPERTS:ALL_EXP], 1.0))
                route_step(bn, 14, v.tensor_tensor(rw[:, :, 0:EXPERTS], sc[:], k12[:], ALU.mult))

            def split_rw(bn, half):
                v.wait_ge(s["fill"], 3 * bn + (RW + 1))
                v.wait_ge(s["rwT"], bn + 1)
                if not (isinstance(bn, int) and bn < 2):
                    v.wait_ge(s["up"], N * bn - N)
                v.tensor_scalar(rwr[0:ALL_EXP, half, :], Tb[0:ALL_EXP, 0, :], 1.0, None, ALU.mult).then_inc(s["rhi"], 1)
                v.wait_ge(s["rhi"], bn + 1)
                v.tensor_tensor(rwr[R_LOW:R_ROWS, half, :], Tb[0:ALL_EXP, 0, :],
                                rwr[0:ALL_EXP, half, :].bitcast(F32), ALU.subtract).then_inc(s["rlo"], 1)
                v.wait_ge(s["rlo"], bn + 1)
                v.sem_inc(s["free"], 1)

            def product(b, j, n):
                q = (13 * (n % 2) + j) % 2
                v.wait_ge(s["u3"], N * b + (j + 1))
                if not (is_int(b, 0) and j < 2):
                    v.wait_ge(s["th"], N * b + (j - 1))
                v.scalar_tensor_tensor(z[:, q, :], Ab[:, q, :], b1[:, j:j + 1], up3[:, q, :],
                                       ALU.add, ALU.mult).then_inc(s["z"], 1)

            def hidden(b, j, n):
                q = (13 * (n % 2) + j) % 2
                v.wait_ge(s["th"], N * b + (j + 1))
                if not (is_int(b, 0) and j < 2):
                    v.wait_ge(s["down"], N * b + (j - 1))
                v.tensor_tensor(hh[:, q, :], Rb[:, q, :], th[:, q, :], ALU.mult).then_inc(s["hh"], 1)

            def gated(b):
                v.wait_ge(s["y"], b + 1)
                if not is_int(b, 0):
                    v.wait_ge(s["xup"], b)
                v.tensor_tensor(t1[:].rearrange("p (t d) -> p t d", t=TILES),
                                Yb[:, 0, :].rearrange("p (t d) -> p t d", t=TILES),
                                gate[:, bass.ds(b, 1), :].to_broadcast([P, TILES, P]), ALU.mult).then_inc(s["t1"], 1)

            def body(b, half):
                for j in range(N):
                    product(b, j, half)
                    if j == 1 and not is_int(b, 0):
                        gated(b - 1)
                    if is_int(b, 0) and j == 0:
                        finish_context(v, sb, at, last_b)
                    if is_int(b, 0) and j == 2:
                        v.wait_ge(s["proj"], 1)
                        finish_gated(v, sb, at, 0, last_b, Tb[:, 0, :])
                    if not is_int(b, last_b):
                        if j == 0:
                            stats(b + 1)
                        if j == 2:
                            normalise(b + 1)
                        if j == 6:
                            route_shift(b + 1)
                        if j == 7:
                            route_softmax(b + 1)
                        if j == 8:
                            route_top(b + 1)
                        if j == 9:
                            route_weights(b + 1)
                        if j == 11:
                            split_rw(b + 1, 1 - half)
                    hidden(b, j, half)

            stats(0)
            normalise(0)
            v.wait_ge(loaded, 48)
            v.tensor_scalar(hi["w1"][:], raw["w1"][:], 1.0, None, ALU.mult).then_inc(s["hi1"], 1)
            v.wait_ge(s["hi1"], 1)
            v.tensor_tensor(lo["w1"][:], raw["w1"][:], hi["w1"][:].bitcast(F32), ALU.subtract).then_inc(s["lo1"], 1)
            finish_recip(v, sb, at, last_b)
            for stage in (route_shift, route_softmax, route_top, route_weights):
                stage(0)
            v.wait_ge(s["zero"], 1)
            split_rw(0, 0)
            pairs(v, body)
            gated(last_b)

        @block.tensor
        def _(pe):
            def norm_T(bn):
                if not is_int(bn, 0):
                    pe.wait_ge(s["free"], 3 * bn + LN)
                pe.wait_ge(s["norm"], bn + 1)
                for t in range(TILES):
                    last = pe.transpose(Tb[:, 0, t * P:(t + 1) * P], xn[:, t, :], ident[:])
                last.then_inc(s["fill"], 1)

            def logits(bn):
                pe.wait_ge(s["free"], 3 * bn + LOGITS)
                pe.wait_ge(s["hT"], bn + 1)
                for t in range(TILES):
                    last = pe.matmul(Tb[:, 0, t * EXPERTS:(t + 1) * EXPERTS], hT[:, t * P:(t + 1) * P], gate_w[:],
                                     start=True, stop=True)
                last.then_inc(s["fill"], 1)

            def rw_T(bn):
                pe.wait_ge(s["free"], 3 * bn + RW)
                pe.wait_ge(s["ch"], CH_PER * (bn + 1))
                for t in range(TILES):
                    last = pe.transpose(Tb[0:ALL_EXP, 0, t * P:(t + 1) * P], rw[:, t, :], ident[:])
                last.then_inc(s["fill"], 1)

            def up(b, j, half):
                q = (13 * half + j) % 2
                if j == 0:
                    pe.wait_ge(s["hlo"], b + 1)
                    pe.wait_ge(s["rlo"], b + 1)
                if not (is_int(b, 0) and j < 2):
                    pe.wait_ge(s["z"], N * b + (j - 1))
                cols = slice(j * P, (j + 1) * P)
                for bankk, w in ((Ab, "w1"), (Bb, "w3")):
                    pe.matmul(bankk[:, q, :], hi[w][:, cols], h_hi[:, half, :], start=True, stop=False)
                    pe.matmul(bankk[:, q, :], hi[w][:, cols], h_lo[:, half, :], start=False, stop=False)
                    pe.matmul(bankk[:, q, :], lo[w][:, cols], h_hi[:, half, :], start=False, stop=True)
                if not (is_int(b, 0) and j < 2):
                    pe.wait_ge(s["hh"], N * b + (j - 1))
                pe.matmul(Rb[:, q, :], selr[:, cols], rwr[0:R_ROWS, half, :], start=True, stop=True)\
                  .then_inc(s["up"], 1)

            def down(b, j, half):
                q = (13 * half + j) % 2
                pe.wait_ge(s["hh"], N * b + (j + 1))
                if j == 0:
                    if not is_int(b, 0):
                        pe.wait_ge(s["t1"], b)
                    for t in range(TILES):
                        pe.matmul(Yb[:, 0, t * P:(t + 1) * P], rwT[:, half, t * P:(t + 1) * P], sb["b2"][:],
                                  start=(t == 0), stop=False, skip_group_check=True)
                for t in range(TILES):
                    last = pe.matmul(Yb[:, 0, t * P:(t + 1) * P], hh[:, q, t * P:(t + 1) * P], w2[:, j, :],
                                     start=False, stop=(j == N - 1), skip_group_check=True)
                last.then_inc(s["down"], 1)
                if j == N - 1:
                    pe.wait_ge(s["down"], N * b + N)
                    pe.sem_inc(s["y"], 1)

            def body(b, half):
                for j in range(N):
                    up(b, j, half)
                    if j >= 2:
                        down(b, j - 2, half)
                    elif not is_int(b, 0):
                        down(b - 1, N - 2 + j, 1 - half)
                    if is_int(b, 0) and j == 1:
                        pe.wait_ge(s["free"], 3)
                        finish_project(pe, sb, at, 0, last_b, Tb[:, 0, :]).then_inc(s["proj"], 1)
                    if not is_int(b, last_b):
                        if j == 3:
                            if is_int(b, 0):
                                pe.wait_ge(at["t1"], NBATCH)
                            norm_T(b + 1)
                        if j == 5:
                            logits(b + 1)
                        if j == 10:
                            rw_T(b + 1)

            norm_T(0)
            logits(0)
            rw_T(0)
            pe.wait_ge(loaded, 48)
            pe.wait_ge(s["selr"], 1)
            pe.wait_ge(s["lo1"], 1)
            pe.wait_ge(s["lo3"], 1)
            pairs(pe, body)
            down(last_b, N - 2, 1)
            down(last_b, N - 1, 1)


def spike_phase(nc, dram, sb, out):
    x, ident, gate, mods = (sb[n] for n in ("x", "ident", "gateB1", "mods"))
    FT = FFN // P
    last_b = NBATCH - 1
    with ExitStack() as ctx:
        def tile(name, shape, dt=F32):
            return ctx.enter_context(nc.sbuf_tensor(f"sp_{name}", shape, dt))

        wfc = tile("wfc", [P, FFN])
        wproj = tile("wproj", [P, FT, P])
        idb = tile("idb", [P, P], BF16)
        st = tile("st", [P, TILES, 6])
        mv = tile("mv", [P, TILES, 2])
        ve = tile("ve", [P, TILES])
        rstd = tile("rstd", [P, TILES])
        xn = tile("xn", [P, TILES, P])
        hT = tile("hT", [P, SEQ])
        relu = tile("relu", [P, FT, SEQ])
        sq = tile("sq", [P, FT, SEQ])
        y = tile("y", [P, 2, SEQ])
        drive = tile("drive", [P, SEQ])
        nmem = tile("nmem", [P, STEPS, SEQ])
        spk = tile("spk", [P, STEPS, SEQ], BF16)
        t1 = tile("t1", [P, SEQ])

        def bank(name, n=1):
            return ctx.enter_context(nc.psum_tensor(f"sp_{name}", [P, n, 512], F32))

        Ub, Yb, Tb, Cb = bank("Ub", FT), bank("Yb"), bank("Tb"), bank("Cb", 2)
        s = semaphores(nc, ctx, "sp", "load idb stats veps rstd norm fill hT up relu sq down y drive nm spk cnt proj t1 "
                       "xup")
        at = sb["attention"]
        s["apart"] = sb["apart"]
        block = ctx.enter_context(nc.Block())

        def is_int(b, k):
            return isinstance(b, int) and b == k

        def pairs(eng, body):
            body(0, 0)
            body(1, 1)
            with eng.Fori(1, NBATCH // 2 - 1) as pair:
                body(pair * 2, 0)
                body(pair * 2 + 1, 1)
            body(last_b - 1, 0)
            body(last_b, 1)

        @block.gpsimd
        def _(p):
            def powers(bn):
                p.wait_ge(s["veps"], bn + 1)
                p.tensor_tensor(rstd[:], ve[:], sb["mhalf"][:], ALU.pow).then_inc(s["rstd"], 1)

            def spike(b, k):
                if k == 0:
                    if not is_int(b, 0):
                        p.wait_ge(s["cnt"], b)
                    wait_apart(s, p, s["y"], b + 1)
                else:
                    wait_apart(s, p, s["nm"], (STEPS - 1) * b + k)
                p.tensor_scalar(spk[:, k, :], nmem[:, k, :], -1.0, None, ALU.is_lt).then_inc(s["spk"], 1)

            def body(b, half):
                for k in range(STEPS):
                    spike(b, k)
                    if k == 1 and not (isinstance(b, int) and b >= last_b - 1):
                        powers(b + 2)
                if is_int(b, 0):
                    finish_x(p, sb, at, 1, last_b)

            powers(0)
            powers(1)
            pairs(p, body)

        @block.sync
        def _(sp):
            def body(b):
                sp.wait_ge(s["xup"], b + 1)
                sp.dma_start(out[bass.ds(b, 1)].rearrange("b (t p) d -> p (b t) d", p=P),
                             x[:, bass.ds(b * SEQ, SEQ)].rearrange("p (t d) -> p t d", t=TILES))\
                  .then_inc(sb["stored"], 16)
            sp.dma_start(wfc[:], dram["wfc"]).then_inc(s["load"], 16)
            sp.dma_start(wproj[:], dram["wproj"]).then_inc(s["load"], 16)
            finish_gather(sp, sb, at, last_b)
            finish_spread(sp, sb, at, last_b)
            body(0)
            with sp.Fori(1, NBATCH) as b:
                body(b)
            sp.wait_ge(sb["stored"], 16 * NBATCH)

        @block.tensor
        def _(pe):
            def norm_T(bn):
                if not is_int(bn, 0):
                    pe.wait_ge(s["hT"], bn)
                pe.wait_ge(s["norm"], bn + 1)
                for t in range(TILES):
                    last = pe.transpose(Tb[:, 0, t * P:(t + 1) * P], xn[:, t, :], ident[:])
                last.then_inc(s["fill"], 1)

            def down(b, f):
                pe.wait_ge(s["sq"], FT * b + (f + 1))
                if f == 0 and not is_int(b, 0):
                    pe.wait_ge(s["y"], b)
                for t in range(TILES):
                    last = pe.matmul(Yb[:, 0, t * P:(t + 1) * P], sq[:, f, t * P:(t + 1) * P], wproj[:, f, :],
                                     start=(f == 0 and t == 0), stop=(f == FT - 1), skip_group_check=True)
                last.then_inc(s["down"], 1)

            def count(b, k, half):
                pe.wait_ge(s["spk"], STEPS * b + (k + 1))
                if is_int(b, 1) and k == 0:
                    pe.wait_ge(at["t1"], NBATCH)
                if k == 0 and not (isinstance(b, int) and b < 2):
                    pe.wait_ge(s["t1"], b - 1)
                last = pe.matmul(Cb[:, half, :], idb[:], spk[:, k, :], start=(k == 0), stop=(k == STEPS - 1))
                if k == STEPS - 1:
                    last.then_inc(s["cnt"], 1)

            def body(b, half):
                pe.wait_ge(s["hT"], b + 1)
                for f in range(FT):
                    if not is_int(b, 0):
                        pe.wait_ge(s["relu"], FT * b - (FT - 1 - f))
                    pe.matmul(Ub[:, f, :], wfc[:, f * P:(f + 1) * P], hT[:], start=True, stop=True)\
                      .then_inc(s["up"], 1)
                    if f >= 2:
                        down(b, f - 2)
                if is_int(b, 0):
                    finish_project(pe, sb, at, 1, last_b, Cb[:, 1, :]).then_inc(s["proj"], 1)
                for f in range(FT - 2, FT):
                    down(b, f)
                if not is_int(b, last_b):
                    norm_T(b + 1)
                if not is_int(b, 0):
                    for k in range(STEPS):
                        count(b - 1, k, 1 - half)

            norm_T(0)
            pe.wait_ge(s["load"], 32)
            pe.wait_ge(s["idb"], 1)
            pairs(pe, body)
            for k in range(STEPS):
                count(last_b, k, 1)

        @block.scalar
        def _(a):
            def read_hT(bn):
                a.wait_ge(s["fill"], bn + 1)
                if not is_int(bn, 0):
                    a.wait_ge(s["up"], FT * bn)
                nc.scalar.activation(hT[:], Tb[:, 0, :], ACT.Identity, bias=mods[:, 1, 2, bass.ds(bn, 1)],
                                     scale=mods[:, 1, 3, bass.ds(bn, 1)]).then_inc(s["hT"], 1)

            def read_Y(b, half):
                a.wait_ge(s["down"], FT * b + FT)
                if not is_int(b, 0):
                    a.wait_ge(s["nm"], (STEPS - 1) * b - (STEPS - 2))
                    a.wait_ge(s["spk"], STEPS * b - (STEPS - 1))
                nc.scalar.activation(nmem[:, 0, :], Yb[:, 0, :], ACT.Copy, scale=-1.0)
                nc.scalar.activation(y[:, half, :], Yb[:, 0, :], ACT.Copy).then_inc(s["y"], 1)

            def body(b, half):
                for f in range(FT + 1):
                    if f < FT:
                        a.wait_ge(s["up"], FT * b + (f + 1))
                        nc.scalar.activation(relu[:, f, :], Ub[:, f, :], ACT.Relu).then_inc(s["relu"], 1)
                    if f > 0:
                        a.wait_ge(s["relu"], FT * b + f)
                        if not is_int(b, 0):
                            a.wait_ge(s["down"], FT * b - (FT - f))
                        nc.scalar.activation(sq[:, f - 1, :], relu[:, f - 1, :], ACT.Square).then_inc(s["sq"], 1)
                read_Y(b, half)
                if not is_int(b, last_b):
                    read_hT(b + 1)

            read_hT(0)
            pairs(a, body)

        @block.vector
        def _(v):
            def stats(bn):
                for t in range(TILES):
                    last = v.bn_stats(st[:, t, :], x[:, bass.ds(bn * SEQ + t * P, P)])
                last.then_inc(s["stats"], 1)
                wait_apart(s, v, s["stats"], 2 * bn + 1)
                for t in range(TILES):
                    last = v.bn_aggr(mv[:, t, :], st[:, t, :])
                last.then_inc(s["stats"], 1)
                v.wait_ge(s["stats"], 2 * bn + 2)
                v.tensor_scalar(ve[:], mv[:, :, 1], EPS, None, ALU.add).then_inc(s["veps"], 1)

            def normalise(bn):
                v.wait_ge(s["rstd"], bn + 1)
                if not is_int(bn, 0):
                    v.wait_ge(s["fill"], bn)
                for t in range(TILES):
                    last = v.tensor_scalar(xn[:, t, :], x[:, bass.ds(bn * SEQ + t * P, P)], mv[:, t, 0:1],
                                           rstd[:, t:t + 1], ALU.subtract, ALU.mult)
                last.then_inc(s["norm"], 1)

            def membranes(b, half):
                v.wait_ge(s["y"], b + 1)
                for k in range(1, STEPS):
                    n = (STEPS - 1) * b + k
                    v.scalar_tensor_tensor(drive[:], nmem[:, k - 1, :], -BETA, y[:, half, :], ALU.mult, ALU.add)\
                     .then_inc(s["drive"], 1)
                    v.wait_ge(s["drive"], n)
                    if not is_int(b, 0):
                        v.wait_ge(s["spk"], STEPS * b - (STEPS - 1 - k))
                    v.scalar_tensor_tensor(nmem[:, k, :], nmem[:, k - 1, :], -1.0, drive[:],
                                           ALU.is_lt, ALU.subtract).then_inc(s["nm"], 1)
                    more = not (isinstance(b, int) and b >= last_b - 1)
                    if k == 1 and more:
                        stats(b + 2)
                    if k == 2 and not is_int(b, 0):
                        gated(b - 1, 1 - half)
                    if k == 3 and more:
                        normalise(b + 2)
                    if k == 3 and is_int(b, 0):
                        v.wait_ge(s["proj"], 1)
                        finish_gated(v, sb, at, 1, last_b, Cb[:, 1, :])
                    v.wait_ge(s["nm"], n)

            def gated(b, half):
                v.wait_ge(s["cnt"], b + 1)
                if not is_int(b, 0):
                    v.wait_ge(s["xup"], b)
                v.scalar_tensor_tensor(t1[:].rearrange("p (t d) -> p t d", t=TILES),
                                       Cb[:, half, :].rearrange("p (t d) -> p t d", t=TILES), 1.0 / STEPS,
                                       gate[:, bass.ds(b, 1), :].to_broadcast([P, TILES, P]),
                                       ALU.mult, ALU.mult).then_inc(s["t1"], 1)
                v.wait_ge(s["t1"], b + 1)
                xb = x[:, bass.ds(b * SEQ, SEQ)]
                v.tensor_tensor(xb, xb, t1[:], ALU.add).then_inc(s["xup"], 1)

            def body(b, half):
                if is_int(b, 1):
                    v.wait_ge(at["bias"], 2 * NBATCH)
                membranes(b, half)

            stats(0)
            v.tensor_copy(idb[:], ident[:]).then_inc(s["idb"], 1)
            normalise(0)
            stats(1)
            normalise(1)
            finish_recip(v, sb, at, last_b)
            finish_context(v, sb, at, last_b)
            pairs(v, body)
            gated(last_b, 1)


def build(nc, dram, out):
    with ExitStack() as ctx:
        sb = {}

        def tile(name, shape, dt=F32):
            sb[name] = ctx.enter_context(nc.sbuf_tensor(name, shape, dt))

        tile("x", [P, NBATCH * SEQ])
        tile("ident", [P, P])
        tile("mhalf", [P, TILES])
        tile("mods", [P, 2, 4, NBATCH])
        tile("Oev", [P, GROUPS, SEQ])
        tile("ctxN", [P, SEQ])
        tile("den", [P, SEQ // 8])
        tile("rden", [P, SEQ // 8])
        tile("rden16", [HEADS, SEQ])
        tile("denB", [P, SEQ])
        tile("ctxT", [P, SEQ])
        tile("t1", [P, SEQ])
        tile("gbo", [P, P])
        sb["keep"] = ctx
        tile("gate_rows", [NBATCH, 4 * P])
        tile("gates", [P, NBATCH, 4 * P])
        tile("columns", [P, COLUMNS["end"]])
        tile("rows", [P, ROWS["end"]])
        tile("b2", [ALL_EXP, D])
        for layer in range(2):
            for i, n in enumerate("AB"):
                k = 2 * layer + i
                sb[f"gate{n}{layer}"] = sb["gates"][:, :, k * P:(k + 1) * P]
        for whole, parts in (("columns", COLUMNS), ("rows", ROWS)):
            names = list(parts)
            for n, after in zip(names, names[1:]):
                sb[n] = sb[whole][:, parts[n]:parts[after]]
        for n in ("x_rest", "gates_ready", "stored", "apart"):
            sb[n] = ctx.enter_context(nc.semaphore(n))
        setup_phase(nc, dram, sb)
        with ExitStack() as expert_ctx:
            def expert_tile(name, shape):
                return expert_ctx.enter_context(nc.sbuf_tensor(name, shape, F32))

            sb["w_raw"] = {n: expert_tile(f"{n}_raw", [P, HPAD]) for n in ("w1", "w3")}
            sb["w2"] = expert_tile("w2", [P, HTILES, D])
            sb["experts_loaded"] = expert_ctx.enter_context(nc.semaphore("experts_loaded"))
            attention_phase(nc, dram, sb, 0)
            expert_phase(nc, dram, sb)
        attention_phase(nc, dram, sb, 1)
        spike_phase(nc, dram, sb, out)


def _bf16_parts(np, a, n):
    out, rest = [], a.astype(np.float64)
    for _ in range(n):
        part = rest.astype(np.float32).astype("bfloat16")
        out.append(part)
        rest = rest - part.astype(np.float64)
    return out


def constants(np):
    slopes = (2.0 ** -0.5) ** np.arange(1, HEADS + 1)
    slopes = slopes.astype(np.float32).astype(np.float64)
    pos = np.arange(SEQ)
    c = {}
    zero = np.zeros((N_ALIBI, HEADS, SEQ), "bfloat16")
    c["aliq0"], c["alik0"] = zero, zero
    sj = _bf16_parts(np, slopes[:, None] * pos[None], 3)
    si = _bf16_parts(np, -slopes[:, None] * pos[None], 3)
    q, k = zero.copy(), zero.copy()
    for kt in range(TILES - 1):
        after = (pos >= (kt + 1) * P)[None]
        inside = ((pos >= kt * P) & (pos < (kt + 1) * P))[None]
        for part in range(3):
            r = 6 * kt + part
            q[r] = after
            k[r] = sj[part] * inside
            q[r + 3] = si[part] * after
            k[r + 3] = np.broadcast_to(inside, k[r].shape)
    c["aliq1"], c["alik1"] = q, k
    c["shiftq0"] = np.zeros((1, HEADS, SEQ), "bfloat16")
    c["shiftq1"] = np.full((1, HEADS, SEQ), ALIBI_SHIFT, "bfloat16")
    c["ones3"] = np.ones((3, HEADS, SEQ), "bfloat16")
    p = np.arange(P)
    c["mask0"] = np.where(p[None] > p[:, None], -1e30, 0.0).astype("bfloat16")
    bias = slopes[None, :, None] * np.minimum(p[None, None] - p[:, None, None], 0)
    c["mask1"] = bias.astype(np.float32).astype("bfloat16")
    c["alibi"] = np.ascontiguousarray(bias.transpose(2, 1, 0)).astype(np.float32)
    sel = np.zeros((64 + ALL_EXP, HPAD), np.float32)
    unit = np.arange(ALL_EXP * HID)
    sel[unit // HID, unit] = 1.0
    sel[64 + unit // HID, unit] = 1.0
    c["sel"] = sel
    return c


def layout(np, i):
    def f(a):
        return np.ascontiguousarray(a)

    def heads(w):
        n = w.shape[0]
        return w.reshape(n, HEADS, DK).transpose(0, 2, 1).reshape(n, D)

    def by_strip(w):
        return w.reshape(GROUPS, GROUP, DK, D).transpose(1, 2, 0, 3).reshape(D, D)

    d = {"x": f(i["L0_attn_embeddings"])}
    wq, wk, wv = (np.asarray(i[f"L0_attn_W{n}"]).transpose(1, 0, 2).reshape(D, D) for n in "qkv")
    d["wqkv0"] = f(np.concatenate([heads(wq), heads(wk), wv], 1))
    bq, bk, bv = (np.asarray(i[f"L0_attn_b{n}"]).reshape(1, D) for n in "qkv")
    d["bqk0"] = f(np.concatenate([heads(bq), heads(bk)], 0).T)
    d["bv0"] = f(bv)
    w, b = np.asarray(i["L1_attn_W_qkv"]), np.asarray(i["L1_attn_b_qkv"]).reshape(1, 3 * D)
    d["wqkv1"] = f(np.concatenate([heads(w[:, 0:D]), heads(w[:, D:2 * D]), w[:, 2 * D:]], 1))
    d["bqk1"] = f(np.concatenate([heads(b[:, 0:D]), heads(b[:, D:2 * D])], 0).T)
    d["bv1"] = f(b[:, 2 * D:])
    d["wo0"], d["wo1"] = (f(by_strip(np.asarray(i[n]))) for n in ("L0_attn_Wo", "L1_attn_W_proj"))
    d["bo0"], d["bo1"] = f(np.asarray(i["L0_attn_bo"])[None]), f(np.asarray(i["L1_attn_b_proj"])[None])
    d["c"] = f(np.stack([np.asarray(i[f"L{layer}_c"]).T for layer in range(2)], 1))
    d["wmod"] = f(np.stack([np.asarray(i[f"L{layer}_wmod"]) for layer in range(2)], 1))
    d["gate_w"] = f(np.asarray(i["L0_ffn_gate_w"]).T)
    d["gate_b"] = f(np.asarray(i["L0_ffn_gate_b"])[None])
    pad = HPAD - ALL_EXP * HID
    for n in ("1", "3"):
        up = np.asarray(i[f"L0_ffn_w{n}"]).transpose(1, 0, 2).reshape(D, EXPERTS * HID)
        d[f"w{n}"] = f(np.pad(np.concatenate([up, np.asarray(i[f"L0_ffn_sw{n}"])], 1), ((0, 0), (0, pad))))
        bb = np.concatenate([np.asarray(i[f"L0_ffn_b{n}"]).reshape(-1), np.asarray(i[f"L0_ffn_sb{n}"])])
        d[f"b{n}"] = f(np.pad(bb, (0, pad)).reshape(HTILES, P).T)
    w2 = np.concatenate([np.asarray(i["L0_ffn_w2"]).reshape(-1, D), np.asarray(i["L0_ffn_sw2"])])
    d["w2"] = f(np.pad(w2, ((0, pad), (0, 0))).reshape(HTILES, P, D).transpose(1, 0, 2))
    d["b2"] = f(np.concatenate([np.asarray(i["L0_ffn_b2"]), np.asarray(i["L0_ffn_sb2"])[None]]))
    d["iota8"] = np.arange(EXPERTS, dtype=np.float32)[None]
    for whole, parts in (("columns", COLUMNS), ("rows", ROWS)):
        d[whole] = f(np.concatenate([d.pop(n) for n in list(parts)[:-1]], 1))
    d["wfc"] = f(np.asarray(i["L1_ffn_W_fc"]).T)
    d["wproj"] = f(np.asarray(i["L1_ffn_W_proj"]).T.reshape(FFN // P, P, D).transpose(1, 0, 2))
    return d


def kernel(**inputs):
    import numpy as np
    import concourse.bacc as bacc
    from concourse.bass_utils import run_bass_kernel_spmd

    arrays = {**layout(np, {k: np.asarray(v) for k, v in inputs.items()}), **constants(np)}
    nc = bacc.Bacc("TRN2", target_bir_lowering=False, num_devices=1)
    dram = {n: nc.dram_tensor(f"in_{n}", a.shape, mybir.dt.from_np(a.dtype), kind="ExternalInput").ap()
            for n, a in arrays.items()}
    out = nc.dram_tensor("out", (NBATCH, SEQ, D), F32, kind="ExternalOutput").ap()
    build(nc, dram, out)
    r = run_bass_kernel_spmd(nc, [{f"in_{n}": a for n, a in arrays.items()}], core_ids=[0])
    return r.results[0]["out"]
```
